# Optimizing a Trainium2 kernel written in Bass

```python
import numpy as np
import jax
import jax.numpy as jnp

def _softmax(x, axis=-1):
    return jax.nn.softmax(x, axis=axis)

def _gelu(x):
    return jax.nn.gelu(x, approximate=True)

def _silu(x):
    return jax.nn.silu(x)

def _sigmoid(x):
    return jax.nn.sigmoid(x)

def _layernorm(x, axis=-1, eps=1e-05):
    m = jnp.mean(x, axis=axis, keepdims=True)
    v = jnp.var(x, axis=axis, keepdims=True)
    return (x - m) / jnp.sqrt(v + eps)

def _scatter_add(tgt, idx, src, axis=0):
    return tgt.at[idx].add(src)

def _segment_sum(src, seg, n):
    return jax.ops.segment_sum(src, seg, n)
kernel_name = 'mk_flamingo_gated_d4_seqx_r8_7754f0'

def setup_inputs(seed: int=0):
    np.random.seed(seed)
    _w = jnp.asarray

    def _rec_inputs():
        import jax
        import jax.numpy as jnp
        _rk = jax.random.key(seed)
        x = -0.000125 + 0.9999 * jax.random.normal(jax.random.fold_in(_rk, 1), (8, 56, 256), jnp.float32)
        _lenS = 56 - jax.random.randint(jax.random.fold_in(_rk, 7), (8,), 0, max(1, 56 // 4) + 1, jnp.int32)
        _lenS2 = 1500 - jax.random.randint(jax.random.fold_in(_rk, 8), (8,), 0, max(1, 1500 // 4) + 1, jnp.int32)
        _ctx_2048P = jax.random.normal(jax.random.fold_in(_rk, 11), (8, 16, 256), jnp.float32)
        _ctx_2048c = jax.random.dirichlet(jax.random.fold_in(_rk, 511), 0.3 * jnp.ones((16,), jnp.float32), (8, 1500))
        _ctx_2048t = jnp.einsum('bsk,bkd->bsd', _ctx_2048c, _ctx_2048P)
        _ctx_2048t = _ctx_2048t * jax.lax.rsqrt(jnp.mean(jnp.square(_ctx_2048t)) + 1e-12) * 0.953939
        ctx_2048 = -0.000514642 + 1.00011 * (_ctx_2048t + 0.3 * jax.random.normal(jax.random.fold_in(_rk, 611), (8, 1500, 256), jnp.float32))
        itok_BxS_0_1023 = jax.random.randint(jax.random.fold_in(_rk, 13), (8, 56), 0, 128, jnp.int32)
        _validS = jnp.arange(56)[None, :] < _lenS[:, None]
        _validS2 = jnp.arange(1500)[None, :] < _lenS2[:, None]
        _causal = jnp.tril(jnp.ones((56, 56), dtype=bool))
        mask_BxS2_bk0 = jnp.logical_not(jnp.broadcast_to(_validS2[:, :], (8, 1500)))
        mask_BxSxS2_ff0 = jnp.where(jnp.ones((8, 56, 1500), dtype=bool), 0.0, -1000000000.0).astype(jnp.float32)
        _g = jax.random.normal(jax.random.fold_in(_rk, 9001), (2, 4), jnp.float32)
        _g = jnp.sign(_g) * jnp.maximum(jnp.abs(_g), 1.0) + (_g == 0) * 1.0
        g_xattn = _g[0]
        g_ffn = _g[1]
        return (x, ctx_2048, itok_BxS_0_1023, mask_BxS2_bk0, mask_BxSxS2_ff0, g_xattn, g_ffn)
    x, ctx_2048, itok_BxS_0_1023, mask_BxS2_bk0, mask_BxSxS2_ff0, g_xattn, g_ffn = _rec_inputs()

    def _L0_xattn_setup():
        import jax, jax.numpy as jnp
        import numpy as np
        H = 256
        NH = 16
        HD = H // NH
        EPS = 1e-06

        def rmsnorm(x, w, eps=EPS):
            var = jnp.mean(x * x, axis=-1, keepdims=True)
            return x * jax.lax.rsqrt(var + eps) * w
        key = jax.random.key(seed)
        ks = jax.random.split(key, 9)
        B, L, M = (4, 512, 32)
        s = 1.0 / np.sqrt(H)
        return {'hidden_states': jax.random.normal(ks[0], (B, L, H), dtype=jnp.float32), 'memory_tokens': jax.random.normal(ks[1], (B, M, H), dtype=jnp.float32), 'memory_mask': jax.random.randint(ks[2], (B, M), 0, 2).astype(bool), 'norm_w': jnp.ones((H,), dtype=jnp.float32), 'wq': jax.random.normal(ks[3], (H, H), dtype=jnp.float32) * s, 'wk': jax.random.normal(ks[4], (H, H), dtype=jnp.float32) * s, 'wv': jax.random.normal(ks[5], (H, H), dtype=jnp.float32) * s, 'wo': jax.random.normal(ks[6], (H, H), dtype=jnp.float32) * s, 'wg': jax.random.normal(ks[7], (H, H), dtype=jnp.float32) * s}
    _L0_xattn_all = _L0_xattn_setup()
    _L0_xattn_in = {k: v for k, v in _L0_xattn_all.items() if k in ('norm_w', 'wq', 'wk', 'wv', 'wo', 'wg')}
    del _L0_xattn_all

    def _L0_ffn_setup():
        import jax, jax.numpy as jnp
        import numpy as np
        H, I, E, TOP_K = (256, 176, 16, 6)
        IS = 352
        NORM_TOPK_PROB = False

        def _silu_and_mul(gate_up):
            d = gate_up.shape[-1] // 2
            g, u = (gate_up[..., :d], gate_up[..., d:])
            return jax.nn.silu(g) * u
        key = jax.random.key(seed)
        ks = jax.random.split(key, 6)
        s = 0.02
        return {'x': jax.random.normal(ks[0], (1, 256, H), jnp.float32), 'gate_w': jax.random.normal(ks[1], (E, H), jnp.float32) * s, 'w1': jax.random.normal(ks[2], (E, 2 * I, H), jnp.float32) * s, 'w2': jax.random.normal(ks[3], (E, H, I), jnp.float32) * s, 'shared_w1': jax.random.normal(ks[4], (2 * IS, H), jnp.float32) * s, 'shared_w2': jax.random.normal(ks[5], (H, IS), jnp.float32) * s}
    _L0_ffn_all = _L0_ffn_setup()
    _L0_ffn_in = {k: v for k, v in _L0_ffn_all.items() if k in ('gate_w', 'w1', 'w2', 'shared_w1', 'shared_w2')}
    del _L0_ffn_all

    def _L1_xattn_setup():
        import jax, jax.numpy as jnp
        import numpy as np
        B, Lq, Lk = (2, 512, 128)
        Q_DIM, KV_DIM = (256, 256)
        H, HD = (16, 128)
        KVC, QC, R = (64, 96, 64)
        LOOKBACK = 8
        NEG = -1e+30

        def _rope(x, L):
            half = x.shape[-1] // 2
            inv_freq = 1.0 / 10000.0 ** (jnp.arange(half, dtype=jnp.float32) / half)
            ang = jnp.arange(L, dtype=jnp.float32)[:, None] * inv_freq
            cos, sin = (jnp.cos(ang), jnp.sin(ang))
            x1, x2 = (x[..., :half], x[..., half:])
            return jnp.concatenate([x1 * cos - x2 * sin, x1 * sin + x2 * cos], axis=-1)
        key = jax.random.key(seed)
        ks = jax.random.split(key, 11)

        def w(k, shape, fan_in):
            return jax.random.normal(k, shape, jnp.float32) / np.sqrt(fan_in).astype(np.float32)
        return {'q': jax.random.normal(ks[0], (B, Lq, Q_DIM), jnp.float32), 'kv': jax.random.normal(ks[1], (B, Lk, KV_DIM), jnp.float32), 'seg_id': jnp.sort(jax.random.randint(ks[2], (B, Lq), 0, Lk), axis=-1), 'W_kvc': w(ks[3], (KV_DIM, KVC), KV_DIM), 'W_dq': w(ks[4], (Q_DIM, QC), Q_DIM), 'W_uq': w(ks[5], (QC, H * HD), QC), 'W_qr': w(ks[6], (QC, H * R), QC), 'W_uk': w(ks[7], (KVC, H * HD), KVC), 'W_kr': w(ks[8], (KVC, R), KVC), 'W_uv': w(ks[9], (KVC, H * HD), KVC), 'W_o': w(ks[10], (H * HD, Q_DIM), H * HD)}
    _L1_xattn_all = _L1_xattn_setup()
    _L1_xattn_in = {k: v for k, v in _L1_xattn_all.items() if k in ('W_kvc', 'W_dq', 'W_uq', 'W_qr', 'W_uk', 'W_kr', 'W_uv', 'W_o')}
    del _L1_xattn_all

    def _L1_ffn_setup():
        import jax, jax.numpy as jnp
        import numpy as np
        TOP_K = 4
        key = jax.random.key(seed)
        ks = jax.random.split(key, 8)
        B, S, D, E, H, HS = (2, 256, 256, 16, 128, 512)
        scaled = lambda k, shape, fan: jax.random.normal(k, shape, jnp.float32) * fan ** (-0.5)
        return {'x': jax.random.normal(ks[0], (B, S, D), jnp.float32), 'w_router': scaled(ks[1], (D, E), D), 'we1': scaled(ks[2], (E, D, H), D), 'we3': scaled(ks[3], (E, D, H), D), 'we2': scaled(ks[4], (E, H, D), H), 'ws1': scaled(ks[5], (D, HS), D), 'ws3': scaled(ks[6], (D, HS), D), 'ws2': scaled(ks[7], (HS, D), HS)}
    _L1_ffn_all = _L1_ffn_setup()
    _L1_ffn_in = {k: v for k, v in _L1_ffn_all.items() if k in ('w_router', 'we1', 'we3', 'we2', 'ws1', 'ws3', 'ws2')}
    del _L1_ffn_all

    def _L2_xattn_setup():
        import jax, jax.numpy as jnp
        import numpy as np
        NUM_HEADS = 16
        EPS = 1e-08

        def _dyn_quant(x):
            s = jnp.maximum(jnp.max(jnp.abs(x), axis=-1, keepdims=True) / 127.0, EPS)
            q = jnp.clip(jnp.round(x / s), -127.0, 127.0)
            return (q, s)

        def _quant_weight(w):
            s = jnp.maximum(jnp.max(jnp.abs(w), axis=1, keepdims=True) / 127.0, EPS)
            q = jnp.clip(jnp.round(w / s), -127.0, 127.0)
            return (q, s)

        def _w8a8_linear(x, w, b):
            qx, sx = _dyn_quant(x)
            qw, sw = _quant_weight(w)
            y = jnp.einsum('bnc,oc->bno', qx, qw) * (sx * sw[:, 0])
            return y + b
        key = jax.random.key(seed)
        ks = jax.random.split(key, 9)
        B, N, L, C = (2, 512, 64, 256)
        sc = 0.02
        return {'x': jax.random.normal(ks[0], (B, N, C), jnp.float32), 'cond': jax.random.normal(ks[1], (B, L, C), jnp.float32), 'mask': jnp.zeros((B, N, L), jnp.float32), 'wq': jax.random.normal(ks[2], (C, C), jnp.float32) * sc, 'bq': jnp.zeros((C,), jnp.float32), 'wk': jax.random.normal(ks[3], (C, C), jnp.float32) * sc, 'bk': jnp.zeros((C,), jnp.float32), 'wv': jax.random.normal(ks[4], (C, C), jnp.float32) * sc, 'bv': jnp.zeros((C,), jnp.float32), 'wo': jax.random.normal(ks[5], (C, C), jnp.float32) * sc, 'bo': jnp.zeros((C,), jnp.float32)}
    _L2_xattn_all = _L2_xattn_setup()
    _L2_xattn_in = {k: v for k, v in _L2_xattn_all.items() if k in ('wq', 'bq', 'wk', 'bk', 'wv', 'bv', 'wo', 'bo')}
    del _L2_xattn_all

    def _L2_ffn_setup():
        import jax, jax.numpy as jnp
        import numpy as np
        NUM_EXPERTS = 8
        TOP_K = 2
        MODEL_DIM = 256
        INTER_DIM = 128
        GATE_SCALE = 1.0
        UP_SCALE = 0.0
        key = jax.random.key(seed)
        k1, k2, k3, k4 = jax.random.split(key, 4)
        hidden_states = jax.random.normal(k1, (2, 256, MODEL_DIM), jnp.float32)
        router_gate = jax.random.normal(k2, (NUM_EXPERTS, MODEL_DIM), jnp.float32) * 0.02
        expert_gate_up = jax.random.normal(k3, (NUM_EXPERTS, MODEL_DIM, 2 * INTER_DIM), jnp.float32) * 0.02
        expert_down = jax.random.normal(k4, (NUM_EXPERTS, INTER_DIM, MODEL_DIM), jnp.float32) * 0.02
        return {'hidden_states': hidden_states, 'router_gate': router_gate, 'expert_gate_up': expert_gate_up, 'expert_down': expert_down}
    _L2_ffn_all = _L2_ffn_setup()
    _L2_ffn_in = {k: v for k, v in _L2_ffn_all.items() if k in ('router_gate', 'expert_gate_up', 'expert_down')}
    del _L2_ffn_all

    def _L3_xattn_setup():
        import jax, jax.numpy as jnp
        import numpy as np
        FEAT = 256
        G = 16
        DG = FEAT // G
        key = jax.random.key(seed)
        ks = jax.random.split(key, 8)
        bs, N1, N2 = (2, 512, 64)
        s = 1.0 / np.sqrt(FEAT)
        return {'ref_feat': jax.random.normal(ks[0], (bs, N1, FEAT), jnp.float32), 'sup_feat': jax.random.normal(ks[1], (bs, N2, FEAT), jnp.float32), 'W_fc': jax.random.normal(ks[2], (FEAT, FEAT), jnp.float32) * s, 'b_fc': jnp.zeros((FEAT,), jnp.float32), 'W_q': jax.random.normal(ks[3], (FEAT, FEAT), jnp.float32) * s, 'b_q': jnp.zeros((FEAT,), jnp.float32), 'W_k': jax.random.normal(ks[4], (FEAT, FEAT), jnp.float32) * s, 'b_k': jnp.zeros((FEAT,), jnp.float32), 'W_v': jax.random.normal(ks[5], (FEAT, FEAT, 1, 1), jnp.float32) * 0.01, 'b_v': jnp.zeros((FEAT,), jnp.float32)}
    _L3_xattn_all = _L3_xattn_setup()
    _L3_xattn_in = {k: v for k, v in _L3_xattn_all.items() if k in ('W_fc', 'b_fc', 'W_q', 'b_q', 'W_k', 'b_k', 'W_v', 'b_v')}
    del _L3_xattn_all

    def _L3_ffn_setup():
        import jax, jax.numpy as jnp
        import numpy as np
        B, S, D, I, E, K = (4, 128, 256, 128, 8, 2)
        key = jax.random.key(seed)
        ks = jax.random.split(key, 7)

        def w(k, shape, fan_in):
            return jax.random.normal(k, shape, dtype=jnp.float32) * fan_in ** (-0.5)
        return {'hidden_states': jax.random.normal(ks[0], (B, S, D), dtype=jnp.float32), 'router_w': w(ks[1], (D, E), D), 'gate_up_w': w(ks[2], (E, D, 2 * I), D), 'down_w': w(ks[3], (E, I, D), I), 'shared_gate_w': w(ks[4], (D, I), D), 'shared_up_w': w(ks[5], (D, I), D), 'shared_down_w': w(ks[6], (I, D), I)}
    _L3_ffn_all = _L3_ffn_setup()
    _L3_ffn_in = {k: v for k, v in _L3_ffn_all.items() if k in ('router_w', 'gate_up_w', 'down_w', 'shared_gate_w', 'shared_up_w', 'shared_down_w')}
    del _L3_ffn_all
    return {'x': x, 'ctx_2048': ctx_2048, 'itok_BxS_0_1023': itok_BxS_0_1023, 'mask_BxS2_bk0': mask_BxS2_bk0, 'mask_BxSxS2_ff0': mask_BxSxS2_ff0, 'g_xattn': g_xattn, 'g_ffn': g_ffn, 'L0_xattn_norm_w': _L0_xattn_in['norm_w'], 'L0_xattn_wq': _L0_xattn_in['wq'], 'L0_xattn_wk': _L0_xattn_in['wk'], 'L0_xattn_wv': _L0_xattn_in['wv'], 'L0_xattn_wo': _L0_xattn_in['wo'], 'L0_xattn_wg': _L0_xattn_in['wg'], 'L0_ffn_gate_w': _L0_ffn_in['gate_w'], 'L0_ffn_w1': _L0_ffn_in['w1'], 'L0_ffn_w2': _L0_ffn_in['w2'], 'L0_ffn_shared_w1': _L0_ffn_in['shared_w1'], 'L0_ffn_shared_w2': _L0_ffn_in['shared_w2'], 'L1_xattn_W_kvc': _L1_xattn_in['W_kvc'], 'L1_xattn_W_dq': _L1_xattn_in['W_dq'], 'L1_xattn_W_uq': _L1_xattn_in['W_uq'], 'L1_xattn_W_qr': _L1_xattn_in['W_qr'], 'L1_xattn_W_uk': _L1_xattn_in['W_uk'], 'L1_xattn_W_kr': _L1_xattn_in['W_kr'], 'L1_xattn_W_uv': _L1_xattn_in['W_uv'], 'L1_xattn_W_o': _L1_xattn_in['W_o'], 'L1_ffn_w_router': _L1_ffn_in['w_router'], 'L1_ffn_we1': _L1_ffn_in['we1'], 'L1_ffn_we3': _L1_ffn_in['we3'], 'L1_ffn_we2': _L1_ffn_in['we2'], 'L1_ffn_ws1': _L1_ffn_in['ws1'], 'L1_ffn_ws3': _L1_ffn_in['ws3'], 'L1_ffn_ws2': _L1_ffn_in['ws2'], 'L2_xattn_wq': _L2_xattn_in['wq'], 'L2_xattn_bq': _L2_xattn_in['bq'], 'L2_xattn_wk': _L2_xattn_in['wk'], 'L2_xattn_bk': _L2_xattn_in['bk'], 'L2_xattn_wv': _L2_xattn_in['wv'], 'L2_xattn_bv': _L2_xattn_in['bv'], 'L2_xattn_wo': _L2_xattn_in['wo'], 'L2_xattn_bo': _L2_xattn_in['bo'], 'L2_ffn_router_gate': _L2_ffn_in['router_gate'], 'L2_ffn_expert_gate_up': _L2_ffn_in['expert_gate_up'], 'L2_ffn_expert_down': _L2_ffn_in['expert_down'], 'L3_xattn_W_fc': _L3_xattn_in['W_fc'], 'L3_xattn_b_fc': _L3_xattn_in['b_fc'], 'L3_xattn_W_q': _L3_xattn_in['W_q'], 'L3_xattn_b_q': _L3_xattn_in['b_q'], 'L3_xattn_W_k': _L3_xattn_in['W_k'], 'L3_xattn_b_k': _L3_xattn_in['b_k'], 'L3_xattn_W_v': _L3_xattn_in['W_v'], 'L3_xattn_b_v': _L3_xattn_in['b_v'], 'L3_ffn_router_w': _L3_ffn_in['router_w'], 'L3_ffn_gate_up_w': _L3_ffn_in['gate_up_w'], 'L3_ffn_down_w': _L3_ffn_in['down_w'], 'L3_ffn_shared_gate_w': _L3_ffn_in['shared_gate_w'], 'L3_ffn_shared_up_w': _L3_ffn_in['shared_up_w'], 'L3_ffn_shared_down_w': _L3_ffn_in['shared_down_w']}

def reference(x, ctx_2048, itok_BxS_0_1023, mask_BxS2_bk0, mask_BxSxS2_ff0, g_xattn, g_ffn, L0_xattn_norm_w, L0_xattn_wq, L0_xattn_wk, L0_xattn_wv, L0_xattn_wo, L0_xattn_wg, L0_ffn_gate_w, L0_ffn_w1, L0_ffn_w2, L0_ffn_shared_w1, L0_ffn_shared_w2, L1_xattn_W_kvc, L1_xattn_W_dq, L1_xattn_W_uq, L1_xattn_W_qr, L1_xattn_W_uk, L1_xattn_W_kr, L1_xattn_W_uv, L1_xattn_W_o, L1_ffn_w_router, L1_ffn_we1, L1_ffn_we3, L1_ffn_we2, L1_ffn_ws1, L1_ffn_ws3, L1_ffn_ws2, L2_xattn_wq, L2_xattn_bq, L2_xattn_wk, L2_xattn_bk, L2_xattn_wv, L2_xattn_bv, L2_xattn_wo, L2_xattn_bo, L2_ffn_router_gate, L2_ffn_expert_gate_up, L2_ffn_expert_down, L3_xattn_W_fc, L3_xattn_b_fc, L3_xattn_W_q, L3_xattn_b_q, L3_xattn_W_k, L3_xattn_b_k, L3_xattn_W_v, L3_xattn_b_v, L3_ffn_router_w, L3_ffn_gate_up_w, L3_ffn_down_w, L3_ffn_shared_gate_w, L3_ffn_shared_up_w, L3_ffn_shared_down_w):
    import jax
    import jax.numpy as jnp

    def _L0_xattn_ref(hidden_states, memory_tokens, memory_mask, norm_w, wq, wk, wv, wo, wg):
        import jax, jax.numpy as jnp
        import numpy as np
        H = 256
        NH = 16
        HD = H // NH
        EPS = 1e-06

        def rmsnorm(x, w, eps=EPS):
            var = jnp.mean(x * x, axis=-1, keepdims=True)
            return x * jax.lax.rsqrt(var + eps) * w
        B, L, C = hidden_states.shape
        M = memory_tokens.shape[1]
        scale = HD ** (-0.5)
        x = rmsnorm(hidden_states, norm_w)
        q = (x @ wq.T).reshape(B, L, NH, HD)
        k = (memory_tokens @ wk.T).reshape(B, M, NH, HD)
        v = (memory_tokens @ wv.T).reshape(B, M, NH, HD)
        attn = jnp.einsum('blhd,bmhd->bhlm', q, k) * scale
        attn = jnp.where(memory_mask[:, None, None, :], attn, -jnp.inf)
        attn = jax.nn.softmax(attn, axis=-1)
        attn = jnp.nan_to_num(attn, nan=0.0)
        out = jnp.einsum('bhlm,bmhd->blhd', attn, v).reshape(B, L, C)
        out = out @ wo.T
        gate = jax.nn.sigmoid(x @ wg.T)
        return gate * out

    def _L0_ffn_ref(x, gate_w, w1, w2, shared_w1, shared_w2):
        import jax, jax.numpy as jnp
        import numpy as np
        H, I, E, TOP_K = (256, 176, 16, 6)
        IS = 352
        NORM_TOPK_PROB = False

        def _silu_and_mul(gate_up):
            d = gate_up.shape[-1] // 2
            g, u = (gate_up[..., :d], gate_up[..., d:])
            return jax.nn.silu(g) * u
        B, S, Hd = x.shape
        xf = x.reshape(-1, Hd)
        T = xf.shape[0]
        shared_out = _silu_and_mul(xf @ shared_w1.T) @ shared_w2.T
        logits = xf @ gate_w.T
        probs = jax.nn.softmax(logits.astype(jnp.float32), axis=-1)
        routing_weights, selected = jax.lax.top_k(probs, TOP_K)
        if NORM_TOPK_PROB:
            routing_weights = routing_weights / routing_weights.sum(-1, keepdims=True)
        combine = jnp.zeros((T, E), jnp.float32).at[jnp.arange(T)[:, None], selected].add(routing_weights).astype(x.dtype)
        gate_up = jnp.einsum('th,eoh->teo', xf, w1)
        act = _silu_and_mul(gate_up)
        moe_out = jnp.einsum('te,tei,ehi->th', combine, act, w2)
        return (moe_out + shared_out).reshape(B, S, Hd)

    def _L1_xattn_ref(q, kv, seg_id, W_kvc, W_dq, W_uq, W_qr, W_uk, W_kr, W_uv, W_o):
        import jax, jax.numpy as jnp
        import numpy as np
        B, Lq, Lk = (2, 512, 128)
        Q_DIM, KV_DIM = (256, 256)
        H, HD = (16, 128)
        KVC, QC, R = (64, 96, 64)
        LOOKBACK = 8
        NEG = -1e+30

        def _rope(x, L):
            half = x.shape[-1] // 2
            inv_freq = 1.0 / 10000.0 ** (jnp.arange(half, dtype=jnp.float32) / half)
            ang = jnp.arange(L, dtype=jnp.float32)[:, None] * inv_freq
            cos, sin = (jnp.cos(ang), jnp.sin(ang))
            x1, x2 = (x[..., :half], x[..., half:])
            return jnp.concatenate([x1 * cos - x2 * sin, x1 * sin + x2 * cos], axis=-1)
        b, lq, _ = q.shape
        lk = kv.shape[1]
        kv_c = kv @ W_kvc
        q_c = q @ W_dq
        q_nope = (q_c @ W_uq).reshape(b, lq, H, HD).transpose(0, 2, 1, 3)
        q_rope = (q_c @ W_qr).reshape(b, lq, H, R).transpose(0, 2, 1, 3)
        k_nope = (kv_c @ W_uk).reshape(b, lk, H, HD)
        v = (kv_c @ W_uv).reshape(b, lk, H, HD)
        k_rope = kv_c @ W_kr
        q_rope = _rope(q_rope, lq)
        k_rope = _rope(k_rope, lk)
        scale = 1.0 / np.sqrt(HD + R).astype(np.float32)
        scores = (jnp.einsum('bhqd,bkhd->bhqk', q_nope, k_nope) + jnp.einsum('bhqr,bkr->bhqk', q_rope, k_rope)) * scale
        k_ids = jnp.arange(lk)[None, None, :]
        qs = seg_id[:, :, None]
        good = (k_ids <= qs) & (k_ids >= qs - LOOKBACK)
        scores = jnp.where(good[:, None, :, :], scores, NEG)
        attn = jax.nn.softmax(scores, axis=-1)
        out = jnp.einsum('bhqk,bkhd->bqhd', attn, v).reshape(b, lq, H * HD)
        return out @ W_o

    def _L1_ffn_ref(x, w_router, we1, we3, we2, ws1, ws3, ws2):
        import jax, jax.numpy as jnp
        import numpy as np
        TOP_K = 4
        B, S, D = x.shape
        T = B * S
        E = w_router.shape[1]
        xt = x.reshape(T, D)
        probs = jax.nn.softmax(xt @ w_router, axis=-1)
        top_w, top_i = jax.lax.top_k(probs, TOP_K)
        top_w = top_w / jnp.sum(top_w, axis=-1, keepdims=True)
        cw = jnp.zeros((T, E), xt.dtype).at[jnp.arange(T)[:, None], top_i].add(top_w)
        g = jax.nn.silu(jnp.einsum('td,edh->teh', xt, we1)) * jnp.einsum('td,edh->teh', xt, we3)
        g = g * cw[:, :, None]
        moe_out = jnp.einsum('teh,ehd->td', g, we2)
        shared = jax.nn.silu(xt @ ws1) * (xt @ ws3) @ ws2
        k = TOP_K
        out = shared / (k + 1) + moe_out * (k / (k + 1))
        return out.reshape(B, S, D)

    def _L2_xattn_ref(x, cond, mask, wq, bq, wk, bk, wv, bv, wo, bo):
        import jax, jax.numpy as jnp
        import numpy as np
        NUM_HEADS = 16
        EPS = 1e-08

        def _dyn_quant(x):
            s = jnp.maximum(jnp.max(jnp.abs(x), axis=-1, keepdims=True) / 127.0, EPS)
            q = jnp.clip(jnp.round(x / s), -127.0, 127.0)
            return (q, s)

        def _quant_weight(w):
            s = jnp.maximum(jnp.max(jnp.abs(w), axis=1, keepdims=True) / 127.0, EPS)
            q = jnp.clip(jnp.round(w / s), -127.0, 127.0)
            return (q, s)

        def _w8a8_linear(x, w, b):
            qx, sx = _dyn_quant(x)
            qw, sw = _quant_weight(w)
            y = jnp.einsum('bnc,oc->bno', qx, qw) * (sx * sw[:, 0])
            return y + b
        B, N, C = x.shape
        L = cond.shape[1]
        H = NUM_HEADS
        D = C // H
        inv_sqrt_d = np.float32(1.0 / np.sqrt(D))
        q = _w8a8_linear(x, wq, bq).reshape(B, N, H, D).transpose(0, 2, 1, 3)
        k = (cond @ wk.T + bk).reshape(B, L, H, D).transpose(0, 2, 1, 3)
        v = (cond @ wv.T + bv).reshape(B, L, H, D).transpose(0, 2, 1, 3)
        scores = jnp.einsum('bhnd,bhld->bhnl', q, k) * inv_sqrt_d + mask[:, None]
        attn = jax.nn.softmax(scores, axis=-1)
        o = jnp.einsum('bhnl,bhld->bhnd', attn, v)
        o = o.transpose(0, 2, 1, 3).reshape(B, N, C)
        return _w8a8_linear(o, wo, bo)

    def _L2_ffn_ref(hidden_states, router_gate, expert_gate_up, expert_down):
        import jax, jax.numpy as jnp
        import numpy as np
        NUM_EXPERTS = 8
        TOP_K = 2
        MODEL_DIM = 256
        INTER_DIM = 128
        GATE_SCALE = 1.0
        UP_SCALE = 0.0
        orig_shape = hidden_states.shape
        hs = hidden_states.reshape(-1, orig_shape[-1])
        T = hs.shape[0]
        logits = hs @ router_gate.T
        probs = jax.nn.softmax(logits.astype(jnp.float32), axis=-1)
        topk_scores, topk_idx = jax.lax.top_k(probs, TOP_K)
        topk_scores = topk_scores / jnp.sum(topk_scores, axis=-1, keepdims=True)
        scores_f = topk_scores.T.reshape(-1).astype(hs.dtype)
        ids_f = topk_idx.T.reshape(-1)
        order = jnp.argsort(ids_f)
        sorted_ids = ids_f[order]
        scores_sorted = scores_f[order]
        token_slots = order % T
        x = hs[token_slots]
        inter = jnp.zeros((x.shape[0], 2 * INTER_DIM), x.dtype)
        for e in range(NUM_EXPERTS):
            m = (sorted_ids == e)[:, None]
            inter = inter + jnp.where(m, x, 0) @ expert_gate_up[e]
        gate = inter[..., 0::2]
        up = inter[..., 1::2]
        h = (up + UP_SCALE) * jax.nn.silu(gate * GATE_SCALE)
        out_rows = jnp.zeros((x.shape[0], MODEL_DIM), x.dtype)
        for e in range(NUM_EXPERTS):
            m = (sorted_ids == e)[:, None]
            out_rows = out_rows + jnp.where(m, h, 0) @ expert_down[e]
        out = jnp.zeros_like(hs).at[token_slots].add(out_rows * scores_sorted[:, None])
        return out.reshape(orig_shape)

    def _L3_xattn_ref(ref_feat, sup_feat, W_fc, b_fc, W_q, b_q, W_k, b_k, W_v, b_v):
        import jax, jax.numpy as jnp
        import numpy as np
        FEAT = 256
        G = 16
        DG = FEAT // G
        bs, N1, _ = ref_feat.shape
        sup = jax.nn.relu(sup_feat @ W_fc.T + b_fc)
        ref = jax.nn.relu(ref_feat @ W_fc.T + b_fc)
        q = (ref @ W_q.T + b_q).reshape(bs, N1, G, DG)
        k = (sup @ W_k.T + b_k).reshape(bs, -1, G, DG)
        aff = jnp.einsum('bqhd,bkhd->bhqk', q, k) * (1.0 / np.sqrt(DG))
        p = jax.nn.softmax(aff, axis=-1)
        out_h = jnp.einsum('bhqk,bkf->bhqf', p, sup)
        Wv = W_v.reshape(G, DG, FEAT)
        attn = jnp.einsum('bhqf,hjf->bqhj', out_h, Wv).reshape(bs, N1, FEAT) + b_v
        return ref + attn

    def _L3_ffn_ref(hidden_states, router_w, gate_up_w, down_w, shared_gate_w, shared_up_w, shared_down_w):
        import jax, jax.numpy as jnp
        import numpy as np
        B, S, D, I, E, K = (4, 128, 256, 128, 8, 2)
        Bb, Ss, Dd = hidden_states.shape
        x = hidden_states.reshape(-1, Dd)
        T = x.shape[0]
        shared = jax.nn.silu(x @ shared_gate_w) * (x @ shared_up_w) @ shared_down_w
        logits = x @ router_w
        top_val, top_idx = jax.lax.top_k(logits, K)
        probs = jnp.zeros_like(logits).at[jnp.arange(T)[:, None], top_idx].set(jax.nn.sigmoid(top_val))
        xin = probs.T[:, :, None] * x[None]
        gu = jnp.einsum('etd,edf->etf', xin, gate_up_w)
        gate, up = jnp.split(gu, 2, axis=-1)
        h = jax.nn.silu(gate) * up
        expert_out = jnp.einsum('eti,eid->etd', h, down_w)
        combined = shared + expert_out.sum(axis=0)
        return combined.reshape(Bb, Ss, Dd)
    x = x + jnp.tanh(g_xattn[0]) * _L0_xattn_ref(_layernorm(x, axis=-1), ctx_2048, mask_BxS2_bk0, L0_xattn_norm_w, L0_xattn_wq, L0_xattn_wk, L0_xattn_wv, L0_xattn_wo, L0_xattn_wg)
    x = x + jnp.tanh(g_ffn[0]) * _L0_ffn_ref(_layernorm(x, axis=-1), L0_ffn_gate_w, L0_ffn_w1, L0_ffn_w2, L0_ffn_shared_w1, L0_ffn_shared_w2)
    x = x + jnp.tanh(g_xattn[1]) * _L1_xattn_ref(_layernorm(x, axis=-1), ctx_2048, itok_BxS_0_1023, L1_xattn_W_kvc, L1_xattn_W_dq, L1_xattn_W_uq, L1_xattn_W_qr, L1_xattn_W_uk, L1_xattn_W_kr, L1_xattn_W_uv, L1_xattn_W_o)
    x = x + jnp.tanh(g_ffn[1]) * _L1_ffn_ref(_layernorm(x, axis=-1), L1_ffn_w_router, L1_ffn_we1, L1_ffn_we3, L1_ffn_we2, L1_ffn_ws1, L1_ffn_ws3, L1_ffn_ws2)
    x = x + jnp.tanh(g_xattn[2]) * _L2_xattn_ref(_layernorm(x, axis=-1), ctx_2048, mask_BxSxS2_ff0, L2_xattn_wq, L2_xattn_bq, L2_xattn_wk, L2_xattn_bk, L2_xattn_wv, L2_xattn_bv, L2_xattn_wo, L2_xattn_bo)
    x = x + jnp.tanh(g_ffn[2]) * _L2_ffn_ref(_layernorm(x, axis=-1), L2_ffn_router_gate, L2_ffn_expert_gate_up, L2_ffn_expert_down)
    x = x + jnp.tanh(g_xattn[3]) * _L3_xattn_ref(_layernorm(x, axis=-1), ctx_2048, L3_xattn_W_fc, L3_xattn_b_fc, L3_xattn_W_q, L3_xattn_b_q, L3_xattn_W_k, L3_xattn_b_k, L3_xattn_W_v, L3_xattn_b_v)
    x = x + jnp.tanh(g_ffn[3]) * _L3_ffn_ref(_layernorm(x, axis=-1), L3_ffn_router_w, L3_ffn_gate_up_w, L3_ffn_down_w, L3_ffn_shared_gate_w, L3_ffn_shared_up_w, L3_ffn_shared_down_w)
    return x

_drawn_inputs = setup_inputs


def setup_inputs(seed=0):
    import zlib

    import numpy as np

    out = dict(_drawn_inputs(seed))
    spreads = {'L0_xattn_norm_w': (1.0, 0.2),
     'L2_xattn_bq': (0.0, 0.8),
     'L2_xattn_bk': (0.0, 0.8),
     'L2_xattn_bv': (0.0, 0.1),
     'L2_xattn_bo': (0.0, 0.1),
     'L3_xattn_b_fc': (0.0, 0.1),
     'L3_xattn_b_q': (0.0, 0.8),
     'L3_xattn_b_k': (0.0, 0.8),
     'L3_xattn_b_v': (0.0, 0.1)}
    factors = {'L0_ffn_gate_w': 6.465,
     'L0_ffn_w1': 3.241,
     'L0_ffn_w2': 5.253,
     'L2_xattn_wq': 8.0,
     'L2_xattn_wk': 8.0,
     'L2_ffn_router_gate': 5.948,
     'L2_ffn_expert_gate_up': 2.752,
     'L2_ffn_expert_down': 2.903,
     'L3_xattn_W_q': 3.442,
     'L3_xattn_W_k': 8.0}
    for name, (base, spread) in spreads.items():
        noise = np.random.default_rng([zlib.crc32(name.encode()), seed]).standard_normal(out[name].shape)
        drawn = base * np.exp(spread * noise) if base else spread * noise
        out[name] = jnp.asarray(drawn.astype(out[name].dtype))
    for name, factor in factors.items():
        out[name] = (out[name] * factor).astype(out[name].dtype)
    return out
```

```python
import numpy as np
from contextlib import ExitStack
import concourse.bass as bass
from concourse import mybir

NSUB = 8

NB, NQ, QP = 8, 56, 64
TT, D, KT = 4, 256, 2
NTOK = NB * QP
NCTX, CH, NCH = 1500, 500, 3
CT, NCT = 125, 12
NH, NP, HD = 16, 8, 16
NEG = -1.0e30

MOE = [dict(I=88, U=36, E=16, K=6, per=2), dict(I=128, U=20, E=16, K=4, per=1),
       dict(I=128, U=8, E=8, K=2, per=1), dict(I=128, U=9, E=8, K=2, per=1)]
MOE_BASE = [0, 36, 56, 64]

LOOK, NW = 8, 9
GT, NG = 8, 7
GW = GT * NW
WB = NQ * NW
GR, NGT = 126, 4
R, QC, HDL = 64, 96, 128
SCALE1 = float(1.0 / np.sqrt(192.0).astype(np.float32))


def flamingo_kernel(nc, A, out):
    F32, I32, U8 = mybir.dt.float32, mybir.dt.int32, mybir.dt.uint8
    U32 = mybir.dt.uint32
    ALU, ACT, AX = mybir.AluOpType, mybir.ActivationFunctionType, mybir.AxisListType
    ctx = ExitStack()
    with ctx:
        def sb(name, shape, dt=F32):
            return ctx.enter_context(nc.sbuf_tensor(name, shape, dt))

        sems = {}

        def sem(name):
            if name not in sems:
                sems[name] = ctx.enter_context(nc.semaphore(name))
            return sems[name]

        x = sb("x", [128, TT, D])
        h = sb("h", [128, TT, D])
        onat = sb("onat", [128, TT, D])
        acc = sb("acc", [128, TT, D])
        tmp = sb("tmp", [128, TT, D])
        hT = sb("hT", [128, KT, NTOK])
        qT = sb("qT", [128, KT, NTOK])
        oT = sb("oT", [128, KT, NTOK])
        ident = sb("ident", [128, 128])
        headmask = sb("headmask", [128, NP])
        tg = sb("tg", [128, 8])
        stats = sb("stats", [128, TT, 6])
        mv = sb("mv", [128, TT, 2])
        sm = sb("sm", [128, 16, TT])
        cols = sb("cols", [128, 16])
        rows = sb("rows", [128, 3, D])
        lg = sb("lg", [128, 10, TT, 16])
        top8 = sb("top8", [128, TT, 8])
        cw = sb("cw", [128, TT, 36])
        w0 = sb("w0", [128, 5, KT, D])
        w2 = sb("w2", [128, 2, KT, D])
        w2n = sb("w2n", [128, 4, D])
        w2T = sb("w2T", [128, 4, D])
        w3 = w0[:, 0:4]
        gw = sb("gw", [128, 4, KT, 16])
        wu = sb("wu", [128, 2, KT, 2 * 128])
        wd = sb("wd", [128, 2, D])

        ctxT = sb("ctxT", [128, 2, KT, NCTX])
        kT = sb("kT", [128, 2, KT, NCTX])
        v = sb("v", [128, 2, NCT, D])
        supT = sb("supT", [128, KT, NCTX])
        maskf = supT
        maskraw = sb("maskraw", [128, 2, NCTX // 4], I32)
        area = sb("area", [128, 4 * NCTX + 2 * NCH * 512])
        Sb = area[:, 0:4 * NCTX].rearrange("p (r n) -> p r n", r=4)
        PT = area[:, 4 * NCTX:].rearrange("p (r g n) -> p r g n", r=2, g=NCH)
        Qb = sb("Qb", [128, 2, KT, 8 * QP])
        mx = sb("mx", [128, 4, 4])
        nm = sb("nm", [128, 4])
        rsum = sb("rsum", [128, 2, NP])
        rinv = sb("rinv", [128, 2, NP])
        oTs = sb("oTs", [128, D])

        meanT = sb("meanT", [128, KT, NB])
        segf = sb("segf", [128, NB * NQ])
        seg = qT[:, 0, 0:NB * NQ].bitcast(I32)
        gidx = sb("gidx", [128, 3, NB * NGT])
        gseg = sb("gseg", [128, NB * NGT], I32)
        grow = sb("grow", [128, NB * NGT], I32)
        grow4 = sb("grow4", [128, 2, NGT], I32)
        anyv = sb("anyv", [128, 2, NQ])
        sm1 = sb("sm1", [128, 4, NG])
        flags = sb("flags", [128, 104])
        mkv = sb("mkv", [128, NB])

        kflat = kT[:, :, :, :].rearrange("p a k n -> p (a k n)")
        wuqT = kflat[:, 0:1536].rearrange("p (h n) -> p h n", h=16)
        wukT = kflat[:, 1536:2560].rearrange("p (h n) -> p h n", h=16)
        wuvT = kflat[:, 2560:3584].rearrange("p (h n) -> p h n", h=16)
        wqr2 = kflat[0:QC, 3584:4608].rearrange("p (h n) -> p h n", h=16)
        wdq = kflat[:, 4608:4800].rearrange("p (k n) -> p k n", k=2)
        wkvc = kflat[:, 4800:4928].rearrange("p (k n) -> p k n", k=2)
        wkr = kflat[0:R, 4928:5056]
        wstk = kflat[:, 5056:5120]
        blk = kflat[:, 5120:5192]
        jrow = kflat[:, 5192:5201]
        vflat = v[:, :, :, :].rearrange("p a j d -> p (a j d)")
        wo1 = vflat[:, 0:4096].rearrange("p (h n) -> p h n", h=16)
        ocT = vflat[:, 0:4096].rearrange("p (h n) -> p h n", h=8)
        wcomb = vflat[0:QC, 4096:6144].rearrange("p (h n) -> p h n", h=16)
        cflat = ctxT[:, :, :, :].rearrange("p a k n -> p (a k n)")
        wuvo = cflat[:, 0:2048].rearrange("p (h n) -> p h n", h=8)
        qcT = cflat[0:QC, 2048:2560]
        G = cflat[0:GR, 2560:5632].rearrange("p (a t n) -> p a t n", a=2, t=NGT)
        sflat = supT[:, :, :].rearrange("p k n -> p (k n)")
        gT = sflat[:, 0:1008].rearrange("p (k n) -> p k n", k=2)
        csT, prod, keff = sflat[:, 1008:1512], sflat[:, 1512:2016], sflat[:, 2016:2520]
        qeff = area[:, 0:8192].rearrange("p (b h q) -> p b h q", b=NB, h=16)
        qflat = Qb[:, :, :, :].rearrange("p a k n -> p (a k n)")
        qb1 = qflat[:, 0:1024].rearrange("p (q h) -> p q h", h=16)
        P1, madd = qflat[:, 1024:1528], qflat[:, 1528:2032]
        kvn = oT[0:GW, :, :].rearrange("p k n -> p (k n)")[:, 0:896].rearrange("p (g c) -> p g c", g=NG)
        PT1 = qT[0:GW, :, :].rearrange("p k n -> p (k n)")[:, 0:896].rearrange("p (g c) -> p g c", g=NG)
        aflat = acc[:, :, :].rearrange("p t d -> p (t d)")
        kid, valid = aflat[:, 0:504], aflat[:, 504:1008]
        cosq = tmp[:, 0:2, :].rearrange("p t d -> p (t d)")
        sinq = tmp[:, 2:4, :].rearrange("p t d -> p (t d)")
        rope2 = onat[:, 0:2, :].rearrange("p t d -> p (t d)")

        sg = Sb[:, 0, 0:1024].rearrange("p (k n) -> p k n", k=2)
        act_b = Sb[:, 1, 0:1024].rearrange("p (k n) -> p k n", k=2)
        pb = Sb[:, 2, 0:1024].rearrange("p (k n) -> p k n", k=2)
        xin = PT[:, :, 0:2, :]

        P = [ctx.enter_context(nc.psum_tensor(f"P{i}", [128, 512], F32)) for i in range(8)]

        block = ctx.enter_context(nc.Block())
        ATT = {0: 0, 2: 1, 3: 2}
        NPROJ = {0: 12, 2: 12, 3: 18}

        @block.gpsimd
        def _(pool):
            pool.wait_ge(sem("sub_done"), 1)
            for dst, name in ((wuqT, "wuqT"), (wukT, "wukT"), (wuvT, "wuvT"), (wqr2, "wqr2"), (wdq, "wdq"),
                              (wkvc, "wkvc"), (wkr, "wkr"), (wstk, "wstk"), (blk, "blk"), (wo1, "wo1"),
                              (wcomb[:, :, 64:128], "wqr"), (cosq[64:128, :], "cosq"), (sinq[64:128, :], "sinq")):
                pool.dma_start(dst, A[name]).then_inc(sem("w1_in"), 16)
            pool.dma_start(w3, A["w3"]).then_inc(sem("w1_in"), 16)
            pool.dma_start(jrow, A["jrow"].partition_broadcast(128)).then_inc(sem("w1_in"), 16)
            pool.wait_ge(sem("rows_ready"), 1)
            with pool.Fori(0, NB // 2) as i:
                for bi in range(2):
                    pool.wait_ge(sem("g_turned"), i * 2 + (bi + 1))
                    nc.gpsimd.tensor_copy(grow4[:, bi, :], grow[:, bass.ds(i * 8 + 4 * bi, NGT)]).then_inc(sem("row_copied"), 1)
                    pool.wait_ge(sem("row_copied"), i * 2 + (bi + 1))
                    pool.sem_inc(sem("waits_met"), 1)
                    for t in range(NGT):
                        pool.indirect_dma_start(out=G[:, bi, t, :], out_offset=None, in_=A["ctxrows"],
                                                in_offset=bass.IndirectOffsetOnAxis(
                                                    ap=grow4[0:GR, bi, t:t + 1].bitcast(U32), axis=0)
                                                ).then_inc(sem(f"g_in{bi}"), 16)

        @block.sync
        def _(sp):
            sp.wait_ge(sem("x_cleared"), 1)
            for b in range(NB):
                sp.dma_start(x[QP * (b % 2):QP * (b % 2) + NQ, b // 2, :], A["x"][b]).then_inc(sem("x_in"), 16)
            for dst, name in ((ident[:, :], "ident"), (headmask[:, :], "headmask"), (cols[:, :], "cols"),
                              (w2n[:, :, :], "w2n"), (w0[:, :, :, :], "w0"), (gw[:, :, :, :], "gw"),
                              (w2[:, :, :, :], "w2")):
                sp.dma_start(dst, A[name]).then_inc(sem("const_in"), 16)
            sp.dma_start(tg[:, :], A["gates"].partition_broadcast(128)).then_inc(sem("const_in"), 16)
            sp.dma_start(seg, A["seg"].partition_broadcast(128)).then_inc(sem("const_in"), 16)
            sp.dma_start(gseg[0:GR, :], A["gseg"]).then_inc(sem("const_in"), 16)
            sp.dma_start(gidx[0:GR, 1:3, :], A["gconst"]).then_inc(sem("const_in"), 16)
            for r in range(3):
                sp.dma_start(rows[:, r, :], A["rows"][r].partition_broadcast(128)).then_inc(sem("const_in"), 16)

            def attention_loads(l):
                a = ATT[l]
                if l:
                    sp.wait_ge(sem("sub_done"), 2 * l)
                with sp.Fori(0, NB // 2) as i:
                    for bi in range(2):
                        sp.wait_ge(sem("proj_done"), (i * 2 + bi) * NPROJ[l] + ((0, 96, 192)[a] + 18 - NPROJ[l]))
                        sp.sem_inc(sem("waits_met"), 1)
                        if l == 0:
                            sp.wait_ge(sem("mean_done"), i * 2 + (bi + 1))
                        sp.sem_inc(sem("waits_met"), 1)
                        sp.dma_start(ctxT[:, bi], A["ctxT"][i * 2 + bi]).then_inc(sem(f"ctx_in{bi}"), 16)
                        if l == 0:
                            sp.wait_ge(sem("mask_used"), i * 2 + (bi + 1))
                            sp.sem_inc(sem("waits_met"), 1)
                            sp.dma_start(maskraw[:, bi, :],
                                         A["mask0"][i * 2 + bi].partition_broadcast(128)).then_inc(sem(f"mask_in{bi}"), 16)
                        if l == 2:
                            sp.wait_ge(sem("mask_cleared"), 1)
                            sp.wait_ge(sem("mask_used"), i * 2 + (8 + bi + 1))
                            sp.sem_inc(sem("waits_met"), 1)
                            for half in range(2):
                                sp.dma_start(maskf[QP * half:QP * half + NQ, bi, :],
                                             A["mask2"][i * 2 + bi]).then_inc(sem(f"mask_in{bi}"), 16)

            def mixture_loads(l):
                I, U, base = MOE[l]["I"], MOE[l]["U"], MOE_BASE[l]

                def unit(k, u):
                    sp.wait_ge(sem("down_done"), u + base)
                    sp.sem_inc(sem("waits_met"), 1)
                    sp.dma_start(wu[:, k, :, 0:2 * I], A[f"up{l}"][u]).then_inc(sem(f"w_in{k}"), 16)
                    sp.dma_start(wd[0:I, k, :], A[f"down{l}"][u]).then_inc(sem(f"w_in{k}"), 16)
                    if l == 3:
                        sp.wait_ge(sem("xin_ready"), u - k)
                        sp.sem_inc(sem("waits_met"), 1)
                        sp.dma_start(pb[:, k, :], A["prT"][u].partition_broadcast(128)).then_inc(sem(f"pb_in{k}"), 16)

                if l == 3:
                    sp.wait_ge(sem("prT_sb"), 1)
                    sp.dma_start(A["prT"], qT[0:8, 0, :]).then_inc(sem("prT_out"), 16)
                    sp.wait_ge(sem("prT_out"), 16)
                with sp.Fori(0, U // 2) as i:
                    unit(0, i * 2)
                    unit(1, i * 2 + 1)
                if U % 2:
                    k, u = 0, U - 1
                    sp.wait_ge(sem("down_done"), u + base)
                    sp.dma_start(wu[:, k, :, 0:2 * I], A[f"up{l}"][u]).then_inc(sem(f"w_in{k}"), 16)
                    sp.dma_start(wd[0:I, k, :], A[f"down{l}"][u]).then_inc(sem(f"w_in{k}"), 16)

            for s in range(NSUB):
                l = s // 2
                if s % 2 == 0 and l in ATT:
                    attention_loads(l)
                elif s % 2:
                    mixture_loads(l)
            sp.wait_ge(sem("sub_done"), NSUB)
            for b in range(NB):
                sp.dma_start(out[b], x[QP * (b % 2):QP * (b % 2) + NQ, b // 2, :]).then_inc(sem("stored"), 16)
            sp.wait_ge(sem("stored"), 16 * NB)

        @block.tensor
        def _(pe):
            n_tr = [0]

            def tokens_to_T(src):
                for k in range(KT):
                    for t in range(TT):
                        last = nc.tensor.transpose(P[6 + k][:, 128 * t:128 * t + 128],
                                                   src[:, t, 128 * k:128 * k + 128], ident[:, :])
                last.then_inc(sem("tr_psum"), 1)
                n_tr[0] += 1

            def wait_T(n=None):
                n = n or n_tr[0]
                pe.wait_ge(sem("tr_act"), n)
                pe.wait_ge(sem("tr_dve"), n)

            def attention(l):
                a = ATT[l]
                wk, wv = (w0[:, 1], w0[:, 2]) if l == 0 else (w2[:, 0], w2[:, 1]) if l == 2 else (w3[:, 2], w3[:, 3])
                na, nv = (0, 48, 96)[a], 48 * a
                pa = NPROJ[l] - 6

                def project(B, i, bi):
                    pe.wait_ge(sem(f"ctx_in{bi}"), i * 16 + 16 * (4 * a + 1))
                    g = 0

                    def bank_free(g):
                        if g < 2:
                            pe.wait_ge(sem("v_ready"), B * 6 + nv)
                        elif g - 2 < pa:
                            pe.wait_ge(sem("k_ready"), B * pa + (na + g - 1))
                        else:
                            pe.wait_ge(sem("v_ready"), B * 6 + (nv + g - 1 - pa))

                    src = ctxT[:, bi]
                    if l == 3:
                        for o in range(KT):
                            for c in range(NCH):
                                bank_free(g)
                                for k in range(KT):
                                    last = nc.tensor.matmul(P[6 + g % 2][:, 0:CH], w3[:, 0, k, 128 * o:128 * o + 128],
                                                            src[:, k, CH * c:CH * c + CH], start=k == 0, stop=k == 1)
                                last.then_inc(sem("proj_done"), 1)
                                g += 1
                        pe.wait_ge(sem("k_ready"), B * pa + (na + 6))
                        src = supT[:, :, :]
                    for o in range(KT):
                        for c in range(NCH):
                            bank_free(g)
                            for k in range(KT):
                                last = nc.tensor.matmul(P[6 + g % 2][:, 0:CH], wk[:, k, 128 * o:128 * o + 128],
                                                        src[:, k, CH * c:CH * c + CH], start=k == 0, stop=k == 1)
                            last.then_inc(sem("proj_done"), 1)
                            g += 1
                    for j in range(6):
                        bank_free(g)
                        for jj in range(2):
                            c0 = CT * (2 * j + jj)
                            for k in range(KT):
                                last = nc.tensor.matmul(P[6 + g % 2][0:CT, D * jj:D * jj + D],
                                                        src[:, k, c0:c0 + CT], wv[:, k, :], start=k == 0, stop=k == 1)
                        last.then_inc(sem("proj_done"), 1)
                        g += 1

                def scores(n, B, bi, p):
                    if p == 0:
                        pe.wait_ge(sem("k_ready"), B * pa + (na + pa))
                    if p == 0:
                        pe.wait_ge(sem("qb_ready"), B * 2 + (16 * a + 2))
                    for c in range(NCH):
                        pe.wait_ge(sem("s_taken"), n * 3 + (c + 1))
                        nc.tensor.matmul(P[c][:, 0:CH], Qb[:, bi, p // 4, 128 * (p % 4):128 * (p % 4) + 128],
                                         kT[:, bi, p // 4, CH * c:CH * c + CH], start=True, stop=True
                                         ).then_inc(sem("s_done"), 1)

                def turn(n, p):
                    pe.wait_ge(sem("exp_done"), n + 1)
                    for g in range(NCH):
                        if g == 0:
                            pe.wait_ge(sem("pt_dve"), n)
                        elif g == 1:
                            pe.wait_ge(sem("pt_act"), n * 2)
                        else:
                            pe.wait_ge(sem("pt_act"), n * 2 + 1)
                        for j in range(4):
                            c0 = CT * (4 * g + j)
                            last = nc.tensor.transpose(P[3 + (3 * p + g) % 2][0:CT, 128 * j:128 * j + 128],
                                                       Sb[:, p % 4, c0:c0 + CT], ident[:, :])
                        last.then_inc(sem("t_done"), 1)

                def values(n, B, bi, p):
                    if p == 0:
                        pe.wait_ge(sem("v_ready"), B * 6 + (nv + 6))
                        pe.wait_ge(sem("o_taken"), B + 8 * a)
                    pe.wait_ge(sem("pt_act"), n * 2 + 2)
                    pe.wait_ge(sem("pt_dve"), n + 1)
                    q = p % 4
                    for j in range(NCT):
                        last = nc.tensor.matmul(P[5][32 * q:32 * q + 32, 128 * (p // 4):128 * (p // 4) + 128],
                                                v[0:CT, bi, j, 32 * p:32 * p + 32],
                                                PT[0:CT, p % 2, j // 4, 128 * (j % 4):128 * (j % 4) + 128],
                                                start=j == 0, stop=j == NCT - 1)
                    last.then_inc(sem("pv_done"), 1)

                with pe.Fori(0, NB // 2) as i:
                    for bi in range(2):
                        B = i * 2 + bi
                        n0 = i * 16 + (64 * a + 8 * bi)
                        if bi == 0:
                            project(B, i, 0)
                        for p in range(NP):
                            scores(n0 + p, B, bi, p)
                            if p >= 1:
                                turn(n0 + (p - 1), p - 1)
                            if p >= 2:
                                values(n0 + (p - 2), B, bi, p - 2)
                        if bi == 0:
                            project(B + 1, i, 1)
                        turn(n0 + 7, 7)
                        values(n0 + 6, B, bi, 6)
                        values(n0 + 7, B, bi, 7)
                        pe.wait_ge(sem("oT_sb"), B + (8 * a + 1))
                        for k in range(KT):
                            last = nc.tensor.transpose(P[5][:, D + 128 * k:D + 128 * k + 128],
                                                       oTs[:, 128 * k:128 * k + 128], ident[:, :])
                        last.then_inc(sem("on_psum"), 1)

            def mixture(l):
                I, U, base, E = MOE[l]["I"], MOE[l]["U"], MOE_BASE[l], MOE[l]["E"]
                wait_T()
                for t in range(TT):
                    for k in range(KT):
                        last = nc.tensor.matmul(P[7][:, 16 * t:16 * t + E], hT[:, k, 128 * t:128 * t + 128],
                                                gw[:, l, k, 0:E], start=k == 0, stop=k == 1)
                last.then_inc(sem("logits"), 1)
                if l == 3:
                    pe.wait_ge(sem("cw_ready"), 4)
                    for t in range(TT):
                        last = nc.tensor.transpose(P[6][0:8, 128 * t:128 * t + 128], lg[:, 9, t, 0:8], ident[:, :])
                    last.then_inc(sem("prT_psum"), 1)

                def up(k, u, i, xin_used):
                    pe.wait_ge(sem(f"w_in{k}"), i * 32 + 32 * (base // 2 + 1))
                    pe.wait_ge(sem("act_ready"), u + base)
                    if xin_used:
                        pe.wait_ge(sem("xin_ready"), u + 1)
                    rhs = xin[:, k] if xin_used else hT
                    for half in range(2):
                        for kk in range(KT):
                            last = nc.tensor.matmul(P[k + 2 * half][0:I, :], wu[:, k, kk, I * half:I * half + I],
                                                    rhs[:, kk, :], start=kk == 0, stop=kk == 1)
                        last.then_inc(sem("gu_done"), 1)

                def down(k, u):
                    pe.wait_ge(sem("act_ready"), u + (base + 2))
                    pe.wait_ge(sem("acc_done"), u + base)
                    for t in range(TT):
                        last = nc.tensor.matmul(P[4 + 2 * k + t // 2][:, D * (t % 2):D * (t % 2) + D],
                                                act_b[0:I, k, 128 * t:128 * t + 128], wd[0:I, k, :],
                                                start=True, stop=True)
                    last.then_inc(sem("down_done"), 1)

                with pe.Fori(0, U // 2) as i:
                    up(0, i * 2, i, l == 3)
                    up(1, i * 2 + 1, i, l == 3)
                    down(0, i * 2)
                    down(1, i * 2 + 1)
                if U % 2:
                    up(0, U - 1, U // 2, False)
                    down(0, U - 1)

            def window():
                pe.wait_ge(sem("w1_in"), 16 * 15)
                for hh in range(NH):
                    last = nc.tensor.matmul(P[hh // 8][0:QC, 64 * (hh % 8):64 * (hh % 8) + 64], wuqT[:, hh, :],
                                            wukT[:, hh, :], start=True, stop=True)
                for hh in range(NH):
                    r, hp = 64 * (hh % 2), hh // 2
                    last = nc.tensor.matmul(P[2 + hp // 2][r:r + 64, D * (hp % 2):D * (hp % 2) + D], wuvT[:, hh, :],
                                            wo1[:, hh, :], start=True, stop=True)
                wait_T()
                for k in range(KT):
                    last = nc.tensor.matmul(P[6][0:QC, :], wdq[:, k, :], hT[:, k, :], start=k == 0, stop=k == 1)
                for k in range(KT):
                    last = nc.tensor.matmul(P[7][0:R, 0:NB], wkvc[:, k, :], meanT[:, k, :], start=k == 0, stop=k == 1)
                last.then_inc(sem("pre1_psum"), 1)
                pe.wait_ge(sem("pre1_act"), 1)
                pe.wait_ge(sem("pre1_dve"), 1)
                for hh in range(NH):
                    r = hh % 4
                    if hh >= 4:
                        pe.wait_ge(sem("qn_taken"), hh - 3)
                        pe.wait_ge(sem("qr_taken"), hh - 3)
                    nc.tensor.matmul(P[r][:, :], wcomb[:, hh, :], qcT, start=True, stop=True)
                    nc.tensor.matmul(P[4 + r][64:128, :], wqr2[:, hh, :], qcT, start=True, stop=True
                                     ).then_inc(sem("qh_psum"), 1)
                pe.wait_ge(sem("qn_taken"), NH)
                pe.wait_ge(sem("qr_taken"), NH)
                with pe.Fori(0, NB // 2) as i:
                    for bi in range(2):
                        b = i * 2 + bi
                        pe.wait_ge(sem(f"g_in{bi}"), i * 64 + 64)
                        pe.wait_ge(sem("p1_taken"), b)
                        for f in range(3):
                            for t in range(NGT):
                                last = nc.tensor.transpose(P[f][:, GR * t:GR * t + GR],
                                                           G[:, bi, t, 128 * f:128 * f + 128], ident[0:GR, 0:GR])
                        last.then_inc(sem("g_turned"), 1)
                        pe.wait_ge(sem("g_act"), b + 1)
                        pe.wait_ge(sem("g_dve"), b + 1)
                        for k in range(KT):
                            last = nc.tensor.matmul(P[5][0:R, 0:WB], wkvc[:, k, :], gT[:, k, :], start=k == 0, stop=k == 1)
                        last.then_inc(sem("kv_psum"), 1)
                        pe.wait_ge(sem("kv_sb"), b + 1)
                        nc.tensor.matmul(P[6][:, 0:WB], wkr, keff[0:R, :], start=True, stop=True).then_inc(sem("kr_psum"), 1)
                        for g in range(NG):
                            last = nc.tensor.transpose(P[7][0:GW, R * g:R * g + R], keff[0:R, GW * g:GW * g + GW],
                                                       ident[0:R, 0:R])
                        last.then_inc(sem("kvn_psum"), 1)
                        pe.wait_ge(sem("prod_sb"), b + 1)
                        nc.tensor.matmul(P[5][64:128, 0:WB], wstk, prod, start=True, stop=True).then_inc(sem("krs_psum"), 1)
                        pe.wait_ge(sem("keff_sb"), b + 1)
                        pe.wait_ge(sem("qb1_sb"), b + 1)
                        for g in range(NG):
                            last = nc.tensor.matmul(P[0][:, GW * g:GW * g + GW], qb1[:, GT * g:GT * g + GT, :].rearrange("p q h -> p (q h)"),
                                                    keff[:, GW * g:GW * g + GW], start=True, stop=True)
                        last.then_inc(sem("s1_psum"), 1)
                        pe.wait_ge(sem("p1_sb"), b + 1)
                        for g in range(NG):
                            last = nc.tensor.transpose(P[1 + g // 4][0:GW, 128 * (g % 4):128 * (g % 4) + 128],
                                                       P1[:, GW * g:GW * g + GW], ident[:, :])
                        last.then_inc(sem("pt1_psum"), 1)
                        pe.wait_ge(sem("pt1_sb"), b + 1)
                        for g in range(NG):
                            last = nc.tensor.matmul(P[3 + g // 4][:, 128 * (g % 4):128 * (g % 4) + 128], kvn[:, g, :],
                                                    PT1[:, g, :], start=True, stop=True)
                        last.then_inc(sem("oc_psum"), 1)
                pe.wait_ge(sem("p1_taken"), NB)
                for t in range(TT):
                    for hp in range(NP):
                        last = nc.tensor.matmul(P[t // 2][:, D * (t % 2):D * (t % 2) + D], ocT[:, hp, 128 * t:128 * t + 128],
                                                wuvo[:, hp, :], start=hp == 0, stop=hp == NP - 1)
                last.then_inc(sem("out1_psum"), 1)

            pe.wait_ge(sem("const_in"), 16 * 14)
            pe.wait_ge(sem("w2n_ready"), 1)
            for m in range(2):
                for k in range(KT):
                    for o in range(KT):
                        last = nc.tensor.transpose(P[m][:, D * k + 128 * o:D * k + 128 * o + 128],
                                                   w2n[:, 2 * m + o, 128 * k:128 * k + 128], ident[:, :])
            last.then_inc(sem("w2T_psum"), 1)

            for s in range(NSUB):
                l = s // 2
                pe.wait_ge(sem("h_ready"), s + 1)
                tokens_to_T(h)
                if s % 2:
                    mixture(l)
                    continue
                if l == 1:
                    window()
                    continue
                a = ATT[l]
                wait_T()
                src = hT
                if l == 3:
                    for o in range(KT):
                        for k in range(KT):
                            last = nc.tensor.matmul(P[o][:, :], w3[:, 0, k, 128 * o:128 * o + 128], hT[:, k, :],
                                                    start=k == 0, stop=k == 1)
                    last.then_inc(sem("refT_psum"), 1)
                    pe.wait_ge(sem("refT_sb"), 2)
                    src = oT
                    for t in range(TT):
                        for k in range(KT):
                            last = nc.tensor.transpose(P[2 + t // 2][:, D * (t % 2) + 128 * k:D * (t % 2) + 128 * k + 128],
                                                       oT[:, k, 128 * t:128 * t + 128], ident[:, :])
                    last.then_inc(sem("ref_psum"), 1)
                    pe.wait_ge(sem("ref_sb"), 1)
                wq = w0[:, 0] if l == 0 else w3[:, 1] if l == 3 else w2T[:, 0:2]
                for o in range(KT):
                    for k in range(KT):
                        last = nc.tensor.matmul(P[o][:, :], wq[:, k, 128 * o:128 * o + 128], src[:, k, :],
                                                start=k == 0, stop=k == 1)
                last.then_inc(sem("q_psum"), 1)
                pe.wait_ge(sem("q_sb"), a + 1)
                attention(l)
                if l == 3:
                    continue
                pe.wait_ge(sem("o_ready"), a + 1)
                tokens_to_T(onat)
                wait_T()
                wo = w0[:, 3] if l == 0 else w2T[:, 2:4]
                for t in range(TT):
                    for k in range(KT):
                        last = nc.tensor.matmul(P[t // 2][:, D * (t % 2):D * (t % 2) + D],
                                                oT[:, k, 128 * t:128 * t + 128], wo[:, k, :],
                                                start=k == 0, stop=k == 1)
                if l == 0:
                    for t in range(TT):
                        for k in range(KT):
                            last = nc.tensor.matmul(P[2 + t // 2][:, D * (t % 2):D * (t % 2) + D],
                                                    hT[:, k, 128 * t:128 * t + 128], w0[:, 4, k, :],
                                                    start=k == 0, stop=k == 1)
                last.then_inc(sem("out_psum"), 1)

        @block.scalar
        def _(act):
            n_tr = [0]

            def transposed(dst, scale=1.0):
                n_tr[0] += 1
                act.wait_ge(sem("tr_psum"), n_tr[0])
                nc.scalar.activation(dst[:, 0, :], P[6][:, :], ACT.Copy, scale=scale).then_inc(sem("tr_act"), 1)

            def root(dst, src, n):
                act.wait_ge(sem("var_ready"), n)
                nc.scalar.activation(dst, src, ACT.Sqrt).then_inc(sem("std_ready"), 1)

            def attention(l):
                a = ATT[l]
                na = (0, 48, 96)[a]
                pa = NPROJ[l] - 6
                pd = (0, 96, 192)[a]

                def project(B, bi):
                    g = 0
                    if l == 3:
                        for o in range(KT):
                            for c in range(NCH):
                                act.wait_ge(sem("proj_done"), B * 18 + (pd + 18 + g + 1))
                                nc.scalar.activation(supT[:, o, CH * c:CH * c + CH], P[6 + g % 2][:, 0:CH], ACT.Relu,
                                                     bias=cols[:, 6 + o:7 + o]).then_inc(sem("k_ready"), 1)
                                g += 1
                    for o in range(KT):
                        for c in range(NCH):
                            act.wait_ge(sem("proj_done"), B * NPROJ[l] + (pd + 18 + g + 1))
                            dst, src = kT[:, bi, o, CH * c:CH * c + CH], P[6 + g % 2][:, 0:CH]
                            if l == 0:
                                nc.scalar.activation(dst, src, ACT.Copy).then_inc(sem("k_ready"), 1)
                            else:
                                col = 4 + o if l == 2 else 10 + o
                                nc.scalar.activation(dst, src, ACT.Identity, bias=cols[:, col:col + 1]
                                                     ).then_inc(sem("k_ready"), 1)
                            g += 1

                def exps(n, bi, p):
                    act.wait_ge(sem("nm_ready"), n + 1)
                    nc.scalar.activation(Sb[:, p % 4, :], Sb[:, p % 4, :], ACT.Exp, bias=nm[:, p % 4:p % 4 + 1],
                                         accum_out=rsum[:, bi, p:p + 1]).then_inc(sem("exp_done"), 1)

                def turned(n, p):
                    act.wait_ge(sem("pv_done"), n)
                    for g in (0, 2):
                        act.wait_ge(sem("t_done"), n * 3 + (12 + g + 1))
                        nc.scalar.activation(PT[0:CT, p % 2, g, :], P[3 + (3 * p + g) % 2][0:CT, :], ACT.Copy
                                             ).then_inc(sem("pt_act"), 1)

                with act.Fori(0, NB // 2) as i:
                    for bi in range(2):
                        B = i * 2 + bi
                        n0 = i * 16 + (64 * a + 8 * bi)
                        if bi == 0:
                            project(B, 0)
                        for p in range(NP):
                            exps(n0 + p, bi, p)
                            if p >= 1:
                                turned(n0 + (p - 1), p - 1)
                        if bi == 0:
                            project(B + 1, 1)
                        turned(n0 + 7, 7)
                        act.wait_ge(sem("pv_done"), n0 + (7 + 2))
                        act.wait_ge(sem("o_taken"), B + 8 * a)
                        nc.scalar.activation(oTs[:, :], P[5][:, 0:D], ACT.Copy).then_inc(sem("oT_sb"), 1)

            def mixture(l):
                I, U, base = MOE[l]["I"], MOE[l]["U"], MOE_BASE[l]
                act.wait_ge(sem("lg_ready"), l + 1)
                if l < 3:
                    nc.scalar.activation(lg[:, 2, :, :], lg[:, 1, :, :], ACT.Exp).then_inc(sem("lg_exp"), 1)
                else:
                    nc.scalar.activation(lg[:, 2, :, 0:8], lg[:, 0, :, 0:8], ACT.Sigmoid).then_inc(sem("lg_exp"), 1)

                def unit(k, u):
                    act.wait_ge(sem("gu_done"), u * 2 + (2 * base + 1))
                    act.wait_ge(sem("act_ready"), u + base)
                    nc.scalar.activation(sg[0:I, k, :], P[k][0:I, :], ACT.Silu).then_inc(sem("silu_done"), 1)

                with act.Fori(0, U // 2) as i:
                    unit(0, i * 2)
                    unit(1, i * 2 + 1)
                if U % 2:
                    unit(0, U - 1)

            def window():
                act.wait_ge(sem("pre1_psum"), 1)
                nc.scalar.activation(qcT, P[6][0:QC, :], ACT.Copy)
                nc.scalar.activation(mkv[0:R, :], P[7][0:R, 0:NB], ACT.Copy, scale=1.0 / NCTX)
                for j in range(2):
                    last = nc.scalar.activation(wcomb[:, 8 * j:8 * j + 8, 0:R],
                                                P[j][0:QC, :].rearrange("p (h n) -> p h n", h=8), ACT.Copy)
                last.then_inc(sem("pre1_act"), 1)
                for hh in range(NH):
                    act.wait_ge(sem("qh_psum"), hh + 1)
                    nc.scalar.activation(qeff[0:64, :, hh, :], P[hh % 4][0:64, :].rearrange("p (b q) -> p b q", b=NB),
                                         ACT.Copy).then_inc(sem("qn_taken"), 1)
                act.wait_ge(sem("qr_taken"), NH)
                with act.Fori(0, NB // 2) as i:
                    for bi in range(2):
                        b = i * 2 + bi
                        act.wait_ge(sem("g_turned"), b + (2 + 1))
                        nc.scalar.activation(gT[:, 0, :], P[0][:, 0:WB], ACT.Copy)
                        nc.scalar.activation(csT, P[2][:, 0:WB], ACT.Copy).then_inc(sem("g_act"), 1)
                        act.wait_ge(sem("p1_taken"), b)
                        nc.scalar.activation(qb1, qeff[:, bass.ds(b, 1), :, :].rearrange("p b h q -> p q (b h)"),
                                             ACT.Copy).then_inc(sem("qb1_sb"), 1)
                        act.wait_ge(sem("kvn_psum"), b + 1)
                        src = P[7][0:GW, 0:NG * R].rearrange("p (g n) -> p g n", g=NG)
                        for j in range(2):
                            last = nc.scalar.activation(kvn[:, :, R * j:R * j + R], src, ACT.Copy)
                        act.wait_ge(sem("krs_psum"), b + 1)
                        nc.scalar.activation(keff[64:128, :], P[5][64:128, 0:WB], ACT.Copy).then_inc(sem("keff_sb"), 1)
                        act.wait_ge(sem("s1_sb"), b + 1)
                        nc.scalar.activation(P1, P1, ACT.Exp, scale=SCALE1).then_inc(sem("e1_sb"), 1)
                        act.wait_ge(sem("pt1_psum"), b + 1)
                        for j, m in ((0, 4), (1, 3)):
                            last = nc.scalar.activation(PT1[:, 4 * j:4 * j + m, :].rearrange("p g n -> p (g n)"),
                                                        P[1 + j][0:GW, 0:128 * m], ACT.Copy)
                        last.then_inc(sem("pt1_sb"), 1)

            act.wait_ge(sem("const_in"), 16 * 14)
            nc.scalar.activation(tg[:, :], tg[:, :], ACT.Tanh).then_inc(sem("tg_ready"), 1)
            nr = 0
            for s in range(NSUB):
                l = s // 2
                nr += 1
                root(sm[:, 1, :], sm[:, 0, :], nr)
                if s == 0:
                    nr += 1
                    root(sm[:, 1, :], sm[:, 0, :], nr)
                transposed(hT, cols[:, 0:1] if s == 0 else 1.0)
                if s % 2:
                    mixture(l)
                    continue
                if l == 1:
                    window()
                    continue
                if l == 3:
                    act.wait_ge(sem("refT_psum"), 1)
                    for o in range(KT):
                        nc.scalar.activation(oT[:, o, :], P[o][:, :], ACT.Relu, bias=cols[:, 6 + o:7 + o]
                                             ).then_inc(sem("refT_sb"), 1)
                attention(l)
                if l < 3:
                    transposed(oT)
                if l == 0:
                    act.wait_ge(sem("out_psum"), 1)
                    for j in range(2):
                        nc.scalar.activation(tmp[:, 2 * j:2 * j + 2, :], P[2 + j][:, :], ACT.Sigmoid
                                             ).then_inc(sem("gate_ready"), 1)

        @block.vector
        def _(dve):
            steps, n_tr, n_root, signals = [0], [0], [0], [0]
            V = nc.vector

            def step(ins):
                steps[0] += 1
                ins.then_inc(sem("dve_step"), 1)
                dve.wait_ge(sem("dve_step"), steps[0])

            def signal(name, n=1):
                signals[0] += 1
                V.memset(flags[:, signals[0]:signals[0] + 1], 0.0).then_inc(sem(name), n)

            def wide(col, n):
                return col.rearrange("p (t o) -> p t o", o=1).broadcast_to([128, TT, n])

            def transposed(dst, scale=None):
                n_tr[0] += 1
                dve.wait_ge(sem("tr_psum"), n_tr[0])
                if scale is None:
                    V.tensor_copy(dst[:, 1, :], P[7][:, :]).then_inc(sem("tr_dve"), 1)
                else:
                    V.tensor_scalar(dst[:, 1, :], P[7][:, :], scale, None, ALU.mult).then_inc(sem("tr_dve"), 1)

            def inverse_root():
                n_root[0] += 1
                V.tensor_scalar(sm[:, 0, :], sm[:, 0, :], 1.0, None, ALU.mult).then_inc(sem("var_ready"), 1)
                dve.wait_ge(sem("std_ready"), n_root[0])
                step(V.reciprocal(sm[:, 2, :], sm[:, 1, :]))

            def layer_norm():
                for t in range(TT):
                    step(V.bn_stats(stats[:, t, :], x[:, t, :]))
                for t in range(TT):
                    step(V.bn_aggr(mv[:, t, :], stats[:, t, :]))
                step(V.tensor_scalar(sm[:, 0, :], mv[:, :, 1], 1e-5, None, ALU.add))
                inverse_root()
                for t in range(TT):
                    step(V.tensor_scalar(h[:, t, :], x[:, t, :], mv[:, t, 0:1], sm[:, 2, t:t + 1],
                                         ALU.subtract, ALU.mult))

            def fake_quantise(w):
                magic = 12582912.0
                step(V.tensor_reduce(sm[:, 4, :], w[:, :, :], AX.X, ALU.max, apply_absolute_value=True))
                step(V.tensor_scalar(sm[:, 5, :], sm[:, 4, :], 1.0 / 127.0, 1e-8, ALU.mult, ALU.max))
                step(V.reciprocal(sm[:, 6, :], sm[:, 5, :]))
                step(V.tensor_tensor(w[:, :, :], w[:, :, :], wide(sm[:, 6, :], D), ALU.mult))
                step(V.tensor_scalar(w[:, :, :], w[:, :, :], magic, magic, ALU.add, ALU.subtract))
                step(V.tensor_scalar(w[:, :, :], w[:, :, :], 127.0, -127.0, ALU.min, ALU.max))
                return V.tensor_tensor(w[:, :, :], w[:, :, :], wide(sm[:, 5, :], D), ALU.mult)

            def residual(g, y):
                V.scalar_tensor_tensor(x[:, :, :].rearrange("p t d -> p (t d)"), y, tg[:, g:g + 1],
                                       x[:, :, :].rearrange("p t d -> p (t d)"), ALU.mult, ALU.add
                                       ).then_inc(sem("sub_done"), 1)
                dve.wait_ge(sem("sub_done"), (2 * g + 1) if g < 4 else 2 * (g - 4) + 2)

            def attention(l):
                a = ATT[l]
                pd = (0, 96, 192)[a]

                def queries(B, bi):
                    for k in range(KT):
                        V.tensor_tensor(Qb[:, bi, k, :].rearrange("p (e q) -> p e q", e=8),
                                        qT[:, k, bass.ds(B * QP, QP)].rearrange("p (o q) -> p o q", o=1).broadcast_to([128, 8, QP]),
                                        headmask[:, :].rearrange("p (e o) -> p e o", o=1).broadcast_to([128, 8, QP]),
                                        ALU.mult).then_inc(sem("qb_ready"), 1)

                def project(B, bi):
                    for j in range(6):
                        g = NPROJ[l] - 6 + j
                        dve.wait_ge(sem("proj_done"), B * NPROJ[l] + (pd + 18 + g + 1))
                        V.tensor_copy(v[0:CT, bi, 2 * j:2 * j + 2, :].rearrange("p j d -> p (j d)"),
                                      P[6 + g % 2][0:CT, :]).then_inc(sem("v_ready"), 1)

                def mask(B, i, bi):
                    if l == 0:
                        dve.wait_ge(sem(f"mask_in{bi}"), i * 16 + 16)
                        V.tensor_scalar(maskf[:, bi, :], maskraw[:, bi, :].bitcast(U8), -NEG, NEG, ALU.mult, ALU.add
                                        ).then_inc(sem("mask_made"), 1)
                        dve.wait_ge(sem("mask_made"), B + 1)
                    if l == 2:
                        dve.wait_ge(sem(f"mask_in{bi}"), i * 32 + 16 * 4 + 32)

                def maxima(n, B, bi, p):
                    r = p % 4
                    dve.wait_ge(sem("t_done"), n * 3 + 3)
                    for c in range(NCH):
                        dve.wait_ge(sem("s_done"), n * 3 + (c + 1))
                        dve.sem_inc(sem("waits_met"), 1)
                        o = Sb[:, r, CH * c:CH * c + CH]
                        if l == 3:
                            V.tensor_scalar(o, P[c][:, 0:CH], 1.0, None, ALU.mult, ALU.max,
                                            accum_out=mx[:, r, c:c + 1]).then_inc(sem("s_taken"), 1)
                        else:
                            V.tensor_tensor_reduce(o, P[c][:, 0:CH], maskf[:, bi, CH * c:CH * c + CH], 1.0, -3.0e38,
                                                   ALU.add, ALU.max, mx[:, r, c:c + 1]).then_inc(sem("s_taken"), 1)
                    dve.wait_ge(sem("s_taken"), n * 3 + (3 + 3))
                    V.tensor_reduce(nm[:, r:r + 1], mx[:, r, 0:4 if l == 0 else 3], AX.X, ALU.max, negate=True
                                    ).then_inc(sem("nm_ready"), 1)

                def turned(n, p):
                    dve.wait_ge(sem("pv_done"), n)
                    dve.wait_ge(sem("t_done"), n * 3 + (12 + 2))
                    V.tensor_copy(PT[0:CT, p % 2, 1, :], P[3 + (3 * p + 1) % 2][0:CT, :]).then_inc(sem("pt_dve"), 1)

                def normalise(B, i, bi):
                    dve.wait_ge(sem("exp_done"), B * 8 + (64 * a + 8))
                    V.tensor_scalar(rinv[:, bi, :], rsum[:, bi, :], 1e-30, None, ALU.max).then_inc(sem("rsum_ok"), 1)
                    dve.wait_ge(sem("rsum_ok"), B + (8 * a + 1))
                    V.reciprocal(rinv[:, bi, :], rinv[:, bi, :]).then_inc(sem("rinv_ok"), 1)
                    dve.wait_ge(sem("rinv_ok"), B + (8 * a + 1))
                    dve.wait_ge(sem("on_psum"), B + (8 * a + 1))
                    for e in range(2):
                        src = P[5][QP * e:QP * e + QP, D:2 * D].rearrange("q (p c) -> q p c", c=32)[:, :, HD * e:HD * e + HD]
                        dst = onat[QP * bi:QP * bi + QP, bass.ds(i, 1), :].rearrange("q o (p c) -> q (o p) c", c=32)[:, :, HD * e:HD * e + HD]
                        last = V.tensor_tensor(dst, src, rinv[QP * e:QP * e + QP, bi, :].rearrange("q (p o) -> q p o", o=1).broadcast_to([QP, NP, HD]),
                                               ALU.mult)
                    last.then_inc(sem("o_taken"), 1)

                with dve.Fori(0, NB // 2) as i:
                    for bi in range(2):
                        queries(i * 2 + bi, bi)
                    for bi in range(2):
                        B = i * 2 + bi
                        n0 = i * 16 + (64 * a + 8 * bi)
                        if bi == 0:
                            project(B, 0)
                        if l == 0:
                            dve.wait_ge(sem(f"ctx_in{bi}"), i * 16 + 16)
                            V.tensor_reduce(meanT[:, :, bass.ds(B, 1)], ctxT[:, bi], AX.X, ALU.add
                                            ).then_inc(sem("mean_done"), 1)
                        mask(B, i, bi)
                        for p in range(NP):
                            maxima(n0 + p, B, bi, p)
                            if p == NP - 1 and l < 3:
                                V.memset(flags[:, 100:101], 0.0).then_inc(sem("mask_used"), 1)
                            if p >= 1:
                                turned(n0 + (p - 1), p - 1)
                        if bi == 0:
                            project(B + 1, 1)
                        turned(n0 + 7, 7)
                        normalise(B, i, bi)
                dve.wait_ge(sem("o_taken"), 8 * (a + 1))

            def routing(l):
                E, K, U, per = (MOE[l][k] for k in ("E", "K", "U", "per"))

                def L(j):
                    return lg[:, j, :, 0:E]

                def s4(j):
                    return sm[:, j, :]

                dve.wait_ge(sem("logits"), l + 1)
                src = P[7][:, 0:64].rearrange("p (t e) -> p t e", t=TT)[:, :, 0:E]
                if l < 3:
                    step(V.tensor_reduce(s4(8), src, AX.X, ALU.max))
                    V.tensor_tensor(L(1), src, wide(s4(8), E), ALU.subtract).then_inc(sem("lg_ready"), 1)
                    dve.wait_ge(sem("lg_exp"), l + 1)
                    step(V.tensor_reduce(s4(9), L(2), AX.X, ALU.add))
                    step(V.reciprocal(s4(10), s4(9)))
                    step(V.tensor_tensor(L(0), L(2), wide(s4(10), E), ALU.mult))
                else:
                    step(V.tensor_copy(L(0), src))
                    signal("lg_ready")
                for t in range(TT):
                    step(V.max(top8[:, t, :], lg[:, 0, t, 0:E]))
                step(V.tensor_tensor(L(3), L(0), top8[:, :, K - 1:K].broadcast_to([128, TT, E]), ALU.is_gt))
                step(V.tensor_tensor(L(4), L(0), top8[:, :, K - 1:K].broadcast_to([128, TT, E]), ALU.is_equal))
                step(V.tensor_reduce(s4(11), L(3), AX.X, ALU.add))
                step(V.tensor_scalar(s4(12), s4(11), -1.0, float(K), ALU.mult, ALU.add))
                step(V.memset(lg[:, 8, :, :], 1.0))
                for t in range(TT):
                    step(V.tensor_tensor_scan(lg[:, 5, t, 0:E], lg[:, 8, t, 0:E], lg[:, 4, t, 0:E], 0.0, ALU.mult, ALU.add))
                step(V.tensor_tensor(L(6), L(5), wide(s4(12), E), ALU.is_le))
                step(V.tensor_tensor(L(6), L(6), L(4), ALU.mult))
                step(V.tensor_tensor(L(6), L(6), L(3), ALU.add))
                if l == 3:
                    dve.wait_ge(sem("lg_exp"), 4)
                    V.tensor_tensor(L(9), L(6), L(2), ALU.mult).then_inc(sem("cw_ready"), 1)
                    step(V.memset(cw[:, :, :], 1.0))
                    dve.wait_ge(sem("prT_psum"), 1)
                    V.tensor_copy(qT[0:8, 0, :], P[6][0:8, :]).then_inc(sem("prT_sb"), 1)
                    return
                step(V.tensor_tensor(L(9), L(6), L(0), ALU.mult))
                if l in (1, 2):
                    step(V.tensor_reduce(s4(13), L(9), AX.X, ALU.add))
                    step(V.reciprocal(s4(14), s4(13)))
                    step(V.tensor_tensor(L(9), L(9), wide(s4(14), E), ALU.mult))
                    if l == 1:
                        step(V.tensor_scalar(L(9), L(9), K / (K + 1.0), None, ALU.mult))
                step(V.memset(cw[:, :, :], 1.0 / (K + 1.0) if l == 1 else 1.0))
                for r in range(per):
                    dst = cw[:, :, 0:per * E].rearrange("p t (e r) -> p t e r", r=per)[:, :, :, r]
                    last = V.tensor_copy(dst, L(9))
                last.then_inc(sem("cw_ready"), 1)
                dve.wait_ge(sem("cw_ready"), l + 1)

            def mixture(l):
                I, U, base = MOE[l]["I"], MOE[l]["U"], MOE_BASE[l]
                routing(l)
                step(V.memset(acc[:, :, :], 0.0))

                def scaled_inputs(k, u, i):
                    dve.wait_ge(sem(f"pb_in{k}"), i * 16 + 16)
                    V.tensor_tensor(xin[:, k], hT[:, :, :], pb[:, k, :].rearrange("p (o n) -> p o n", o=1).broadcast_to([128, KT, NTOK]),
                                    ALU.mult).then_inc(sem("xin_ready"), 1)

                def gate(k, u):
                    dve.wait_ge(sem("silu_done"), u + (base + 1))
                    dve.wait_ge(sem("gu_done"), u * 2 + (2 * base + 2))
                    dve.wait_ge(sem("down_done"), u + base)
                    V.tensor_tensor(act_b[0:I, k, :], sg[0:I, k, :], P[2 + k][0:I, :], ALU.mult
                                    ).then_inc(sem("act_ready"), 1)

                def accumulate(k, u):
                    dve.wait_ge(sem("down_done"), u + (base + 2))
                    dve.wait_ge(sem("acc_done"), u + (base + 1))
                    for t in range(TT):
                        last = V.scalar_tensor_tensor(acc[:, t, :], P[4 + 2 * k + t // 2][:, D * (t % 2):D * (t % 2) + D],
                                                      cw[:, t, bass.ds(u, 1)], acc[:, t, :], ALU.mult, ALU.add)
                    last.then_inc(sem("acc_done"), 1)

                with dve.Fori(0, U // 2) as i:
                    if l == 3:
                        for k in range(2):
                            dve.wait_ge(sem("gu_done"), i * 4 + (2 * base))
                            scaled_inputs(k, i * 2 + k, i)
                    for k in range(2):
                        gate(k, i * 2 + k)
                    for k in range(2):
                        accumulate(k, i * 2 + k)
                if U % 2:
                    gate(0, U - 1)
                    accumulate(0, U - 1)
                dve.wait_ge(sem("acc_done"), base + U + 1)
                residual(4 + l, acc[:, :, :].rearrange("p t d -> p (t d)"))

            def gather_rows():
                step(V.tensor_copy(segf[:, :], seg))
                step(V.tensor_copy(gidx[0:GR, 0, :], gseg[0:GR, :]))
                step(V.tensor_tensor(gidx[0:GR, 0, :], gidx[0:GR, 0, :], gidx[0:GR, 1, :], ALU.subtract))
                step(V.tensor_scalar(gidx[0:GR, 0, :], gidx[0:GR, 0, :], 0.0, NCTX - 1.0, ALU.max, ALU.min))
                step(V.tensor_tensor(gidx[0:GR, 0, :], gidx[0:GR, 0, :], gidx[0:GR, 2, :], ALU.add))
                step(V.memset(grow[:, :], 0))
                V.tensor_copy(grow[0:GR, :], gidx[0:GR, 0, :]).then_inc(sem("rows_ready"), 1)

            def window():
                dve.wait_ge(sem("pre1_psum"), 1)
                for j in range(4):
                    last = V.tensor_copy(wuvo[:, 2 * j:2 * j + 2, :].rearrange("p h n -> p (h n)"), P[2 + j][:, :])
                V.memset(ocT[:, :, :], 0.0).then_inc(sem("pre1_dve"), 1)
                for hh in range(NH):
                    dve.wait_ge(sem("qh_psum"), hh + 1)
                    dst = qeff[64:128, :, hh, :]
                    b8 = lambda y: y.rearrange("p (b q) -> p b q", b=NB)
                    step(V.tensor_tensor(dst, b8(P[hh % 4][64:128, :]), b8(cosq[64:128, :]), ALU.mult))
                    step(V.tensor_tensor(rope2[64:128, :], P[4 + hh % 4][64:128, :], sinq[64:128, :], ALU.mult))
                    V.tensor_tensor(dst, dst, b8(rope2[64:128, :]), ALU.add).then_inc(sem("qr_taken"), 1)
                with dve.Fori(0, NB // 2) as i:
                    for bi in range(2):
                        b = i * 2 + bi

                        def after(name, k, n=1):
                            dve.wait_ge(sem(name), b * n + k)

                        by9 = lambda y: y.rearrange("p (t j) -> p t j", j=NW)
                        by72 = lambda y: y.rearrange("p (g n) -> p g n", g=NG)
                        V.tensor_tensor(by9(kid), segf[:, bass.ds(b * NQ, NQ)].rearrange("p (t o) -> p t o", o=1).broadcast_to([128, NQ, NW]),
                                        jrow.rearrange("p (o j) -> p o j", o=1).broadcast_to([128, NQ, NW]), ALU.subtract
                                        ).then_inc(sem("w1_step"), 1)
                        after("w1_step", 1, 13)
                        V.tensor_scalar(valid, kid, -0.5, None, ALU.is_gt).then_inc(sem("w1_step"), 1)
                        after("w1_step", 2, 13)
                        V.scalar_tensor_tensor(valid, kid, NCTX - 0.5, valid, ALU.is_lt, ALU.mult).then_inc(sem("w1_step"), 1)
                        after("w1_step", 3, 13)
                        V.tensor_reduce(anyv[:, 0, :], by9(valid), AX.X, ALU.max).then_inc(sem("w1_step"), 1)
                        V.tensor_scalar(madd, valid, -NEG, NEG, ALU.mult, ALU.add).then_inc(sem("w1_step"), 1)
                        after("w1_step", 5, 13)
                        V.tensor_scalar(anyv[:, 1, :], anyv[:, 0, :], -1.0, 1.0, ALU.mult, ALU.add).then_inc(sem("w1_step"), 1)
                        V.tensor_tensor(by72(madd), by72(madd), blk.rearrange("p (o n) -> p o n", o=1).broadcast_to([128, NG, GW]),
                                        ALU.add).then_inc(sem("w1_step"), 1)
                        after("g_turned", 3)
                        V.tensor_copy(gT[:, 1, :], P[1][:, 0:WB]).then_inc(sem("g_dve"), 1)
                        after("kv_psum", 1)
                        after("w1_step", 7, 13)
                        V.tensor_tensor(by9(valid)[0:R], by9(P[5][0:R, 0:WB]), anyv[0:R, 0, :].rearrange("p (t o) -> p t o", o=1).broadcast_to([R, NQ, NW]),
                                        ALU.mult).then_inc(sem("w1_step"), 1)
                        after("w1_step", 8, 13)
                        V.scalar_tensor_tensor(by9(keff)[0:R], anyv[0:R, 1, :].rearrange("p (t o) -> p t o", o=1).broadcast_to([R, NQ, NW]),
                                               mkv[0:R, bass.ds(b, 1)], by9(valid)[0:R], ALU.mult, ALU.add).then_inc(sem("kv_sb"), 1)
                        after("kr_psum", 1)
                        after("g_act", 1)
                        V.tensor_tensor(prod, P[6][:, 0:WB], csT, ALU.mult).then_inc(sem("prod_sb"), 1)
                        after("s1_psum", 1)
                        V.tensor_tensor(P1, P[0][:, 0:WB], madd, ALU.add).then_inc(sem("w1_step"), 1)
                        after("w1_step", 9, 13)
                        V.tensor_reduce(sm1[:, 0, :], by72(P1), AX.X, ALU.max).then_inc(sem("w1_step"), 1)
                        after("w1_step", 10, 13)
                        bc = lambda y: y.rearrange("p (g o) -> p g o", o=1).broadcast_to([128, NG, GW])
                        V.tensor_tensor(by72(P1), by72(P1), bc(sm1[:, 0, :]), ALU.subtract).then_inc(sem("s1_sb"), 1)
                        after("e1_sb", 1)
                        V.tensor_reduce(sm1[:, 1, :], by72(P1), AX.X, ALU.add).then_inc(sem("w1_step"), 1)
                        after("w1_step", 11, 13)
                        V.reciprocal(sm1[:, 2, :], sm1[:, 1, :]).then_inc(sem("w1_step"), 1)
                        after("w1_step", 12, 13)
                        V.tensor_tensor(by72(P1), by72(P1), bc(sm1[:, 2, :]), ALU.mult).then_inc(sem("p1_sb"), 1)
                        after("oc_psum", 1)
                        for e in range(2):
                            for j, m in ((0, 4), (1, 3)):
                                src = P[3 + j][64 * e:64 * e + 64, 0:128 * m].rearrange("p (t h x) -> p h t x", h=8, x=2)[:, :, :, e]
                                last = V.tensor_copy(ocT[64 * e:64 * e + 64, :, bass.ds(b * QP + GT * 4 * j, GT * m)], src)
                        last.then_inc(sem("w1_step"), 1)
                        V.memset(flags[:, 101:102], 0.0).then_inc(sem("p1_taken"), 1)
                dve.wait_ge(sem("out1_psum"), 1)
                for j in range(2):
                    step(V.tensor_copy(tmp[:, 2 * j:2 * j + 2, :].rearrange("p t d -> p (t d)"), P[j][:, :]))
                residual(1, tmp[:, :, :].rearrange("p t d -> p (t d)"))

            V.memset(x[:, :, :], 0.0).then_inc(sem("x_cleared"), 1)
            V.memset(mx[:, :, :], -1.0e29).then_inc(sem("s_taken"), 3)
            signal("t_done", 12)
            signal("pv_done", 1)
            signal("proj_done", 18)
            signal("mean_done", 2)
            signal("g_turned", 2)
            signal("mask_used", 2)
            signal("down_done", 1)
            signal("act_ready", 1)
            signal("acc_done", 1)
            dve.wait_ge(sem("const_in"), 16 * 14)
            gather_rows()
            fake_quantise(w2n).then_inc(sem("w2n_ready"), 1)
            dve.wait_ge(sem("w2T_psum"), 1)
            for m in range(2):
                step(V.tensor_copy(w2T[:, 2 * m:2 * m + 2, :].rearrange("p k d -> p (k d)"), P[m][:, :]))
            dve.wait_ge(sem("x_in"), 16 * NB)

            for s in range(NSUB):
                l = s // 2
                layer_norm()
                if s == 0:
                    for t in range(TT):
                        step(V.tensor_tensor_reduce(tmp[:, t, :], h[:, t, :], h[:, t, :], 1.0, 0.0, ALU.mult, ALU.add,
                                                    sm[:, 3, t:t + 1]))
                    step(V.tensor_scalar(sm[:, 0, :], sm[:, 3, :], 1.0 / D, 1e-6, ALU.mult, ALU.add))
                    inverse_root()
                    step(V.tensor_tensor(h[:, :, :], h[:, :, :], wide(sm[:, 2, :], D), ALU.mult))
                if s == 4:
                    step(fake_quantise(h))
                signal("h_ready")
                if s == 4:
                    V.memset(maskf[:, :, :], 0.0).then_inc(sem("mask_cleared"), 1)
                transposed(hT, cols[:, 1:2] if s == 0 else None)
                if s % 2:
                    mixture(l)
                    continue
                if l == 1:
                    window()
                    continue
                a = ATT[l]
                if l == 3:
                    dve.wait_ge(sem("ref_psum"), 1)
                    for j in range(2):
                        step(V.tensor_copy(tmp[:, 2 * j:2 * j + 2, :].rearrange("p t d -> p (t d)"), P[2 + j][:, :]))
                    signal("ref_sb")
                dve.wait_ge(sem("q_psum"), a + 1)
                for o in range(KT):
                    if l == 0:
                        step(V.tensor_scalar(qT[:, o, :], P[o][:, :], 0.25, None, ALU.mult))
                    else:
                        col = (2 if l == 2 else 8) + o
                        step(V.tensor_scalar(qT[:, o, :], P[o][:, :], cols[:, col:col + 1], 0.25, ALU.add, ALU.mult))
                signal("q_sb")
                attention(l)
                flat = tmp[:, :, :].rearrange("p t d -> p (t d)")
                row = lambda r: rows[:, r, :].rearrange("p (o d) -> p o d", o=1).broadcast_to([128, TT, D])
                if l == 0:
                    signal("o_ready")
                    transposed(oT)
                    for j in range(2):
                        dve.wait_ge(sem("gate_ready"), j + 1)
                        step(V.tensor_tensor(tmp[:, 2 * j:2 * j + 2, :].rearrange("p t d -> p (t d)"),
                                             tmp[:, 2 * j:2 * j + 2, :].rearrange("p t d -> p (t d)"), P[j][:, :], ALU.mult))
                    dve.wait_ge(sem("tg_ready"), 1)
                    residual(0, flat)
                if l == 2:
                    step(V.tensor_tensor(onat[:, :, :], onat[:, :, :], row(0), ALU.add))
                    fake_quantise(onat).then_inc(sem("o_ready"), 1)
                    transposed(oT)
                    dve.wait_ge(sem("out_psum"), 2)
                    for j in range(2):
                        step(V.tensor_tensor(tmp[:, 2 * j:2 * j + 2, :], P[j][:, :].rearrange("p (t d) -> p t d", t=2),
                                             rows[:, 1, :].rearrange("p (o d) -> p o d", o=1).broadcast_to([128, 2, D]), ALU.add))
                    residual(2, flat)
                if l == 3:
                    step(V.tensor_tensor(tmp[:, :, :], tmp[:, :, :], onat[:, :, :], ALU.add))
                    step(V.tensor_tensor(tmp[:, :, :], tmp[:, :, :], row(2), ALU.add))
                    residual(3, flat)


def _consts():
    c = {}
    c["ident"] = np.eye(128, dtype=np.float32)
    c["headmask"] = (np.arange(128)[:, None] // HD == np.arange(NP)[None, :]).astype(np.float32)
    half = R // 2
    inv_freq = (1.0 / 10000.0 ** (np.arange(half, dtype=np.float32) / np.float32(half))).astype(np.float32)
    ang = np.arange(NCTX, dtype=np.float32)[:, None] * inv_freq
    cos, sin = np.cos(ang).astype(np.float32), np.sin(ang).astype(np.float32)
    c["rope"] = np.concatenate([cos, cos, -sin, sin], axis=1)
    q = np.zeros((NTOK, 128), np.float32)
    for b in range(NB):
        q[QP * b:QP * b + NQ] = c["rope"][0:NQ]
    c["cosq"], c["sinq"] = np.ascontiguousarray(q[:, 0:R].T), np.ascontiguousarray(q[:, R:2 * R].T)
    p = np.arange(128)[:, None] // NH
    c["blk"] = np.where(np.arange(GW)[None, :] // NW == p, 0.0, 3 * NEG).astype(np.float32)
    c["jrow"] = np.arange(NW, dtype=np.float32)
    c["wstk"] = np.concatenate([np.eye(R), np.eye(R)]).astype(np.float32)
    j = np.tile((np.arange(GR) % NW).astype(np.float32)[:, None], (1, NB * NGT))
    first = np.tile((np.arange(NB * NGT) // NGT * NCTX).astype(np.float32)[None, :], (GR, 1))
    c["gconst"] = np.stack([j, first], axis=1)
    return c


def _io(w):
    return w.reshape(-1, 128, w.shape[1]).transpose(1, 0, 2)


def kernel(**inputs):
    import concourse.bacc as bacc
    from concourse.bass_utils import run_bass_kernel_spmd as run
    a = {k: np.asarray(v) for k, v in inputs.items()}
    c = _consts()
    m = {k: c[k] for k in ("ident", "headmask", "cosq", "sinq", "blk", "jrow", "wstk", "gconst")}
    m["x"] = a["x"]
    ctx = a["ctx_2048"]
    m["ctxT"] = ctx.transpose(0, 2, 1).reshape(NB, KT, 128, NCTX).transpose(0, 2, 1, 3)
    m["ctxrows"] = np.concatenate([ctx.reshape(NB * NCTX, D), np.tile(c["rope"], (NB, 1))], axis=1)
    m["mask0"] = a["mask_BxS2_bk0"].view(np.int32)
    m["mask2"] = a["mask_BxSxS2_ff0"]
    seg = a["itok_BxS_0_1023"]
    m["seg"] = seg.reshape(-1)
    m["gseg"] = np.repeat(seg.reshape(NB, NGT, GR // NW), NW, axis=2).reshape(NB * NGT, GR).T
    m["gates"] = np.concatenate([a["g_xattn"], a["g_ffn"]])
    zero = np.zeros(D, np.float32)
    m["rows"] = np.stack([a["L2_xattn_bv"], a["L2_xattn_bo"], a["L3_xattn_b_v"]])
    m["cols"] = np.concatenate([v.reshape(KT, 128).T for v in (
        a["L0_xattn_norm_w"], a["L2_xattn_bq"], a["L2_xattn_bk"], a["L3_xattn_b_fc"], a["L3_xattn_b_q"],
        a["L3_xattn_b_k"], zero, zero)], axis=1)
    m["w0"] = np.stack([_io(a["L0_xattn_" + n].T) for n in ("wq", "wk", "wv", "wo", "wg")], axis=1)
    m["w2"] = np.stack([_io(a["L2_xattn_" + n].T) for n in ("wk", "wv")], axis=1)
    m["w2n"] = np.concatenate([_io(a["L2_xattn_" + n]) for n in ("wq", "wo")], axis=1)
    m["w3"] = np.stack([_io(a["L3_xattn_W_fc"].T), _io(a["L3_xattn_W_q"].T), _io(a["L3_xattn_W_k"].T),
                        _io(a["L3_xattn_W_v"].reshape(D, D).T)], axis=1)
    gate = [a["L0_ffn_gate_w"].T, a["L1_ffn_w_router"], a["L2_ffn_router_gate"].T, a["L3_ffn_router_w"]]
    m["gw"] = np.stack([np.pad(_io(g), ((0, 0), (0, 0), (0, 16 - g.shape[1]))) for g in gate], axis=1)

    def heads(w, n):
        return w.reshape(w.shape[0], NH, n)

    m["wuqT"] = heads(a["L1_xattn_W_uq"], HDL).transpose(2, 1, 0)
    m["wukT"] = heads(a["L1_xattn_W_uk"], HDL).transpose(2, 1, 0)
    m["wuvT"] = heads(a["L1_xattn_W_uv"], HDL).transpose(2, 1, 0)
    qr = heads(a["L1_xattn_W_qr"], R)
    m["wqr"] = qr
    m["wqr2"] = np.concatenate([qr[:, :, R // 2:], qr[:, :, :R // 2]], axis=2)
    m["wdq"] = _io(a["L1_xattn_W_dq"])
    m["wkvc"] = _io(a["L1_xattn_W_kvc"])
    kr = a["L1_xattn_W_kr"]
    m["wkr"] = np.concatenate([kr, kr[:, R // 2:], kr[:, :R // 2]], axis=1)
    m["wo1"] = a["L1_xattn_W_o"].reshape(NH, HDL, D).transpose(1, 0, 2)

    def ups(gate_w, up_w):
        w = np.concatenate([gate_w, up_w], axis=2)
        return w.reshape(len(w), KT, 128, -1).transpose(0, 2, 1, 3)

    def cut(w, n):
        return w.reshape(w.shape[0], D, n, -1).transpose(0, 2, 1, 3).reshape(w.shape[0] * n, D, -1)

    w1, s1 = a["L0_ffn_w1"].transpose(0, 2, 1), a["L0_ffn_shared_w1"].T[None]
    m["up0"] = np.concatenate([ups(cut(w1[:, :, :176], 2), cut(w1[:, :, 176:], 2)),
                               ups(cut(s1[:, :, :352], 4), cut(s1[:, :, 352:], 4))])
    m["down0"] = np.concatenate([a["L0_ffn_w2"].transpose(0, 2, 1).reshape(32, 88, D),
                                 a["L0_ffn_shared_w2"].T.reshape(4, 88, D)])
    m["up1"] = np.concatenate([ups(a["L1_ffn_we1"], a["L1_ffn_we3"]),
                               ups(cut(a["L1_ffn_ws1"][None], 4), cut(a["L1_ffn_ws3"][None], 4))])
    m["down1"] = np.concatenate([a["L1_ffn_we2"], a["L1_ffn_ws2"].reshape(4, 128, D)])
    gu = a["L2_ffn_expert_gate_up"]
    m["up2"], m["down2"] = ups(gu[:, :, 0::2], gu[:, :, 1::2]), a["L2_ffn_expert_down"]
    gu = a["L3_ffn_gate_up_w"]
    m["up3"] = np.concatenate([ups(gu[:, :, :128], gu[:, :, 128:]),
                               ups(a["L3_ffn_shared_gate_w"][None], a["L3_ffn_shared_up_w"][None])])
    m["down3"] = np.concatenate([a["L3_ffn_down_w"], a["L3_ffn_shared_down_w"][None]])

    nc = bacc.Bacc("TRN2", target_bir_lowering=False, num_devices=1)
    arrays = {f"in_{k}": np.ascontiguousarray(w) for k, w in m.items()}
    A = {k[3:]: nc.dram_tensor(k, w.shape, mybir.dt.from_np(w.dtype), kind="ExternalInput").ap()
         for k, w in arrays.items()}
    A["prT"] = nc.dram_tensor("prT", (8, NTOK), mybir.dt.float32, kind="Internal").ap()
    out = nc.dram_tensor("out_x", (NB, NQ, D), mybir.dt.float32, kind="ExternalOutput").ap()
    flamingo_kernel(nc, A, out)
    r = run(nc, [arrays], core_ids=[0])
    return r.results[0]["out_x"]
```

```python
import numpy as np
from contextlib import ExitStack
import concourse.bass as bass
from concourse import mybir

NSUB = 8

NB, NQ, QP = 8, 56, 64
TT, D, KT = 4, 256, 2
NTOK = NB * QP
NCTX, CH, NCH = 1500, 500, 3
CT, NCT = 125, 12
NH, NP, HD = 16, 8, 16
NEG = -1.0e30

MOE = [dict(I=96, U=36, E=16, K=6, per=2), dict(I=128, U=20, E=16, K=4, per=1),
       dict(I=128, U=8, E=8, K=2, per=1), dict(I=128, U=9, E=8, K=2, per=1)]
MOE_BASE = [0, 36, 56, 64]

LOOK, NW = 8, 9
GT, NG = 8, 7
GW = GT * NW
WB = NQ * NW
GR, NGT = 126, 4
R, QC, HDL = 64, 96, 128
SCALE1 = float(1.0 / np.sqrt(192.0).astype(np.float32))


def flamingo_kernel(nc, A, out):
    F32, I32, U8 = mybir.dt.float32, mybir.dt.int32, mybir.dt.uint8
    U32 = mybir.dt.uint32
    ALU, ACT, AX = mybir.AluOpType, mybir.ActivationFunctionType, mybir.AxisListType
    ctx = ExitStack()
    with ctx:
        def sb(name, shape, dt=F32):
            return ctx.enter_context(nc.sbuf_tensor(name, shape, dt))

        sems = {}

        def sem(name):
            if name not in sems:
                sems[name] = ctx.enter_context(nc.semaphore(name))
            return sems[name]

        x = sb("x", [128, TT, D])
        h = sb("h", [128, TT, D])
        onat = sb("onat", [128, TT, D])
        acc = sb("acc", [128, TT, D])
        tmp = sb("tmp", [128, TT, D])
        hT = sb("hT", [128, KT, NTOK])
        qT = sb("qT", [128, KT, NTOK])
        oT = sb("oT", [128, KT, NTOK])
        ident = sb("ident", [128, 128])
        turned_ident = sb("turned_ident", [128, 128])
        headmask = sb("headmask", [128, NP])
        tg = sb("tg", [128, 8])
        stats = sb("stats", [128, TT, 6])
        mv = sb("mv", [128, TT, 2])
        sm = sb("sm", [128, 16, TT])
        cols = sb("cols", [128, 16])
        rows = sb("rows", [128, 3, D])
        lg = sb("lg", [128, 10, TT, 16])
        top8 = sb("top8", [128, TT, 8])
        cw = sb("cw", [128, TT, 36])
        w0 = sb("w0", [128, 5, KT, D])
        w2 = sb("w2", [128, 2, KT, D])
        w2n = sb("w2n", [128, 4, D])
        w2T = sb("w2T", [128, 4, D])
        w3 = w0[:, 0:4]
        gw = sb("gw", [128, 4, KT, 16])
        wu = sb("wu", [128, 4, KT, 2 * 128])
        wd = sb("wd", [128, 4, D])

        ctxT = sb("ctxT", [128, 2, KT, NCTX])
        kT = sb("kT", [128, 2, KT, NCTX])
        v = sb("v", [128, 2, NCT, D])
        supT = sb("supT", [128, KT, NCTX])
        maskf = supT
        maskraw = sb("maskraw", [128, 2, NCTX // 4], I32)
        area = sb("area", [128, NH * NTOK])
        Sb = area[:, 0:2 * NCTX].rearrange("p (r n) -> p r n", r=2)
        PT = area[:, 2 * NCTX:2 * NCTX + 2 * NCH * 512].rearrange("p (r g n) -> p r g n", r=2, g=NCH)
        Qb = sb("Qb", [128, 2, KT, 8 * QP])
        mx = sb("mx", [128, 4, 4])
        nm = sb("nm", [128, 4])
        rsum = sb("rsum", [128, 2, NP])
        rinv = sb("rinv", [128, 2, NP])
        oTs = sb("oTs", [128, 2, D])

        meanT = sb("meanT", [128, KT, NB])
        segf = sb("segf", [128, NB * NQ])
        seg = qT[:, 0, 0:NB * NQ].bitcast(I32)
        gidx = sb("gidx", [128, 3, NB * NGT])
        gseg = sb("gseg", [128, NB * NGT], I32)
        grow = sb("grow", [128, NB * NGT], I32)
        grow4 = sb("grow4", [128, 2, NGT], I32)
        anyv = sb("anyv", [128, 2, 2, NQ])
        sm1 = sb("sm1", [128, 4, NG])
        flags = sb("flags", [128, 104])
        mkv = sb("mkv", [128, NB])

        kflat = kT[:, :, :, :].rearrange("p a k n -> p (a k n)")
        wuqT = kflat[:, 0:1536].rearrange("p (h n) -> p h n", h=16)
        wukT = kflat[:, 1536:2560].rearrange("p (h n) -> p h n", h=16)
        wuvT = kflat[:, 2560:3584].rearrange("p (h n) -> p h n", h=16)
        wqr2 = kflat[0:QC, 3584:4608].rearrange("p (h n) -> p h n", h=16)
        wdq = kflat[:, 4608:4800].rearrange("p (k n) -> p k n", k=2)
        wkvc = kflat[:, 4800:4928].rearrange("p (k n) -> p k n", k=2)
        wkr = kflat[0:R, 4928:5056]
        wstk = kflat[:, 5056:5120]
        blk = kflat[:, 5120:5192]
        jrow = kflat[:, 5192:5201]
        vflat = v[:, :, :, :].rearrange("p a j d -> p (a j d)")
        wo1 = vflat[:, 0:4096].rearrange("p (h n) -> p h n", h=16)
        ocT = vflat[:, 0:4096].rearrange("p (h n) -> p h n", h=8)
        wcomb = vflat[0:QC, 4096:6144].rearrange("p (h n) -> p h n", h=16)
        cflat = ctxT[:, :, :, :].rearrange("p a k n -> p (a k n)")
        wuvo = cflat[:, 0:2048].rearrange("p (h n) -> p h n", h=8)
        qcT = cflat[0:QC, 2048:2560]
        G = cflat[0:GR, 2560:5632].rearrange("p (a t n) -> p a t n", a=2, t=NGT)
        sflat = supT[:, :, :].rearrange("p k n -> p (k n)")
        gT = sflat[:, 0:1008].rearrange("p (k n) -> p k n", k=2)
        csT, prod, P1 = sflat[:, 1008:1512], sflat[:, 1512:2016], sflat[:, 2016:2520]
        kvm = kflat[:, 5201:5705]
        qeff = area[:, 0:8192].rearrange("p (b h q) -> p b h q", b=NB, h=16)
        qflat = Qb[:, :, :, :].rearrange("p a k n -> p (a k n)")
        qb1 = [qflat[:, 1024 * j:1024 * j + 1024].rearrange("p (q h) -> p q h", h=16) for j in range(2)]
        kvn = [y[0:GW].rearrange("p k n -> p (k n)")[:, 0:896].rearrange("p (g c) -> p g c", g=NG)
               for y in (oT[:, :, :], h[:, :, :])]
        PT1 = qT[0:GW, :, :].rearrange("p k n -> p (k n)")[:, 0:896].rearrange("p (g c) -> p g c", g=NG)
        aflat = acc[:, :, :].rearrange("p t d -> p (t d)")
        kid, valid = aflat[:, 0:504], aflat[:, 504:1008]
        cosq = tmp[:, 0:2, :].rearrange("p t d -> p (t d)")
        sinq = tmp[:, 2:4, :].rearrange("p t d -> p (t d)")
        rope2 = h[:, 0:2, :].rearrange("p t d -> p (t d)")
        tflat = tmp[:, :, :].rearrange("p t d -> p (t d)")
        keff = [tflat[:, WB * j:WB * j + WB] for j in range(2)]
        oflat = onat[:, :, :].rearrange("p t d -> p (t d)")
        madd = [oflat[:, WB * j:WB * j + WB] for j in range(2)]

        sg = Sb[:, 0, 0:1024].rearrange("p (k n) -> p k n", k=2)
        act_b = Sb[:, 1, 0:1024].rearrange("p (k n) -> p k n", k=2)
        pb = PT[:, 0, 0:2, :]
        xin = area[:, 4096:6144].rearrange("p (a k n) -> p a k n", a=2, k=2)

        P = [ctx.enter_context(nc.psum_tensor(f"P{i}", [128, 512], F32)) for i in range(8)]

        block = ctx.enter_context(nc.Block())

        def real(y):
            return y.rearrange("p (b q) -> p b q", q=QP)[:, :, 0:NQ]

        ATT = {0: 0, 2: 1, 3: 2}
        NPROJ = {0: 12, 2: 12, 3: 18}
        TURN = (3, 4, 6)

        @block.gpsimd
        def _(pool):
            pool.wait_ge(sem("sub_done"), 1)
            for dst, name in ((wuqT, "wuqT"), (wukT, "wukT"), (wuvT, "wuvT"), (wqr2, "wqr2"), (wdq, "wdq"),
                              (wkvc, "wkvc"), (wkr, "wkr"), (wstk, "wstk"), (blk, "blk"), (wo1, "wo1"),
                              (wcomb[:, :, 64:128], "wqr"), (cosq[64:128, :], "cosq"), (sinq[64:128, :], "sinq")):
                pool.dma_start(dst, A[name]).then_inc(sem("w1_in"), 16)
            pool.dma_start(w3, A["w3"]).then_inc(sem("w1_in"), 16)
            pool.dma_start(jrow, A["jrow"].partition_broadcast(128)).then_inc(sem("w1_in"), 16)
            pool.wait_ge(sem("rows_ready"), 1)
            pool.wait_ge(sem("w1_in"), 16 * 15)
            pool.wait_ge(sem("sub_done"), 2)

            def masks(b, bi):
                by9 = lambda y: y.rearrange("p (t j) -> p t j", j=NW)
                by72 = lambda y: y.rearrange("p (g n) -> p g n", g=NG)
                G_ = nc.gpsimd

                def step(k, ins):
                    ins.then_inc(sem("mask1_step"), 1)
                    pool.wait_ge(sem("mask1_step"), b * 7 + k)
                    pool.sem_inc(sem("waits_met"), 1)

                pool.wait_ge(sem("p1_taken"), b + 1)
                pool.sem_inc(sem("waits_met"), 1)
                step(1, G_.tensor_tensor(by9(kid), segf[:, bass.ds(b * NQ, NQ)].rearrange("p (t o) -> p t o", o=1).broadcast_to([128, NQ, NW]),
                                         jrow.rearrange("p (o j) -> p o j", o=1).broadcast_to([128, NQ, NW]), ALU.subtract))
                step(2, G_.tensor_scalar(valid, kid, -0.5, None, ALU.is_gt))
                step(3, G_.tensor_scalar(kid, kid, NCTX - 0.5, None, ALU.is_lt))
                step(4, G_.tensor_tensor(anyv[:, bi, 0, :], by9(valid)[:, :, 0], by9(kid)[:, :, NW - 1], ALU.mult))
                step(5, G_.tensor_tensor(valid, kid, valid, ALU.mult))
                step(6, G_.tensor_scalar(madd[bi], valid, -NEG, NEG, ALU.mult, ALU.add))
                step(7, G_.tensor_tensor(by72(madd[bi]), by72(madd[bi]), blk.rearrange("p (o n) -> p o n", o=1).broadcast_to([128, NG, GW]),
                                         ALU.add))
                G_.tensor_scalar(anyv[:, bi, 1, :], anyv[:, bi, 0, :], -1.0, 1.0, ALU.mult, ALU.add).then_inc(sem("mask1_made"), 1)

            with pool.Fori(0, NB // 2) as i:
                for bi in range(2):
                    b = i * 2 + bi
                    pool.wait_ge(sem("g_turned"), b + 1)
                    nc.gpsimd.tensor_copy(grow4[:, bi, :], grow[:, bass.ds(i * 8 + 4 * bi, NGT)]).then_inc(sem("row_copied"), 1)
                    pool.wait_ge(sem("row_copied"), b + 1)
                    pool.sem_inc(sem("waits_met"), 1)
                    for t in range(NGT):
                        pool.indirect_dma_start(out=G[:, bi, t, :], out_offset=None, in_=A["ctxrows"],
                                                in_offset=bass.IndirectOffsetOnAxis(
                                                    ap=grow4[0:GR, bi, t:t + 1].bitcast(U32), axis=0)
                                                ).then_inc(sem(f"g_in{bi}"), 16)
                    masks(b, bi)
            if NSUB > 4:
                pool.wait_ge(sem("sub_done"), 3)
                nc.gpsimd.memset(maskf[:, :, :], 0.0).then_inc(sem("mask_cleared"), 1)

        @block.sync
        def _(sp):
            sp.wait_ge(sem("x_cleared"), 1)
            for b in range(NB):
                sp.dma_start(x[QP * (b % 2):QP * (b % 2) + NQ, b // 2, :], A["x"][b]).then_inc(sem("x_in"), 16)
            for dst, name in ((ident[:, :], "ident"), (turned_ident[:, :], "turned_ident"), (headmask[:, :], "headmask"), (cols[:, :], "cols"),
                              (w2n[:, :, :], "w2n"), (w0[:, :, :, :], "w0"), (gw[:, :, :, :], "gw"),
                              (w2[:, :, :, :], "w2")):
                sp.dma_start(dst, A[name]).then_inc(sem("const_in"), 16)
            sp.dma_start(tg[:, :], A["gates"].partition_broadcast(128)).then_inc(sem("const_in"), 16)
            sp.dma_start(seg, A["seg"].partition_broadcast(128)).then_inc(sem("const_in"), 16)
            sp.dma_start(gseg[0:GR, :], A["gseg"]).then_inc(sem("const_in"), 16)
            sp.dma_start(gidx[0:GR, 1:3, :], A["gconst"]).then_inc(sem("const_in"), 16)
            for r in range(3):
                sp.dma_start(rows[:, r, :], A["rows"][r].partition_broadcast(128)).then_inc(sem("const_in"), 16)

            def attention_loads(l):
                a = ATT[l]
                if l:
                    sp.wait_ge(sem("sub_done"), 2 * l - 1)
                with sp.Fori(0, NB // 2) as i:
                    for bi in range(2):
                        sp.wait_ge(sem("proj_done"), (i * 2 + bi) * NPROJ[l] + ((0, 96, 192)[a] + 18 - NPROJ[l]))
                        sp.sem_inc(sem("waits_met"), 1)
                        if l == 0:
                            sp.wait_ge(sem("mean_done"), i * 2 + (bi + 1))
                        sp.sem_inc(sem("waits_met"), 1)
                        sp.dma_start(ctxT[:, bi], A["ctxT"][i * 2 + bi]).then_inc(sem(f"ctx_in{bi}"), 16)
                        if l == 0:
                            sp.wait_ge(sem("mask_used"), i * 2 + (bi + 1))
                            sp.sem_inc(sem("waits_met"), 1)
                            sp.dma_start(maskraw[:, bi, :],
                                         A["mask0"][i * 2 + bi].partition_broadcast(128)).then_inc(sem(f"mask_in{bi}"), 16)
                        if l == 2:
                            sp.wait_ge(sem("mask_cleared"), 1)
                            sp.wait_ge(sem("mask_used"), i * 2 + (8 + bi + 1))
                            sp.sem_inc(sem("waits_met"), 1)
                            for half in range(2):
                                sp.dma_start(maskf[QP * half:QP * half + NQ, bi, :],
                                             A["mask2"][i * 2 + bi]).then_inc(sem(f"mask_in{bi}"), 16)

            def mixture_loads(l):
                I, U, base = MOE[l]["I"], MOE[l]["U"], MOE_BASE[l]

                def unit(q, u):
                    sp.wait_ge(sem("down_done"), u + (base + 1))
                    sp.sem_inc(sem("waits_met"), 1)
                    sp.dma_start(wu[:, q, :, 0:2 * I], A[f"up{l}"][u]).then_inc(sem(f"w_in{q}"), 16)
                    sp.dma_start(wd[0:I, q, :], A[f"down{l}"][u]).then_inc(sem(f"w_in{q}"), 16)

                def probabilities(u):
                    sp.wait_ge(sem("xin_ready"), u + 1)
                    sp.dma_start(pb[:, u % 2, :], A["prT"][u].partition_broadcast(128)).then_inc(sem(f"pb_in{u % 2}"), 16)

                if l == 3:
                    for u in range(4):
                        unit(u, u)
                    sp.wait_ge(sem("prT_sb"), 1)
                    sp.dma_start(A["prT"], qT[0:8, 0, :]).then_inc(sem("prT_out"), 16)
                    sp.wait_ge(sem("prT_out"), 16)
                    for u in range(U - 1):
                        probabilities(u)
                        if 2 <= u < U - 2:
                            unit((u + 2) % 4, u + 2)
                    return
                with sp.Fori(0, U // 4) as i:
                    for q in range(4):
                        unit(q, i * 4 + q)

            for s in range(NSUB):
                l = s // 2
                if s % 2 == 0 and l in ATT:
                    attention_loads(l)
                elif s % 2:
                    mixture_loads(l)
            sp.wait_ge(sem("sub_done"), NSUB)
            for b in range(NB):
                sp.dma_start(out[b], x[QP * (b % 2):QP * (b % 2) + NQ, b // 2, :]).then_inc(sem("stored"), 16)
            sp.wait_ge(sem("stored"), 16 * NB)

        @block.tensor
        def _(pe):
            n_tr = [0]

            def tokens_to_T(src):
                for k in range(KT):
                    for t in range(TT):
                        last = nc.tensor.transpose(P[6 + k][:, 128 * t:128 * t + 128],
                                                   src[:, t, 128 * k:128 * k + 128], ident[:, :])
                last.then_inc(sem("tr_psum"), 1)
                n_tr[0] += 1

            def wait_T(n=None):
                n = n or n_tr[0]
                pe.wait_ge(sem("tr_act"), n)
                pe.wait_ge(sem("tr_dve"), n)

            def attention(l, part):
                a = ATT[l]
                wk, wv = (w0[:, 1], w0[:, 2]) if l == 0 else (w2[:, 0], w2[:, 1]) if l == 2 else (w3[:, 2], w3[:, 3])
                na, nv = (0, 48, 96)[a], 48 * a
                pa = NPROJ[l] - 6

                def bank_free(B, g):
                    if g < 2:
                        pe.wait_ge(sem("v_ready"), B * 6 + (nv + 1))
                    elif g - 2 < pa:
                        pe.wait_ge(sem("k_ready"), B * pa + (na + g - 1))
                    else:
                        pe.wait_ge(sem("v_ready"), B * 6 + (nv + g - pa))

                def project_features(B, bi, g, w, src):
                    for o in range(KT):
                        for c in range(NCH):
                            bank_free(B, g)
                            for k in range(KT):
                                last = nc.tensor.matmul(P[6 + g % 2][:, 0:CH], w[:, k, 128 * o:128 * o + 128],
                                                        src[:, k, CH * c:CH * c + CH], start=k == 0, stop=k == 1)
                            last.then_inc(sem("proj_done"), 1)
                            g += 1

                def project_keys(B, i, bi):
                    pe.wait_ge(sem(f"ctx_in{bi}"), i * 16 + 16 * (4 * a + 1))
                    if l == 3:
                        project_features(B, bi, 0, w3[:, 0], ctxT[:, bi])
                        pe.wait_ge(sem("k_ready"), B * pa + (na + 6))
                    project_features(B, bi, pa - 6, wk, supT[:, :, :] if l == 3 else ctxT[:, bi])

                def project_values(B, bi):
                    src = supT[:, :, :] if l == 3 else ctxT[:, bi]
                    for j in range(6):
                        g = pa + j
                        bank_free(B, g)
                        for jj in range(2):
                            c0 = CT * (2 * j + jj)
                            for k in range(KT):
                                last = nc.tensor.matmul(P[6 + g % 2][0:CT, D * jj:D * jj + D],
                                                        src[:, k, c0:c0 + CT], wv[:, k, :], start=k == 0, stop=k == 1)
                        last.then_inc(sem("proj_done"), 1)

                def scores(n, B, bi, p):
                    if p == 0:
                        pe.wait_ge(sem("k_ready"), B * pa + (na + pa))
                    if p == 0:
                        pe.wait_ge(sem("qb_ready"), B * 2 + (16 * a + 2))
                    for c in range(NCH):
                        pe.wait_ge(sem("s_taken"), n * 3 + (c + 1))
                        nc.tensor.matmul(P[c][:, 0:CH], Qb[:, bi, p // 4, 128 * (p % 4):128 * (p % 4) + 128],
                                         kT[:, bi, p // 4, CH * c:CH * c + CH], start=True, stop=True
                                         ).then_inc(sem("s_done"), 1)

                def turn(n, B, p):
                    pe.wait_ge(sem("exp_done"), n + 1)
                    for g in range(NCH):
                        if g == 0:
                            pe.wait_ge(sem("pt_act"), n * 2 + 1)
                        elif g == 1:
                            pe.wait_ge(sem("pt_dve"), n + 1)
                        else:
                            pe.wait_ge(sem("pt_act"), n * 2 + 2)
                            if p == 0:
                                pe.wait_ge(sem("v_ready"), B * 6 + (nv + 7))
                        for j in range(4):
                            c0 = CT * (4 * g + j)
                            last = nc.tensor.transpose(P[TURN[g]][0:CT, 128 * j:128 * j + 128],
                                                       Sb[:, p % 2, c0:c0 + CT], ident[:, :])
                        last.then_inc(sem("t_done"), 1)

                def values(n, B, bi, p):
                    if p == 0:
                        pe.wait_ge(sem("v_ready"), B * 6 + (nv + 7))
                        pe.wait_ge(sem("o_taken"), B + (8 * a + 1))
                    pe.wait_ge(sem("pt_act"), n * 2 + 4)
                    pe.wait_ge(sem("pt_dve"), n + 2)
                    for j in range(NCT):
                        r, c0 = 32 * ((p + 2 * (j % 2)) % 4), D * (j % 2) + 128 * (p // 4)
                        last = nc.tensor.matmul(real(P[5][r:r + 32, c0:c0 + 128]), v[0:CT, bi, j, 32 * p:32 * p + 32],
                                                real(PT[0:CT, p % 2, j // 4, 128 * (j % 4):128 * (j % 4) + 128]),
                                                start=j < 2, stop=j >= NCT - 2)
                    last.then_inc(sem("pv_done"), 1)

                def heads_to_rows(B):
                    pe.wait_ge(sem("oT_sb"), B + (8 * a + 1))
                    for k in range(KT):
                        for e, turn_to in enumerate((ident, turned_ident)):
                            last = nc.tensor.matmul(P[5][:, 128 * k:128 * k + 128], oTs[:, e, 128 * k:128 * k + 128],
                                                    turn_to[:, :], start=e == 0, stop=e == 1)
                    last.then_inc(sem("on_psum"), 1)

                def batch(i, bi, more):
                    B = i * 2 + bi
                    n0 = i * 16 + (64 * a + 8 * bi)
                    for p in range(NP - 1):
                        scores(n0 + (p + 1), B, bi, p + 1)
                        turn(n0 + p, B, p)
                        if p >= 1:
                            values(n0 + (p - 1), B, bi, p - 1)
                    if more:
                        pe.wait_ge(sem("pt_act"), n0 * 2 + 16)
                        project_keys(B + 1, i + bi, 1 - bi)
                        pe.wait_ge(sem("k_ready"), B * pa + (na + 2 * pa))
                    turn(n0 + 7, B, 7)
                    values(n0 + 6, B, bi, 6)
                    values(n0 + 7, B, bi, 7)
                    if more:
                        project_values(B + 1, 1 - bi)
                        scores(n0 + 8, B + 1, 1 - bi, 0)
                    heads_to_rows(B)

                if part == "keys":
                    project_keys(0, 0, 0)
                    pe.wait_ge(sem("k_ready"), na + pa)
                    return
                project_values(0, 0)
                scores(64 * a, 0, 0, 0)
                with pe.Fori(0, NB // 2 - 1) as i:
                    batch(i, 0, True)
                    batch(i, 1, True)
                batch(NB // 2 - 1, 0, True)
                batch(NB // 2 - 1, 1, False)

            def mixture(l):
                I, U, base, E = MOE[l]["I"], MOE[l]["U"], MOE_BASE[l], MOE[l]["E"]
                wait_T()
                for t in range(TT):
                    for k in range(KT):
                        last = nc.tensor.matmul(P[7][:, 16 * t:16 * t + E], hT[:, k, 128 * t:128 * t + 128],
                                                gw[:, l, k, 0:E], start=k == 0, stop=k == 1)
                last.then_inc(sem("logits"), 1)
                if l == 3:
                    pe.wait_ge(sem("cw_ready"), 4)
                    for t in range(TT):
                        last = nc.tensor.transpose(P[6][0:8, 128 * t:128 * t + 128], lg[:, 9, t, 0:8], ident[:, :])
                    last.then_inc(sem("prT_psum"), 1)

                def up(q, u, i, xin_used):
                    k = q % 2
                    pe.wait_ge(sem(f"w_in{q}"), i * 32 + 32 * (base // 4 + 1))
                    pe.wait_ge(sem("act_ready"), u + (base + 1))
                    if xin_used:
                        pe.wait_ge(sem("xin_ready"), u + 3)
                    rhs = xin[:, k] if xin_used else hT
                    for half in range(2):
                        for kk in range(KT):
                            last = nc.tensor.matmul(P[k + 2 * half][0:I, 0:NB * NQ], wu[:, q, kk, I * half:I * half + I],
                                                    real(rhs[:, kk, :]), start=kk == 0, stop=kk == 1)
                        last.then_inc(sem("gu_done"), 1)

                def down(q, u):
                    k = q % 2
                    pe.wait_ge(sem("act_ready"), u + (base + 3))
                    pe.wait_ge(sem("acc_done"), u + (base + 1))
                    for t in range(TT):
                        last = nc.tensor.matmul(P[4 + 2 * k + t // 2][:, D * (t % 2):D * (t % 2) + D],
                                                act_b[0:I, k, 128 * t:128 * t + 128], wd[0:I, q, :],
                                                start=True, stop=True)
                    last.then_inc(sem("down_done"), 1)

                if l == 3:
                    up(0, 0, 0, True)
                    for u in range(1, U):
                        up(u % 4, u, u // 4, u < U - 1)
                        down((u - 1) % 4, u - 1)
                    down((U - 1) % 4, U - 1)
                    return
                up(0, 0, 0, False)
                with pe.Fori(0, U // 4 - 1) as i:
                    for q in range(4):
                        up((q + 1) % 4, i * 4 + (q + 1), i + (q + 1) // 4, False)
                        down(q, i * 4 + q)
                for q in range(4):
                    if q < 3:
                        up(q + 1, U - 3 + q, U // 4 - 1, False)
                    down(q, U - 4 + q)

            def absorbed_weights():
                pe.wait_ge(sem("act_ready"), MOE_BASE[1] + 2)
                pe.wait_ge(sem("acc_done"), MOE_BASE[1] + 1)
                pe.wait_ge(sem("w1_in"), 16 * 15)
                for hh in range(NH):
                    last = nc.tensor.matmul(P[hh // 8][0:QC, 64 * (hh % 8):64 * (hh % 8) + 64], wuqT[:, hh, :],
                                            wukT[:, hh, :], start=True, stop=True)
                for hh in range(NH):
                    r, hp = 64 * (hh % 2), hh // 2
                    last = nc.tensor.matmul(P[2 + hp // 2][r:r + 64, D * (hp % 2):D * (hp % 2) + D], wuvT[:, hh, :],
                                            wo1[:, hh, :], start=True, stop=True)

            def window():
                wait_T()
                for k in range(KT):
                    last = nc.tensor.matmul(P[6][0:QC, :], wdq[:, k, :], hT[:, k, :], start=k == 0, stop=k == 1)
                for k in range(KT):
                    last = nc.tensor.matmul(P[7][0:R, 0:NB], wkvc[:, k, :], meanT[:, k, :], start=k == 0, stop=k == 1)
                last.then_inc(sem("pre1_psum"), 1)
                pe.wait_ge(sem("pre1_act"), 1)
                pe.wait_ge(sem("pre1_dve"), 1)
                for hh in range(NH):
                    r = hh % 4
                    if hh >= 4:
                        pe.wait_ge(sem("qn_taken"), hh - 3)
                        pe.wait_ge(sem("qr_taken"), hh - 3)
                    nc.tensor.matmul(P[r][:, :], wcomb[:, hh, :], qcT, start=True, stop=True)
                    nc.tensor.matmul(P[4 + r][64:128, :], wqr2[:, hh, :], qcT, start=True, stop=True
                                     ).then_inc(sem("qh_psum"), 1)
                pe.wait_ge(sem("qn_taken"), NH)
                pe.wait_ge(sem("qr_taken"), NH)

                def turn_rows(b, i, bi):
                    pe.wait_ge(sem(f"g_in{bi}"), i * 64 + 64)
                    pe.wait_ge(sem("keff_sb"), b + 1)
                    for f in range(3):
                        for t in range(NGT):
                            last = nc.tensor.transpose(P[f][:, GR * t:GR * t + GR],
                                                       G[:, bi, t, 128 * f:128 * f + 128], ident[0:GR, 0:GR])
                    last.then_inc(sem("g_turned"), 1)

                def compress(b):
                    pe.wait_ge(sem("g_act"), b + 1)
                    pe.wait_ge(sem("g_dve"), b + 1)
                    for k in range(KT):
                        last = nc.tensor.matmul(P[0][0:R, 0:WB], wkvc[:, k, :], gT[:, k, :], start=k == 0, stop=k == 1)
                    last.then_inc(sem("kv_psum"), 1)

                def key_terms(b, bi):
                    pe.wait_ge(sem("kv_sb"), b + 1)
                    nc.tensor.matmul(P[1][:, 0:WB], wkr, keff[bi][0:R, :], start=True, stop=True).then_inc(sem("kr_psum"), 1)
                    for g in range(NG):
                        last = nc.tensor.transpose(P[2][0:GW, R * g:R * g + R], keff[bi][0:R, GW * g:GW * g + GW],
                                                   ident[0:R, 0:R])
                    last.then_inc(sem("kvn_psum"), 1)

                def rotate(b):
                    pe.wait_ge(sem("prod_sb"), b + 1)
                    nc.tensor.matmul(P[0][64:128, 0:WB], wstk, prod, start=True, stop=True).then_inc(sem("krs_psum"), 1)

                def scores1(b, bi):
                    pe.wait_ge(sem("keff_sb"), b + 2)
                    pe.wait_ge(sem("qb1_sb"), b + 1)
                    for g in range(NG):
                        last = nc.tensor.matmul(P[3][:, GW * g:GW * g + GW], qb1[bi][:, GT * g:GT * g + GT, :].rearrange("p q h -> p (q h)"),
                                                keff[bi][:, GW * g:GW * g + GW], start=True, stop=True)
                    last.then_inc(sem("s1_psum"), 1)

                def turn_weights(b):
                    pe.wait_ge(sem("p1_sb"), b + 1)
                    for g in range(NG):
                        last = nc.tensor.transpose(P[4 + g // 4][0:GW, 128 * (g % 4):128 * (g % 4) + 128],
                                                   P1[:, GW * g:GW * g + GW], ident[:, :])
                    last.then_inc(sem("pt1_psum"), 1)

                def sums(b, bi):
                    pe.wait_ge(sem("pt1_sb"), b + 1)
                    pe.wait_ge(sem("p1_taken"), b + 2)
                    for g in range(NG):
                        last = nc.tensor.matmul(P[6 + g // 4][:, 128 * (g % 4):128 * (g % 4) + 128], kvn[bi][:, g, :],
                                                PT1[:, g, :], start=True, stop=True)
                    last.then_inc(sem("oc_psum"), 1)

                def batch(i, bi, more):
                    b = i * 2 + bi
                    scores1(b, bi)
                    if more:
                        turn_rows(b + 1, i + bi, 1 - bi)
                        compress(b + 1)
                    turn_weights(b)
                    if more:
                        key_terms(b + 1, 1 - bi)
                    sums(b, bi)
                    if more:
                        rotate(b + 1)

                turn_rows(0, 0, 0)
                compress(0)
                key_terms(0, 0)
                rotate(0)
                with pe.Fori(0, NB // 2 - 1) as i:
                    batch(i, 0, True)
                    batch(i, 1, True)
                batch(NB // 2 - 1, 0, True)
                batch(NB // 2 - 1, 1, False)
                pe.wait_ge(sem("p1_taken"), NB + 2)
                for t in range(TT):
                    for hp in range(NP):
                        last = nc.tensor.matmul(P[t // 2][:, D * (t % 2):D * (t % 2) + D], ocT[:, hp, 128 * t:128 * t + 128],
                                                wuvo[:, hp, :], start=hp == 0, stop=hp == NP - 1)
                last.then_inc(sem("out1_psum"), 1)

            pe.wait_ge(sem("const_in"), 16 * 15)
            pe.wait_ge(sem("w2n_ready"), 1)
            for m in range(2):
                for k in range(KT):
                    for o in range(KT):
                        last = nc.tensor.transpose(P[m][:, D * k + 128 * o:D * k + 128 * o + 128],
                                                   w2n[:, 2 * m + o, 128 * k:128 * k + 128], ident[:, :])
            last.then_inc(sem("w2T_psum"), 1)

            for s in range(NSUB):
                l = s // 2
                if s % 2 == 0 and l in ATT:
                    if l:
                        pe.wait_ge(sem("acc_done"), MOE_BASE[l] + 2)
                        pe.wait_ge(sem("w1_in"), 16 * 15)
                    attention(l, "keys")
                if s == 2:
                    absorbed_weights()
                pe.wait_ge(sem("h_ready"), s + 1)
                tokens_to_T(h)
                if s % 2:
                    mixture(l)
                    continue
                if l == 1:
                    window()
                    continue
                a = ATT[l]
                wait_T()
                src = hT
                if l == 3:
                    for o in range(KT):
                        for k in range(KT):
                            last = nc.tensor.matmul(P[o][:, :], w3[:, 0, k, 128 * o:128 * o + 128], hT[:, k, :],
                                                    start=k == 0, stop=k == 1)
                    last.then_inc(sem("refT_psum"), 1)
                    pe.wait_ge(sem("refT_sb"), 2)
                    src = oT
                    for t in range(TT):
                        for k in range(KT):
                            last = nc.tensor.transpose(P[2 + t // 2][:, D * (t % 2) + 128 * k:D * (t % 2) + 128 * k + 128],
                                                       oT[:, k, 128 * t:128 * t + 128], ident[:, :])
                    last.then_inc(sem("ref_psum"), 1)
                    pe.wait_ge(sem("ref_sb"), 1)
                wq = w0[:, 0] if l == 0 else w3[:, 1] if l == 3 else w2T[:, 0:2]
                for o in range(KT):
                    for k in range(KT):
                        last = nc.tensor.matmul(P[o][:, :], wq[:, k, 128 * o:128 * o + 128], src[:, k, :],
                                                start=k == 0, stop=k == 1)
                last.then_inc(sem("q_psum"), 1)
                pe.wait_ge(sem("q_sb"), a + 1)
                attention(l, "pairs")
                if l == 3:
                    continue
                pe.wait_ge(sem("o_ready"), a + 1)
                tokens_to_T(onat)
                wait_T()
                wo = w0[:, 3] if l == 0 else w2T[:, 2:4]
                for t in range(TT):
                    for k in range(KT):
                        last = nc.tensor.matmul(P[t // 2][:, D * (t % 2):D * (t % 2) + D],
                                                oT[:, k, 128 * t:128 * t + 128], wo[:, k, :],
                                                start=k == 0, stop=k == 1)
                if l == 0:
                    for t in range(TT):
                        for k in range(KT):
                            last = nc.tensor.matmul(P[2 + t // 2][:, D * (t % 2):D * (t % 2) + D],
                                                    hT[:, k, 128 * t:128 * t + 128], w0[:, 4, k, :],
                                                    start=k == 0, stop=k == 1)
                last.then_inc(sem("out_psum"), 1)

        @block.scalar
        def _(act):
            n_tr = [0]

            def transposed(dst, scale=1.0):
                n_tr[0] += 1
                act.wait_ge(sem("tr_psum"), n_tr[0])
                nc.scalar.activation(dst[:, 0, :], P[6][:, :], ACT.Copy, scale=scale).then_inc(sem("tr_act"), 1)

            def root(dst, src, n):
                act.wait_ge(sem("var_ready"), n)
                nc.scalar.activation(dst, src, ACT.Sqrt).then_inc(sem("std_ready"), 1)

            def attention(l, part):
                a = ATT[l]
                na = (0, 48, 96)[a]
                pa = NPROJ[l] - 6
                pd = (0, 96, 192)[a]

                def project_keys(B, bi):
                    g = 0
                    if l == 3:
                        for o in range(KT):
                            for c in range(NCH):
                                act.wait_ge(sem("proj_done"), B * 18 + (pd + 18 + g + 1))
                                nc.scalar.activation(supT[:, o, CH * c:CH * c + CH], P[6 + g % 2][:, 0:CH], ACT.Relu,
                                                     bias=cols[:, 6 + o:7 + o]).then_inc(sem("k_ready"), 1)
                                g += 1
                    for o in range(KT):
                        for c in range(NCH):
                            act.wait_ge(sem("proj_done"), B * NPROJ[l] + (pd + 18 + g + 1))
                            dst, src = kT[:, bi, o, CH * c:CH * c + CH], P[6 + g % 2][:, 0:CH]
                            if l == 0:
                                nc.scalar.activation(dst, src, ACT.Copy).then_inc(sem("k_ready"), 1)
                            else:
                                col = 4 + o if l == 2 else 10 + o
                                nc.scalar.activation(dst, src, ACT.Identity, bias=cols[:, col:col + 1]
                                                     ).then_inc(sem("k_ready"), 1)
                            g += 1

                def exps(n, bi, p):
                    act.wait_ge(sem("nm_ready"), n + 1)
                    nc.scalar.activation(Sb[:, p % 2, :], Sb[:, p % 2, :], ACT.Exp, bias=nm[:, p % 4:p % 4 + 1],
                                         accum_out=rsum[:, bi, p:p + 1]).then_inc(sem("exp_done"), 1)

                def turned(n, p):
                    act.wait_ge(sem("pv_done"), n + 1)
                    for g in (0, 2):
                        act.wait_ge(sem("t_done"), n * 3 + (12 + g + 1))
                        nc.scalar.activation(real(PT[0:CT, p % 2, g, :]), real(P[TURN[g]][0:CT, :]), ACT.Copy
                                             ).then_inc(sem("pt_act"), 1)

                def batch(i, bi, more):
                    B = i * 2 + bi
                    n0 = i * 16 + (64 * a + 8 * bi)
                    for p in range(NP - 1):
                        turned(n0 + p, p)
                        exps(n0 + (p + 1), bi, p + 1)
                    if more:
                        project_keys(B + 1, 1 - bi)
                    turned(n0 + 7, 7)
                    act.wait_ge(sem("pv_done"), n0 + (8 + 2))
                    act.wait_ge(sem("o_taken"), B + (8 * a + 1))
                    nc.scalar.activation(real(oTs[:, :, :].rearrange("p e d -> p (e d)")), real(P[5][:, :]), ACT.Copy
                                         ).then_inc(sem("oT_sb"), 1)
                    if more:
                        exps(n0 + 8, 1 - bi, 0)

                if part == "keys":
                    project_keys(0, 0)
                    return
                exps(64 * a, 0, 0)
                with act.Fori(0, NB // 2 - 1) as i:
                    batch(i, 0, True)
                    batch(i, 1, True)
                batch(NB // 2 - 1, 0, True)
                batch(NB // 2 - 1, 1, False)

            def mixture(l):
                I, U, base = MOE[l]["I"], MOE[l]["U"], MOE_BASE[l]
                act.wait_ge(sem("lg_ready"), l + 1)
                if l < 3:
                    nc.scalar.activation(lg[:, 2, :, :], lg[:, 1, :, :], ACT.Exp).then_inc(sem("lg_exp"), 1)
                else:
                    nc.scalar.activation(lg[:, 2, :, 0:8], lg[:, 0, :, 0:8], ACT.Sigmoid).then_inc(sem("lg_exp"), 1)

                def unit(k, u):
                    act.wait_ge(sem("gu_done"), u * 2 + (2 * base + 1))
                    act.wait_ge(sem("act_ready"), u + (base + 1))
                    nc.scalar.activation(sg[0:I, k, 0:NB * NQ], P[k][0:I, 0:NB * NQ], ACT.Silu).then_inc(sem("silu_done"), 1)

                with act.Fori(0, U // 2) as i:
                    unit(0, i * 2)
                    unit(1, i * 2 + 1)
                if U % 2:
                    unit(0, U - 1)

            def window():
                act.wait_ge(sem("pre1_psum"), 1)
                nc.scalar.activation(qcT, P[6][0:QC, :], ACT.Copy)
                nc.scalar.activation(mkv[0:R, :], P[7][0:R, 0:NB], ACT.Copy, scale=1.0 / NCTX)
                for j in range(2):
                    last = nc.scalar.activation(wcomb[:, 8 * j:8 * j + 8, 0:R],
                                                P[j][0:QC, :].rearrange("p (h n) -> p h n", h=8), ACT.Copy)
                last.then_inc(sem("pre1_act"), 1)
                for hh in range(NH):
                    act.wait_ge(sem("qh_psum"), hh + 1)
                    nc.scalar.activation(qeff[0:64, :, hh, :], P[hh % 4][0:64, :].rearrange("p (b q) -> p b q", b=NB),
                                         ACT.Copy).then_inc(sem("qn_taken"), 1)
                act.wait_ge(sem("qr_taken"), NH)

                def take_rows(b, bi):
                    act.wait_ge(sem("g_turned"), b + (2 + 1))
                    nc.scalar.activation(gT[:, 0, :], P[0][:, 0:WB], ACT.Copy)
                    nc.scalar.activation(csT, P[2][:, 0:WB], ACT.Copy).then_inc(sem("g_act"), 1)

                def take_queries(b, bi):
                    nc.scalar.activation(qb1[bi], qeff[:, bass.ds(b, 1), :, :].rearrange("p b h q -> p q (b h)"),
                                         ACT.Copy).then_inc(sem("qb1_sb"), 1)

                def take_keys(b, bi):
                    act.wait_ge(sem("kvn_psum"), b + 1)
                    src = P[2][0:GW, 0:NG * R].rearrange("p (g n) -> p g n", g=NG)
                    for j in range(2):
                        nc.scalar.activation(kvn[bi][:, :, R * j:R * j + R], src, ACT.Copy)
                    act.wait_ge(sem("krs_psum"), b + 1)
                    nc.scalar.activation(keff[bi][64:128, :], P[0][64:128, 0:WB], ACT.Copy).then_inc(sem("keff_sb"), 1)

                def batch(i, bi, more):
                    b = i * 2 + bi
                    if more:
                        take_rows(b + 1, 1 - bi)
                    act.wait_ge(sem("s1_sb"), b + 1)
                    nc.scalar.activation(P1, P1, ACT.Exp, scale=SCALE1).then_inc(sem("e1_sb"), 1)
                    if more:
                        take_queries(b + 1, 1 - bi)
                    act.wait_ge(sem("pt1_psum"), b + 1)
                    for j, m in ((0, 4), (1, 3)):
                        last = nc.scalar.activation(PT1[:, 4 * j:4 * j + m, :].rearrange("p g n -> p (g n)"),
                                                    P[4 + j][0:GW, 0:128 * m], ACT.Copy)
                    last.then_inc(sem("pt1_sb"), 1)
                    if more:
                        take_keys(b + 1, 1 - bi)

                take_rows(0, 0)
                take_queries(0, 0)
                take_keys(0, 0)
                with act.Fori(0, NB // 2 - 1) as i:
                    batch(i, 0, True)
                    batch(i, 1, True)
                batch(NB // 2 - 1, 0, True)
                batch(NB // 2 - 1, 1, False)

            act.wait_ge(sem("const_in"), 16 * 15)
            nc.scalar.activation(tg[:, :], tg[:, :], ACT.Tanh).then_inc(sem("tg_ready"), 1)
            nr = 0
            for s in range(NSUB):
                l = s // 2
                nr += 1
                if s % 2 == 0 and l in ATT:
                    attention(l, "keys")
                root(sm[:, 1, :], sm[:, 0, :], nr)
                if s == 0:
                    nr += 1
                    root(sm[:, 1, :], sm[:, 0, :], nr)
                transposed(hT, cols[:, 0:1] if s == 0 else 1.0)
                if s % 2:
                    mixture(l)
                    continue
                if l == 1:
                    window()
                    continue
                if l == 3:
                    act.wait_ge(sem("refT_psum"), 1)
                    for o in range(KT):
                        nc.scalar.activation(oT[:, o, :], P[o][:, :], ACT.Relu, bias=cols[:, 6 + o:7 + o]
                                             ).then_inc(sem("refT_sb"), 1)
                attention(l, "pairs")
                if l < 3:
                    transposed(oT)
                if l == 0:
                    act.wait_ge(sem("out_psum"), 1)
                    for j in range(2):
                        nc.scalar.activation(tmp[:, 2 * j:2 * j + 2, :], P[2 + j][:, :], ACT.Sigmoid
                                             ).then_inc(sem("gate_ready"), 1)

        @block.vector
        def _(dve):
            steps, n_tr, n_root, signals = [0], [0], [0], [0]
            V = nc.vector

            def step(ins):
                steps[0] += 1
                ins.then_inc(sem("dve_step"), 1)
                dve.wait_ge(sem("dve_step"), steps[0])

            def signal(name, n=1):
                signals[0] += 1
                V.memset(flags[:, signals[0]:signals[0] + 1], 0.0).then_inc(sem(name), n)

            def wide(col, n):
                return col.rearrange("p (t o) -> p t o", o=1).broadcast_to([128, TT, n])

            def transposed(dst, scale=None):
                n_tr[0] += 1
                dve.wait_ge(sem("tr_psum"), n_tr[0])
                if scale is None:
                    V.tensor_copy(dst[:, 1, :], P[7][:, :]).then_inc(sem("tr_dve"), 1)
                else:
                    V.tensor_scalar(dst[:, 1, :], P[7][:, :], scale, None, ALU.mult).then_inc(sem("tr_dve"), 1)

            def inverse_root():
                n_root[0] += 1
                V.tensor_scalar(sm[:, 0, :], sm[:, 0, :], 1.0, None, ALU.mult).then_inc(sem("var_ready"), 1)
                dve.wait_ge(sem("std_ready"), n_root[0])
                step(V.reciprocal(sm[:, 2, :], sm[:, 1, :]))

            def layer_norm():
                for t in range(TT):
                    step(V.bn_stats(stats[:, t, :], x[:, t, :]))
                for t in range(TT):
                    step(V.bn_aggr(mv[:, t, :], stats[:, t, :]))
                step(V.tensor_scalar(sm[:, 0, :], mv[:, :, 1], 1e-5, None, ALU.add))
                inverse_root()
                for t in range(TT):
                    step(V.tensor_scalar(h[:, t, :], x[:, t, :], mv[:, t, 0:1], sm[:, 2, t:t + 1],
                                         ALU.subtract, ALU.mult))

            def fake_quantise(w):
                magic = 12582912.0
                step(V.tensor_reduce(sm[:, 4, :], w[:, :, :], AX.X, ALU.max, apply_absolute_value=True))
                step(V.tensor_scalar(sm[:, 5, :], sm[:, 4, :], 1.0 / 127.0, 1e-8, ALU.mult, ALU.max))
                step(V.reciprocal(sm[:, 6, :], sm[:, 5, :]))
                step(V.tensor_tensor(w[:, :, :], w[:, :, :], wide(sm[:, 6, :], D), ALU.mult))
                step(V.tensor_scalar(w[:, :, :], w[:, :, :], magic, magic, ALU.add, ALU.subtract))
                step(V.tensor_scalar(w[:, :, :], w[:, :, :], 127.0, -127.0, ALU.min, ALU.max))
                return V.tensor_tensor(w[:, :, :], w[:, :, :], wide(sm[:, 5, :], D), ALU.mult)

            def residual(g, y):
                V.scalar_tensor_tensor(x[:, :, :].rearrange("p t d -> p (t d)"), y, tg[:, g:g + 1],
                                       x[:, :, :].rearrange("p t d -> p (t d)"), ALU.mult, ALU.add
                                       ).then_inc(sem("sub_done"), 1)
                dve.wait_ge(sem("sub_done"), (2 * g + 1) if g < 4 else 2 * (g - 4) + 2)

            def attention(l):
                a = ATT[l]
                pd = (0, 96, 192)[a]

                def queries(B, bi):
                    for k in range(KT):
                        V.tensor_tensor(Qb[:, bi, k, :].rearrange("p (e q) -> p e q", e=8),
                                        qT[:, k, bass.ds(B * QP, QP)].rearrange("p (o q) -> p o q", o=1).broadcast_to([128, 8, QP]),
                                        headmask[:, :].rearrange("p (e o) -> p e o", o=1).broadcast_to([128, 8, QP]),
                                        ALU.mult).then_inc(sem("qb_ready"), 1)

                def project_values(B, bi):
                    for j in range(6):
                        g = NPROJ[l] - 6 + j
                        dve.wait_ge(sem("proj_done"), B * NPROJ[l] + (pd + 18 + g + 1))
                        V.tensor_copy(v[0:CT, bi, 2 * j:2 * j + 2, :].rearrange("p j d -> p (j d)"),
                                      P[6 + g % 2][0:CT, :]).then_inc(sem("v_ready"), 1)

                def mask(B, i, bi):
                    if l == 0:
                        dve.wait_ge(sem(f"mask_in{bi}"), i * 16 + 16)
                        V.tensor_scalar(maskf[:, bi, :], maskraw[:, bi, :].bitcast(U8), -NEG, NEG, ALU.mult, ALU.add
                                        ).then_inc(sem("mask_made"), 1)
                        dve.wait_ge(sem("mask_made"), B + 1)
                    if l == 2:
                        dve.wait_ge(sem(f"mask_in{bi}"), i * 32 + 16 * 4 + 32)

                def maxima(n, B, bi, p):
                    r = p % 4
                    dve.wait_ge(sem("t_done"), n * 3 + 9)
                    for c in range(NCH):
                        dve.wait_ge(sem("s_done"), n * 3 + (c + 1))
                        dve.sem_inc(sem("waits_met"), 1)
                        o = Sb[:, p % 2, CH * c:CH * c + CH]
                        if l == 3:
                            V.tensor_scalar(o, P[c][:, 0:CH], 1.0, None, ALU.mult, ALU.max,
                                            accum_out=mx[:, r, c:c + 1]).then_inc(sem("s_taken"), 1)
                        else:
                            V.tensor_tensor_reduce(o, P[c][:, 0:CH], maskf[:, bi, CH * c:CH * c + CH], 1.0, -3.0e38,
                                                   ALU.add, ALU.max, mx[:, r, c:c + 1]).then_inc(sem("s_taken"), 1)
                    dve.wait_ge(sem("s_taken"), n * 3 + (3 + 3))
                    V.tensor_reduce(nm[:, r:r + 1], mx[:, r, 0:4 if l == 0 else 3], AX.X, ALU.max, negate=True
                                    ).then_inc(sem("nm_ready"), 1)

                def turned(n, p):
                    dve.wait_ge(sem("pv_done"), n + 1)
                    dve.wait_ge(sem("t_done"), n * 3 + (12 + 2))
                    V.tensor_copy(real(PT[0:CT, p % 2, 1, :]), real(P[TURN[1]][0:CT, :])).then_inc(sem("pt_dve"), 1)

                def normalise(B, i, bi):
                    dve.wait_ge(sem("exp_done"), B * 8 + (64 * a + 8))
                    V.tensor_scalar(rinv[:, bi, :], rsum[:, bi, :], 1e-30, None, ALU.max).then_inc(sem("rsum_ok"), 1)
                    dve.wait_ge(sem("rsum_ok"), B + (8 * a + 1))
                    V.reciprocal(rinv[:, bi, :], rinv[:, bi, :]).then_inc(sem("rinv_ok"), 1)
                    dve.wait_ge(sem("rinv_ok"), B + (8 * a + 1))
                    dve.wait_ge(sem("on_psum"), B + (8 * a + 1))
                    for e in range(2):
                        src = P[5][QP * e:QP * e + QP, 0:D].rearrange("q (p c) -> q p c", c=32)[:, :, HD * e:HD * e + HD]
                        dst = onat[QP * bi:QP * bi + QP, bass.ds(i, 1), :].rearrange("q o (p c) -> q (o p) c", c=32)[:, :, HD * e:HD * e + HD]
                        last = V.tensor_tensor(dst, src, rinv[QP * e:QP * e + QP, bi, :].rearrange("q (p o) -> q p o", o=1).broadcast_to([QP, NP, HD]),
                                               ALU.mult)
                    last.then_inc(sem("o_taken"), 1)

                def begin(B, i, bi):
                    queries(B, bi)
                    if l == 0:
                        dve.wait_ge(sem(f"ctx_in{bi}"), i * 16 + 16)
                        V.tensor_reduce(meanT[:, :, bass.ds(B, 1)], ctxT[:, bi], AX.X, ALU.add
                                        ).then_inc(sem("mean_done"), 1)

                def batch(i, bi, more):
                    B = i * 2 + bi
                    n0 = i * 16 + (64 * a + 8 * bi)
                    for p in range(NP - 1):
                        maxima(n0 + (p + 1), B, bi, p + 1)
                        if p == NP - 2 and l < 3:
                            V.memset(flags[:, 100:101], 0.0).then_inc(sem("mask_used"), 1)
                        turned(n0 + p, p)
                    if more:
                        begin(B + 1, i + bi, 1 - bi)
                    turned(n0 + 7, 7)
                    if more:
                        project_values(B + 1, 1 - bi)
                        mask(B + 1, i + bi, 1 - bi)
                        maxima(n0 + 8, B + 1, 1 - bi, 0)
                    normalise(B, i, bi)

                begin(0, 0, 0)
                project_values(0, 0)
                mask(0, 0, 0)
                maxima(64 * a, 0, 0, 0)
                with dve.Fori(0, NB // 2 - 1) as i:
                    batch(i, 0, True)
                    batch(i, 1, True)
                batch(NB // 2 - 1, 0, True)
                batch(NB // 2 - 1, 1, False)
                dve.wait_ge(sem("o_taken"), 8 * (a + 1) + 1)

            def routing(l):
                E, K, U, per = (MOE[l][k] for k in ("E", "K", "U", "per"))

                def L(j):
                    return lg[:, j, :, 0:E]

                def s4(j):
                    return sm[:, j, :]

                dve.wait_ge(sem("logits"), l + 1)
                src = P[7][:, 0:64].rearrange("p (t e) -> p t e", t=TT)[:, :, 0:E]
                if l < 3:
                    step(V.tensor_reduce(s4(8), src, AX.X, ALU.max))
                    V.tensor_tensor(L(1), src, wide(s4(8), E), ALU.subtract).then_inc(sem("lg_ready"), 1)
                    dve.wait_ge(sem("lg_exp"), l + 1)
                    step(V.tensor_reduce(s4(9), L(2), AX.X, ALU.add))
                    step(V.reciprocal(s4(10), s4(9)))
                    step(V.tensor_tensor(L(0), L(2), wide(s4(10), E), ALU.mult))
                else:
                    step(V.tensor_copy(L(0), src))
                    signal("lg_ready")
                for t in range(TT):
                    step(V.max(top8[:, t, :], lg[:, 0, t, 0:E]))
                step(V.tensor_tensor(L(3), L(0), top8[:, :, K - 1:K].broadcast_to([128, TT, E]), ALU.is_gt))
                step(V.tensor_tensor(L(4), L(0), top8[:, :, K - 1:K].broadcast_to([128, TT, E]), ALU.is_equal))
                step(V.tensor_reduce(s4(11), L(3), AX.X, ALU.add))
                step(V.tensor_scalar(s4(12), s4(11), -1.0, float(K), ALU.mult, ALU.add))
                step(V.memset(lg[:, 8, :, :], 1.0))
                for t in range(TT):
                    step(V.tensor_tensor_scan(lg[:, 5, t, 0:E], lg[:, 8, t, 0:E], lg[:, 4, t, 0:E], 0.0, ALU.mult, ALU.add))
                step(V.tensor_tensor(L(6), L(5), wide(s4(12), E), ALU.is_le))
                step(V.tensor_tensor(L(6), L(6), L(4), ALU.mult))
                step(V.tensor_tensor(L(6), L(6), L(3), ALU.add))
                if l == 3:
                    dve.wait_ge(sem("lg_exp"), 4)
                    V.tensor_tensor(L(9), L(6), L(2), ALU.mult).then_inc(sem("cw_ready"), 1)
                    step(V.memset(cw[:, :, :], 1.0))
                    dve.wait_ge(sem("prT_psum"), 1)
                    V.tensor_copy(qT[0:8, 0, :], P[6][0:8, :]).then_inc(sem("prT_sb"), 1)
                    return
                step(V.tensor_tensor(L(9), L(6), L(0), ALU.mult))
                if l in (1, 2):
                    step(V.tensor_reduce(s4(13), L(9), AX.X, ALU.add))
                    step(V.reciprocal(s4(14), s4(13)))
                    step(V.tensor_tensor(L(9), L(9), wide(s4(14), E), ALU.mult))
                    if l == 1:
                        step(V.tensor_scalar(L(9), L(9), K / (K + 1.0), None, ALU.mult))
                step(V.memset(cw[:, :, :], 1.0 / (K + 1.0) if l == 1 else 1.0))
                for r in range(per):
                    dst = cw[:, :, 0:per * E].rearrange("p t (e r) -> p t e r", r=per)[:, :, :, r]
                    last = V.tensor_copy(dst, L(9))
                last.then_inc(sem("cw_ready"), 1)
                dve.wait_ge(sem("cw_ready"), l + 1)

            def mixture(l):
                I, U, base = MOE[l]["I"], MOE[l]["U"], MOE_BASE[l]
                V.memset(acc[:, :, :], 0.0)
                for k in range(2):
                    last = V.memset(act_b[:, k, :].rearrange("p (b q) -> p b q", q=QP)[:, :, NQ:QP], 0.0)
                step(last)
                routing(l)

                def scaled_inputs(u):
                    k = u % 2
                    dve.wait_ge(sem(f"pb_in{k}"), 16 * (u // 2 + 1))
                    V.tensor_tensor(xin[:, k], hT[:, :, :], pb[:, k, :].rearrange("p (o n) -> p o n", o=1).broadcast_to([128, KT, NTOK]),
                                    ALU.mult).then_inc(sem("xin_ready"), 1)

                def gate(k, u):
                    dve.wait_ge(sem("silu_done"), u + (base + 1))
                    dve.wait_ge(sem("gu_done"), u * 2 + (2 * base + 2))
                    dve.wait_ge(sem("down_done"), u + (base + 3))
                    by_batch = lambda y: y.rearrange("p (b q) -> p b q", q=NQ)
                    V.tensor_tensor(real(act_b[0:I, k, :]), by_batch(sg[0:I, k, 0:NB * NQ]), by_batch(P[2 + k][0:I, 0:NB * NQ]), ALU.mult
                                    ).then_inc(sem("act_ready"), 1)

                def accumulate(k, u):
                    dve.wait_ge(sem("down_done"), u + (base + 5))
                    dve.wait_ge(sem("acc_done"), u + (base + 2))
                    for t in range(TT):
                        last = V.scalar_tensor_tensor(acc[:, t, :], P[4 + 2 * k + t // 2][:, D * (t % 2):D * (t % 2) + D],
                                                      cw[:, t, bass.ds(u, 1)], acc[:, t, :], ALU.mult, ALU.add)
                    last.then_inc(sem("acc_done"), 1)

                if l == 3:
                    scaled_inputs(0)
                    scaled_inputs(1)
                    gate(0, 0)
                    for u in range(1, U):
                        if u < U - 2:
                            scaled_inputs(u + 1)
                        gate(u % 2, u)
                        accumulate((u - 1) % 2, u - 1)
                    accumulate((U - 1) % 2, U - 1)
                else:
                    gate(0, 0)
                    with dve.Fori(0, U // 2 - 1) as i:
                        gate(1, i * 2 + 1)
                        accumulate(0, i * 2)
                        gate(0, i * 2 + 2)
                        accumulate(1, i * 2 + 1)
                    gate(1, U - 1)
                    accumulate(0, U - 2)
                    accumulate(1, U - 1)
                dve.wait_ge(sem("acc_done"), base + U + 2)
                residual(4 + l, acc[:, :, :].rearrange("p t d -> p (t d)"))

            def gather_rows():
                step(V.tensor_copy(segf[:, :], seg))
                step(V.tensor_copy(gidx[0:GR, 0, :], gseg[0:GR, :]))
                step(V.tensor_tensor(gidx[0:GR, 0, :], gidx[0:GR, 0, :], gidx[0:GR, 1, :], ALU.subtract))
                step(V.tensor_scalar(gidx[0:GR, 0, :], gidx[0:GR, 0, :], 0.0, NCTX - 1.0, ALU.max, ALU.min))
                step(V.tensor_tensor(gidx[0:GR, 0, :], gidx[0:GR, 0, :], gidx[0:GR, 2, :], ALU.add))
                step(V.memset(grow[:, :], 0))
                V.tensor_copy(grow[0:GR, :], gidx[0:GR, 0, :]).then_inc(sem("rows_ready"), 1)

            def window():
                dve.wait_ge(sem("pre1_psum"), 1)
                for j in range(4):
                    last = V.tensor_copy(wuvo[:, 2 * j:2 * j + 2, :].rearrange("p h n -> p (h n)"), P[2 + j][:, :])
                V.memset(ocT[:, :, :].rearrange("p h (b q) -> p h b q", q=QP)[:, :, :, NQ:QP], 0.0).then_inc(sem("pre1_dve"), 1)
                for hh in range(NH):
                    dve.wait_ge(sem("qh_psum"), hh + 1)
                    dst = qeff[64:128, :, hh, :]
                    b8 = lambda y: y.rearrange("p (b q) -> p b q", b=NB)
                    step(V.tensor_tensor(dst, b8(P[hh % 4][64:128, :]), b8(cosq[64:128, :]), ALU.mult))
                    step(V.tensor_tensor(rope2[64:128, :], P[4 + hh % 4][64:128, :], sinq[64:128, :], ALU.mult))
                    V.tensor_tensor(dst, dst, b8(rope2[64:128, :]), ALU.add).then_inc(sem("qr_taken"), 1)
                by9 = lambda y: y.rearrange("p (t j) -> p t j", j=NW)
                by72 = lambda y: y.rearrange("p (g n) -> p g n", g=NG)

                def take_rows(b):
                    dve.wait_ge(sem("g_turned"), b + 3)
                    V.tensor_copy(gT[:, 1, :], P[1][:, 0:WB]).then_inc(sem("g_dve"), 1)

                def compressed_keys(b, bi):
                    dve.wait_ge(sem("kv_psum"), b + 1)
                    dve.wait_ge(sem("mask1_made"), b + 1)
                    V.tensor_tensor(by9(kvm)[0:R], by9(P[0][0:R, 0:WB]), anyv[0:R, bi, 0, :].rearrange("p (t o) -> p t o", o=1).broadcast_to([R, NQ, NW]),
                                    ALU.mult).then_inc(sem("kvm_made"), 1)
                    dve.wait_ge(sem("kvm_made"), b + 1)
                    V.scalar_tensor_tensor(by9(keff[bi])[0:R], anyv[0:R, bi, 1, :].rearrange("p (t o) -> p t o", o=1).broadcast_to([R, NQ, NW]),
                                           mkv[0:R, bass.ds(b, 1)], by9(kvm)[0:R], ALU.mult, ALU.add).then_inc(sem("kv_sb"), 1)

                def rotations(b):
                    dve.wait_ge(sem("kr_psum"), b + 1)
                    dve.wait_ge(sem("g_act"), b + 1)
                    V.tensor_tensor(prod, P[1][:, 0:WB], csT, ALU.mult).then_inc(sem("prod_sb"), 1)

                def batch(i, bi, more):
                    b = i * 2 + bi
                    bc = lambda y: y.rearrange("p (g o) -> p g o", o=1).broadcast_to([128, NG, GW])

                    def own(k, ins):
                        ins.then_inc(sem("w1_step"), 1)
                        dve.wait_ge(sem("w1_step"), b * 4 + k)

                    dve.wait_ge(sem("s1_psum"), b + 1)
                    own(1, V.tensor_tensor(P1, P[3][:, 0:WB], madd[bi], ALU.add))
                    own(2, V.tensor_reduce(sm1[:, 0, :], by72(P1), AX.X, ALU.max))
                    V.tensor_tensor(by72(P1), by72(P1), bc(sm1[:, 0, :]), ALU.subtract).then_inc(sem("s1_sb"), 1)
                    if more:
                        take_rows(b + 1)
                    dve.wait_ge(sem("e1_sb"), b + 1)
                    own(3, V.tensor_reduce(sm1[:, 1, :], by72(P1), AX.X, ALU.add))
                    own(4, V.reciprocal(sm1[:, 2, :], sm1[:, 1, :]))
                    V.tensor_tensor(by72(P1), by72(P1), bc(sm1[:, 2, :]), ALU.mult).then_inc(sem("p1_sb"), 1)
                    if more:
                        compressed_keys(b + 1, 1 - bi)
                        rotations(b + 1)
                    dve.wait_ge(sem("oc_psum"), b + 1)
                    for e in range(2):
                        for j, m in ((0, 4), (1, 3)):
                            src = P[6 + j][64 * e:64 * e + 64, 0:128 * m].rearrange("p (t h x) -> p h t x", h=8, x=2)[:, :, :, e]
                            last = V.tensor_copy(ocT[64 * e:64 * e + 64, :, bass.ds(b * QP + GT * 4 * j, GT * m)], src)
                    last.then_inc(sem("p1_taken"), 1)

                take_rows(0)
                compressed_keys(0, 0)
                rotations(0)
                with dve.Fori(0, NB // 2 - 1) as i:
                    batch(i, 0, True)
                    batch(i, 1, True)
                batch(NB // 2 - 1, 0, True)
                batch(NB // 2 - 1, 1, False)
                dve.wait_ge(sem("out1_psum"), 1)
                for j in range(2):
                    step(V.tensor_copy(tmp[:, 2 * j:2 * j + 2, :].rearrange("p t d -> p (t d)"), P[j][:, :]))
                residual(1, tmp[:, :, :].rearrange("p t d -> p (t d)"))

            V.memset(x[:, :, :], 0.0).then_inc(sem("x_cleared"), 1)
            V.memset(oTs[:, :, :], 0.0)
            V.memset(mx[:, :, :], -1.0e29).then_inc(sem("s_taken"), 3)
            signal("t_done", 12)
            signal("pv_done", 2)
            signal("proj_done", 18)
            signal("mean_done", 2)
            signal("g_turned", 2)
            signal("mask_used", 2)
            signal("down_done", 4)
            signal("act_ready", 2)
            signal("acc_done", 2)
            signal("pt_act", 2)
            for name in ("v_ready", "pt_dve", "o_taken", "keff_sb"):
                signal(name)
            signal("p1_taken", 2)
            signal("xin_ready", 2)
            dve.wait_ge(sem("const_in"), 16 * 15)
            gather_rows()
            fake_quantise(w2n).then_inc(sem("w2n_ready"), 1)
            dve.wait_ge(sem("w2T_psum"), 1)
            for m in range(2):
                step(V.tensor_copy(w2T[:, 2 * m:2 * m + 2, :].rearrange("p k d -> p (k d)"), P[m][:, :]))
            dve.wait_ge(sem("x_in"), 16 * NB)

            for s in range(NSUB):
                l = s // 2
                layer_norm()
                if s == 0:
                    for t in range(TT):
                        step(V.tensor_tensor_reduce(tmp[:, t, :], h[:, t, :], h[:, t, :], 1.0, 0.0, ALU.mult, ALU.add,
                                                    sm[:, 3, t:t + 1]))
                    step(V.tensor_scalar(sm[:, 0, :], sm[:, 3, :], 1.0 / D, 1e-6, ALU.mult, ALU.add))
                    inverse_root()
                    step(V.tensor_tensor(h[:, :, :], h[:, :, :], wide(sm[:, 2, :], D), ALU.mult))
                if s == 4:
                    step(fake_quantise(h))
                signal("h_ready")
                transposed(hT, cols[:, 1:2] if s == 0 else None)
                if s % 2:
                    mixture(l)
                    continue
                if l == 1:
                    window()
                    continue
                a = ATT[l]
                if l == 3:
                    dve.wait_ge(sem("ref_psum"), 1)
                    for j in range(2):
                        step(V.tensor_copy(tmp[:, 2 * j:2 * j + 2, :].rearrange("p t d -> p (t d)"), P[2 + j][:, :]))
                    signal("ref_sb")
                dve.wait_ge(sem("q_psum"), a + 1)
                for o in range(KT):
                    if l == 0:
                        step(V.tensor_scalar(qT[:, o, :], P[o][:, :], 0.25, None, ALU.mult))
                    else:
                        col = (2 if l == 2 else 8) + o
                        step(V.tensor_scalar(qT[:, o, :], P[o][:, :], cols[:, col:col + 1], 0.25, ALU.add, ALU.mult))
                signal("q_sb")
                attention(l)
                flat = tmp[:, :, :].rearrange("p t d -> p (t d)")
                row = lambda r: rows[:, r, :].rearrange("p (o d) -> p o d", o=1).broadcast_to([128, TT, D])
                if l == 0:
                    signal("o_ready")
                    transposed(oT)
                    for j in range(2):
                        dve.wait_ge(sem("gate_ready"), j + 1)
                        step(V.tensor_tensor(tmp[:, 2 * j:2 * j + 2, :].rearrange("p t d -> p (t d)"),
                                             tmp[:, 2 * j:2 * j + 2, :].rearrange("p t d -> p (t d)"), P[j][:, :], ALU.mult))
                    dve.wait_ge(sem("tg_ready"), 1)
                    residual(0, flat)
                if l == 2:
                    step(V.tensor_tensor(onat[:, :, :], onat[:, :, :], row(0), ALU.add))
                    fake_quantise(onat).then_inc(sem("o_ready"), 1)
                    transposed(oT)
                    dve.wait_ge(sem("out_psum"), 2)
                    for j in range(2):
                        step(V.tensor_tensor(tmp[:, 2 * j:2 * j + 2, :], P[j][:, :].rearrange("p (t d) -> p t d", t=2),
                                             rows[:, 1, :].rearrange("p (o d) -> p o d", o=1).broadcast_to([128, 2, D]), ALU.add))
                    residual(2, flat)
                if l == 3:
                    step(V.tensor_tensor(tmp[:, :, :], tmp[:, :, :], onat[:, :, :], ALU.add))
                    step(V.tensor_tensor(tmp[:, :, :], tmp[:, :, :], row(2), ALU.add))
                    residual(3, flat)


def _consts():
    c = {}
    c["ident"] = np.eye(128, dtype=np.float32)
    c["turned_ident"] = np.roll(c["ident"], 64, axis=1)
    c["headmask"] = (np.arange(128)[:, None] // HD == np.arange(NP)[None, :]).astype(np.float32)
    half = R // 2
    inv_freq = (1.0 / 10000.0 ** (np.arange(half, dtype=np.float32) / np.float32(half))).astype(np.float32)
    ang = np.arange(NCTX, dtype=np.float32)[:, None] * inv_freq
    cos, sin = np.cos(ang).astype(np.float32), np.sin(ang).astype(np.float32)
    c["rope"] = np.concatenate([cos, cos, -sin, sin], axis=1)
    q = np.zeros((NTOK, 128), np.float32)
    for b in range(NB):
        q[QP * b:QP * b + NQ] = c["rope"][0:NQ]
    c["cosq"], c["sinq"] = np.ascontiguousarray(q[:, 0:R].T), np.ascontiguousarray(q[:, R:2 * R].T)
    p = np.arange(128)[:, None] // NH
    c["blk"] = np.where(np.arange(GW)[None, :] // NW == p, 0.0, 3 * NEG).astype(np.float32)
    c["jrow"] = np.arange(NW, dtype=np.float32)
    c["wstk"] = np.concatenate([np.eye(R), np.eye(R)]).astype(np.float32)
    j = np.tile((np.arange(GR) % NW).astype(np.float32)[:, None], (1, NB * NGT))
    first = np.tile((np.arange(NB * NGT) // NGT * NCTX).astype(np.float32)[None, :], (GR, 1))
    c["gconst"] = np.stack([j, first], axis=1)
    return c


def _io(w):
    return w.reshape(-1, 128, w.shape[1]).transpose(1, 0, 2)


def kernel(**inputs):
    import concourse.bacc as bacc
    from concourse.bass_utils import run_bass_kernel_spmd as run
    a = {k: np.asarray(v) for k, v in inputs.items()}
    c = _consts()
    m = {k: c[k] for k in ("ident", "turned_ident", "headmask", "cosq", "sinq", "blk", "jrow", "wstk", "gconst")}
    m["x"] = a["x"]
    ctx = a["ctx_2048"]
    m["ctxT"] = ctx.transpose(0, 2, 1).reshape(NB, KT, 128, NCTX).transpose(0, 2, 1, 3)
    m["ctxrows"] = np.concatenate([ctx.reshape(NB * NCTX, D), np.tile(c["rope"], (NB, 1))], axis=1)
    m["mask0"] = a["mask_BxS2_bk0"].view(np.int32)
    m["mask2"] = a["mask_BxSxS2_ff0"]
    seg = a["itok_BxS_0_1023"]
    m["seg"] = seg.reshape(-1)
    m["gseg"] = np.repeat(seg.reshape(NB, NGT, GR // NW), NW, axis=2).reshape(NB * NGT, GR).T
    m["gates"] = np.concatenate([a["g_xattn"], a["g_ffn"]])
    zero = np.zeros(D, np.float32)
    m["rows"] = np.stack([a["L2_xattn_bv"], a["L2_xattn_bo"], a["L3_xattn_b_v"]])
    m["cols"] = np.concatenate([v.reshape(KT, 128).T for v in (
        a["L0_xattn_norm_w"], a["L2_xattn_bq"], a["L2_xattn_bk"], a["L3_xattn_b_fc"], a["L3_xattn_b_q"],
        a["L3_xattn_b_k"], zero, zero)], axis=1)
    m["w0"] = np.stack([_io(a["L0_xattn_" + n].T) for n in ("wq", "wk", "wv", "wo", "wg")], axis=1)
    m["w2"] = np.stack([_io(a["L2_xattn_" + n].T) for n in ("wk", "wv")], axis=1)
    m["w2n"] = np.concatenate([_io(a["L2_xattn_" + n]) for n in ("wq", "wo")], axis=1)
    m["w3"] = np.stack([_io(a["L3_xattn_W_fc"].T), _io(a["L3_xattn_W_q"].T), _io(a["L3_xattn_W_k"].T),
                        _io(a["L3_xattn_W_v"].reshape(D, D).T)], axis=1)
    gate = [a["L0_ffn_gate_w"].T, a["L1_ffn_w_router"], a["L2_ffn_router_gate"].T, a["L3_ffn_router_w"]]
    m["gw"] = np.stack([np.pad(_io(g), ((0, 0), (0, 0), (0, 16 - g.shape[1]))) for g in gate], axis=1)

    def heads(w, n):
        return w.reshape(w.shape[0], NH, n)

    m["wuqT"] = heads(a["L1_xattn_W_uq"], HDL).transpose(2, 1, 0)
    m["wukT"] = heads(a["L1_xattn_W_uk"], HDL).transpose(2, 1, 0)
    m["wuvT"] = heads(a["L1_xattn_W_uv"], HDL).transpose(2, 1, 0)
    qr = heads(a["L1_xattn_W_qr"], R)
    m["wqr"] = qr
    m["wqr2"] = np.concatenate([qr[:, :, R // 2:], qr[:, :, :R // 2]], axis=2)
    m["wdq"] = _io(a["L1_xattn_W_dq"])
    m["wkvc"] = _io(a["L1_xattn_W_kvc"])
    kr = a["L1_xattn_W_kr"]
    m["wkr"] = np.concatenate([kr, kr[:, R // 2:], kr[:, :R // 2]], axis=1)
    m["wo1"] = a["L1_xattn_W_o"].reshape(NH, HDL, D).transpose(1, 0, 2)

    def ups(gate_w, up_w):
        w = np.concatenate([gate_w, up_w], axis=2)
        return w.reshape(len(w), KT, 128, -1).transpose(0, 2, 1, 3)

    def cut(w, n):
        return w.reshape(w.shape[0], D, n, -1).transpose(0, 2, 1, 3).reshape(w.shape[0] * n, D, -1)

    w1, s1 = a["L0_ffn_w1"].transpose(0, 2, 1), a["L0_ffn_shared_w1"].T[None]
    m["up0"] = np.concatenate([ups(cut(w1[:, :, :176], 2), cut(w1[:, :, 176:], 2)),
                               ups(cut(s1[:, :, :352], 4), cut(s1[:, :, 352:], 4))])
    m["down0"] = np.concatenate([a["L0_ffn_w2"].transpose(0, 2, 1).reshape(32, 88, D),
                                 a["L0_ffn_shared_w2"].T.reshape(4, 88, D)])
    m["up0"] = np.pad(m["up0"].reshape(36, 128, KT, 2, 88), ((0, 0),) * 4 + ((0, 8),)).reshape(36, 128, KT, 192)
    m["down0"] = np.pad(m["down0"], ((0, 0), (0, 8), (0, 0)))
    m["up1"] = np.concatenate([ups(a["L1_ffn_we1"], a["L1_ffn_we3"]),
                               ups(cut(a["L1_ffn_ws1"][None], 4), cut(a["L1_ffn_ws3"][None], 4))])
    m["down1"] = np.concatenate([a["L1_ffn_we2"], a["L1_ffn_ws2"].reshape(4, 128, D)])
    gu = a["L2_ffn_expert_gate_up"]
    m["up2"], m["down2"] = ups(gu[:, :, 0::2], gu[:, :, 1::2]), a["L2_ffn_expert_down"]
    gu = a["L3_ffn_gate_up_w"]
    m["up3"] = np.concatenate([ups(gu[:, :, :128], gu[:, :, 128:]),
                               ups(a["L3_ffn_shared_gate_w"][None], a["L3_ffn_shared_up_w"][None])])
    m["down3"] = np.concatenate([a["L3_ffn_down_w"], a["L3_ffn_shared_down_w"][None]])

    nc = bacc.Bacc("TRN2", target_bir_lowering=False, num_devices=1)
    arrays = {f"in_{k}": np.ascontiguousarray(w) for k, w in m.items()}
    A = {k[3:]: nc.dram_tensor(k, w.shape, mybir.dt.from_np(w.dtype), kind="ExternalInput").ap()
         for k, w in arrays.items()}
    A["prT"] = nc.dram_tensor("prT", (8, NTOK), mybir.dt.float32, kind="Internal").ap()
    out = nc.dram_tensor("out_x", (NB, NQ, D), mybir.dt.float32, kind="ExternalOutput").ap()
    flamingo_kernel(nc, A, out)
    r = run(nc, [arrays], core_ids=[0])
    return r.results[0]["out_x"]
```

```python
import numpy as np
from contextlib import ExitStack
import concourse.bass as bass
from concourse import mybir

NSUB = 8

NB, NQ, QP = 8, 56, 64
TT, D, KT = 4, 256, 2
NTOK = NB * QP
PR = 2 * NQ
NCTX, CH, NCH = 1500, 500, 3
CT, NCT = 125, 12
NH, NP, HD = 16, 8, 16
NEG = -1.0e30

MOE = [dict(I=96, U=36, E=16, K=6, per=2), dict(I=128, U=20, E=16, K=4, per=1),
       dict(I=128, U=8, E=8, K=2, per=1), dict(I=128, U=9, E=8, K=2, per=1)]
MOE_BASE = [0, 36, 56, 64]

LOOK, NW = 8, 9
GT, NG = 8, 7
GW = GT * NW
WB = NQ * NW
GR, NGT = 126, 4
R, QC, HDL = 64, 96, 128
SCALE1 = float(1.0 / np.sqrt(192.0).astype(np.float32))


def flamingo_kernel(nc, A, out):
    F32, I32, U8, F32R = mybir.dt.float32, mybir.dt.int32, mybir.dt.uint8, mybir.dt.float32r
    U32 = mybir.dt.uint32
    ALU, ACT, AX = mybir.AluOpType, mybir.ActivationFunctionType, mybir.AxisListType
    ctx = ExitStack()
    with ctx:
        def sb(name, shape, dt=F32):
            return ctx.enter_context(nc.sbuf_tensor(name, shape, dt))

        sems = {}

        def sem(name):
            if name not in sems:
                sems[name] = ctx.enter_context(nc.semaphore(name))
            return sems[name]

        x = sb("x", [128, TT, D])
        h = sb("h", [128, TT, D])
        onat = sb("onat", [128, TT, D])
        acc = onat
        tmp = sb("tmp", [128, TT, D])
        hT = sb("hT", [128, KT, NTOK])
        qT = sb("qT", [128, KT, NTOK])
        oT = sb("oT", [128, KT, NTOK])
        ident = sb("ident", [128, 128])
        turned_ident = sb("turned_ident", [128, 128])
        spread = sb("spread", [PR, 128])
        headmask = sb("headmask", [128, 2, NP])
        tg = sb("tg", [128, 8])
        stats = sb("stats", [128, TT, 6])
        mv = sb("mv", [128, TT, 2])
        sm = sb("sm", [128, 16, TT])
        cols = sb("cols", [128, 16])
        rows = sb("rows", [128, 3, D])
        lg = sb("lg", [128, 10, TT, 16])
        top8 = sb("top8", [128, TT, 8])
        cw = sb("cw", [128, TT, 36])
        w0 = sb("w0", [128, 5, KT, D])
        w2 = tmp[:, :, :].rearrange("p (m k) d -> p m k d", m=2)
        w2n = onat
        w2T = sb("w2T", [128, 4, D])
        w3 = w0[:, 0:4]
        gw = sb("gw", [128, 4, KT, 16])
        same_place = ctx.enter_context(ExitStack())
        K2 = same_place.enter_context(nc.sbuf_tensor("K2", [128, KT, NCTX], F32R))
        same_place.close()
        wu = sb("wu", [128, 4, KT, 2 * 128])
        wd = sb("wd", [128, 4, D])

        ws = sb("ws", [128, 3, 2, KT, D], F32R)
        SUP = same_place.enter_context(nc.sbuf_tensor("SUP", [128, 2, KT, NCTX], F32R))
        C = same_place.enter_context(nc.sbuf_tensor("C", [128, 2, KT, NCTX], F32R))
        K = same_place.enter_context(nc.sbuf_tensor("K", [128, 2, KT, NCTX], F32R))
        Qb = same_place.enter_context(nc.sbuf_tensor("Qb", [128, 2, KT, 8 * QP], F32R))
        same_place.close()
        maskf = same_place.enter_context(nc.sbuf_tensor("maskf", [128, 2, NCTX], F32))
        maskraw = same_place.enter_context(nc.sbuf_tensor("maskraw", [128, 2, NCTX // 4], I32))
        same_place.close()
        same_place.enter_context(nc.sbuf_tensor("below_queries", [128, 6 * KT * NCTX], F32))
        wus_b = same_place.enter_context(nc.sbuf_tensor("wus_b", [128, 2, 2, KT, 2 * 128], F32R))
        same_place.close()
        win = sb("win", [128, 3 * 2 * KT * NCTX + 2 * KT * 8 * QP])
        same_place.enter_context(nc.sbuf_tensor("below_mixture", [128, KT * NCTX], F32))
        mix = lambda name, shape, dt: same_place.enter_context(nc.sbuf_tensor(name, shape, dt))
        hs = mix("hs", [128, 2, KT, NB * NQ], F32R)
        act_b = mix("act_b", [128, 2, 2, NTOK], F32R)
        wus_a = mix("wus_a", [128, 2, 2, KT, 2 * 128], F32R)
        wds = mix("wds", [128, 2, 2, D], F32R)
        sg = mix("sg", [128, 2, NB * NQ], F32)
        pb = mix("pb", [128, 2, NB * NQ], F32)
        same_place.close()
        area = sb("area", [128, KT * NCTX + 2 * NCTX + 2 * NCH * 512])
        v = sb("v", [128, NCT, D])
        qT2 = area[:, 4 * NCTX:4 * NCTX + KT * NTOK].rearrange("p (k n) -> p k n", k=KT)
        ctxT = area[:, 0:KT * NCTX].rearrange("p (k n) -> p k n", k=KT)
        Sb = area[:, 2 * NCTX:4 * NCTX].rearrange("p (r n) -> p r n", r=2)
        PT = area[:, 4 * NCTX:].rearrange("p (r g n) -> p r g n", r=2, g=NCH)
        qlo = oT
        sup_f = h[:, :, :].rearrange("p t d -> p (t d)")[:, 0:2 * CH].rearrange("p (r n) -> p r n", r=2)
        mx = sb("mx", [128, 4, 4])
        nm = sb("nm", [128, 4])
        rsum = sb("rsum", [128, 2, NP])
        rinv = sb("rinv", [128, 2, NP])
        factors = sb("factors", [128, NP])
        oTs = sb("oTs", [128, 2, D])

        meanT = sb("meanT", [128, KT, NB])
        segf = sb("segf", [128, NB * NQ])
        seg = qT[:, 0, 0:NB * NQ].bitcast(I32)
        gidx = sb("gidx", [128, 3, NB * NGT])
        gseg = sb("gseg", [128, NB * NGT], I32)
        grow = sb("grow", [128, NB * NGT], I32)
        grow4 = sb("grow4", [128, 2, NGT], I32)
        anyv = sb("anyv", [128, 2, 2, NQ])
        sm1 = sb("sm1", [128, 4, NG])
        flags = sb("flags", [128, 104])
        mkv = sb("mkv", [128, NB])

        kflat = win[:, 0:6000]
        wuqT = kflat[:, 0:1536].rearrange("p (h n) -> p h n", h=16)
        wukT = kflat[:, 1536:2560].rearrange("p (h n) -> p h n", h=16)
        wuvT = kflat[:, 2560:3584].rearrange("p (h n) -> p h n", h=16)
        wqr2 = kflat[0:QC, 3584:4608].rearrange("p (h n) -> p h n", h=16)
        wdq = kflat[:, 4608:4800].rearrange("p (k n) -> p k n", k=2)
        wkvc = kflat[:, 4800:4928].rearrange("p (k n) -> p k n", k=2)
        wkr = kflat[0:R, 4928:5056]
        wstk = kflat[:, 5056:5120]
        blk = kflat[:, 5120:5192]
        jrow = kflat[:, 5192:5201]
        kvm = kflat[:, 5201:5705]
        wo1 = win[:, 6000:10096].rearrange("p (h n) -> p h n", h=16)
        ocT = win[:, 6000:10096].rearrange("p (h n) -> p h n", h=8)
        wcomb = win[0:QC, 10096:12144].rearrange("p (h n) -> p h n", h=16)
        wuvo = win[:, 12144:14192].rearrange("p (h n) -> p h n", h=8)
        qcT = win[0:QC, 14192:14704]
        G = win[0:GR, 14704:17776].rearrange("p (a t n) -> p a t n", a=2, t=NGT)
        qb1 = [win[:, 17776 + 1024 * j:18800 + 1024 * j].rearrange("p (q h) -> p q h", h=16) for j in range(2)]
        sflat = v[:, :, :].rearrange("p j d -> p (j d)")
        gT = sflat[:, 0:1008].rearrange("p (k n) -> p k n", k=2)
        csT, prod, P1 = sflat[:, 1008:1512], sflat[:, 1512:2016], sflat[:, 2016:2520]
        qeff = area[:, 0:8192].rearrange("p (b h q) -> p b h q", b=NB, h=16)
        madd = [area[:, 8192:8192 + WB], sflat[:, 2520:2520 + WB]]
        kvn = [y[0:GW].rearrange("p k n -> p (k n)")[:, 0:896].rearrange("p (g c) -> p g c", g=NG)
               for y in (oT[:, :, :], h[:, :, :])]
        PT1 = qT[0:GW, :, :].rearrange("p k n -> p (k n)")[:, 0:896].rearrange("p (g c) -> p g c", g=NG)
        aflat = acc[:, :, :].rearrange("p t d -> p (t d)")
        kid, valid = aflat[:, 0:504], aflat[:, 504:1008]
        cosq = tmp[:, 0:2, :].rearrange("p t d -> p (t d)")
        sinq = tmp[:, 2:4, :].rearrange("p t d -> p (t d)")
        rope2 = h[:, 0:2, :].rearrange("p t d -> p (t d)")
        tflat = tmp[:, :, :].rearrange("p t d -> p (t d)")
        keff = [tflat[:, WB * j:WB * j + WB] for j in range(2)]

        wus = [wus_a[:, 0], wus_a[:, 1], wus_b[:, 0], wus_b[:, 1]]
        P = [ctx.enter_context(nc.psum_tensor(f"P{i}", [128, 512], F32)) for i in range(8)]

        block = ctx.enter_context(nc.Block())

        def real(y):
            return y.rearrange("p (b q) -> p b q", q=QP)[:, :, 0:NQ]

        ATT = {0: 0, 2: 1, 3: 2}
        NPROJ = {0: 12, 2: 12, 3: 18}
        PB = (0, 1, 2, 7)
        QBANK = {0: (6, 7), 2: (6, 7), 3: (6, 3)}
        FIRST = 6
        TURN = (3, 4, 6)

        @block.gpsimd
        def _(pool):
            def split_weights(m, src):
                split_count[0] += 1
                pool.wait_ge(sem("ws_lead"), split_count[0])
                nc.gpsimd.tensor_tensor(ws[:, m, 1, :, :], src, ws[:, m, 0, :, :].bitcast(F32), ALU.subtract
                                        ).then_inc(sem("ws_split"), 1)

            split_count = [0]

            def context_rest(l, b, pieces=range(4)):
                for j in pieces:
                    pool.wait_ge(sem("ctx_hi"), b * 4 + (32 * ATT[l] + j + 1))
                    pool.sem_inc(sem("waits_met"), 1)
                    o, c0 = j // 2, NCTX // 2 * (j % 2)
                    nc.gpsimd.tensor_tensor(C[:, 1, o, c0:c0 + NCTX // 2], ctxT[:, o, c0:c0 + NCTX // 2],
                                            C[:, 0, o, c0:c0 + NCTX // 2].bitcast(F32), ALU.subtract).then_inc(sem("ctx_lo"), 1)

            def queries(l, b):
                if isinstance(b, int):
                    pool.wait_ge(sem("qlo_sb"), ATT[l] + 1)
                else:
                    pool.wait_ge(sem("s_done"), b * 24 + 192 * ATT[l])
                pool.sem_inc(sem("waits_met"), 1)
                for k in range(KT):
                    for e, src in enumerate((qT, qlo)):
                        nc.gpsimd.tensor_tensor(Qb[:, e, k, 0:8 * NQ].rearrange("p (e q) -> p e q", e=8),
                                                src[:, k, bass.ds(b * QP, NQ)].rearrange("p (o q) -> p o q", o=1).broadcast_to([128, 8, NQ]),
                                                headmask[:, e, :].rearrange("p (e o) -> p e o", o=1).broadcast_to([128, 8, NQ]),
                                                ALU.mult).then_inc(sem("qb_ready"), 1)
                pool.wait_ge(sem("qb_ready"), b * 6 + (48 * ATT[l] + 4))
                pool.sem_inc(sem("waits_met"), 1)
                for k in range(KT):
                    nc.gpsimd.tensor_tensor(Qb[:, 1, k, 0:8 * NQ], Qb[:, 0, k, 0:8 * NQ].bitcast(F32), Qb[:, 1, k, 0:8 * NQ].bitcast(F32),
                                            ALU.add).then_inc(sem("qb_ready"), 1)

            def support_rest(b):
                for g in range(FIRST):
                    pool.wait_ge(sem("k_lo"), b * 12 + (96 + g + 1))
                    pool.sem_inc(sem("waits_met"), 1)
                    o, c = g // NCH, g % NCH
                    nc.gpsimd.tensor_tensor(SUP[:, 1, o, CH * c:CH * c + CH], sup_f[:, g % 2, :],
                                            SUP[:, 0, o, CH * c:CH * c + CH].bitcast(F32), ALU.subtract).then_inc(sem("sup_lo"), 1)

            def up_rest(l, q, u):
                I, base = MOE[l]["I"], MOE_BASE[l]
                pool.wait_ge(sem("up_lead"), u + (base + 1))
                pool.sem_inc(sem("waits_met"), 1)
                nc.gpsimd.tensor_tensor(wus[q][:, 1, :, 0:2 * I], wu[:, q, :, 0:2 * I], wus[q][:, 0, :, 0:2 * I].bitcast(F32),
                                        ALU.subtract).then_inc(sem("up_split"), 1)

            def down_rest(l, q, u):
                I, base = MOE[l]["I"], MOE_BASE[l]
                pool.wait_ge(sem("down_lead"), u + (base + 1))
                pool.sem_inc(sem("waits_met"), 1)
                nc.gpsimd.tensor_tensor(wds[0:I, q % 2, 1, :], wd[0:I, q, :], wds[0:I, q % 2, 0, :].bitcast(F32),
                                        ALU.subtract).then_inc(sem("down_split"), 1)

            def first_units(l):
                for u in range(2):
                    up_rest(l, u, u)

            def one_unit(l, u):
                if u + 2 < MOE[l]["U"]:
                    up_rest(l, (u + 2) % 4, u + 2)
                down_rest(l, u % 4, u)

            def other_units(l):
                U = MOE[l]["U"]
                for u in range(4):
                    one_unit(l, u)
                    if l == 1 and u in (1, 2):
                        split_weights(u - 1, w2[:, u - 1])
                    if l == 2 and u < 3 and NSUB > 6:
                        split_weights((2, 0, 1)[u], w3[:, (0, 2, 3)[u]])
                if U > 12:
                    with pool.Fori(1, U // 4 - 1) as i:
                        for q in range(4):
                            up_rest(l, (q + 2) % 4, i * 4 + (q + 2))
                            down_rest(l, q, i * 4 + q)
                for u in range(U // 4 * 4 - 4, U):
                    one_unit(l, u)
                    if l in (1, 2) and NSUB > 2 * l + 2:
                        context_rest(l + 1, 0, (u % 4,))

            split_weights(0, w0[:, 1])
            split_weights(1, w0[:, 2])
            context_rest(0, 0)
            queries(0, 0)
            with pool.Fori(1, NB) as b:
                context_rest(0, b)
                queries(0, b)
            if NSUB > 1:
                first_units(0)
                other_units(0)
            pool.wait_ge(sem("rows_ready"), 1)
            pool.wait_ge(sem("w1_in"), 16 * 15)
            pool.wait_ge(sem("sub_done"), 2)

            def masks(b, bi):
                by9 = lambda y: y.rearrange("p (t j) -> p t j", j=NW)
                by72 = lambda y: y.rearrange("p (g n) -> p g n", g=NG)
                G_ = nc.gpsimd

                def step(k, ins):
                    ins.then_inc(sem("mask1_step"), 1)
                    pool.wait_ge(sem("mask1_step"), b * 7 + k)
                    pool.sem_inc(sem("waits_met"), 1)

                pool.wait_ge(sem("s1_sb"), b + 1)
                pool.sem_inc(sem("waits_met"), 1)
                step(1, G_.tensor_tensor(by9(kid), segf[:, bass.ds(b * NQ, NQ)].rearrange("p (t o) -> p t o", o=1).broadcast_to([128, NQ, NW]),
                                         jrow.rearrange("p (o j) -> p o j", o=1).broadcast_to([128, NQ, NW]), ALU.subtract))
                step(2, G_.tensor_scalar(valid, kid, -0.5, None, ALU.is_gt))
                step(3, G_.tensor_scalar(kid, kid, NCTX - 0.5, None, ALU.is_lt))
                step(4, G_.tensor_tensor(anyv[:, bi, 0, :], by9(valid)[:, :, 0], by9(kid)[:, :, NW - 1], ALU.mult))
                step(5, G_.tensor_tensor(valid, kid, valid, ALU.mult))
                step(6, G_.tensor_scalar(madd[bi], valid, -NEG, NEG, ALU.mult, ALU.add))
                step(7, G_.tensor_tensor(by72(madd[bi]), by72(madd[bi]), blk.rearrange("p (o n) -> p o n", o=1).broadcast_to([128, NG, GW]),
                                         ALU.add))
                G_.tensor_scalar(anyv[:, bi, 1, :], anyv[:, bi, 0, :], -1.0, 1.0, ALU.mult, ALU.add).then_inc(sem("mask1_made"), 1)

            with pool.Fori(0, NB // 2) as i:
                for bi in range(2):
                    b = i * 2 + bi
                    pool.wait_ge(sem("g_turned"), b + 1)
                    nc.gpsimd.tensor_copy(grow4[:, bi, :], grow[:, bass.ds(i * 8 + 4 * bi, NGT)]).then_inc(sem("row_copied"), 1)
                    pool.wait_ge(sem("row_copied"), b + 1)
                    pool.sem_inc(sem("waits_met"), 1)
                    for t in range(NGT):
                        pool.indirect_dma_start(out=G[:, bi, t, :], out_offset=None, in_=A["ctxrows"],
                                                in_offset=bass.IndirectOffsetOnAxis(
                                                    ap=grow4[0:GR, bi, t:t + 1].bitcast(U32), axis=0)
                                                ).then_inc(sem(f"g_in{bi}"), 16)
                    masks(b, bi)
            if NSUB > 3:
                pool.wait_ge(sem("sub_done"), 3)
                pool.dma_start(w2, A["w2"]).then_inc(sem("w2_in"), 16)
                first_units(1)
                other_units(1)
            if NSUB > 4:
                queries(2, 0)
                with pool.Fori(1, NB) as b:
                    context_rest(2, b)
                    queries(2, b)
            if NSUB > 5:
                first_units(2)
                other_units(2)
            if NSUB > 6:
                support_rest(0)
                queries(3, 0)
                with pool.Fori(1, NB) as b:
                    context_rest(3, b)
                    support_rest(b)
                    queries(3, b)
            if NSUB > 7:
                first_units(3)
                other_units(3)

        @block.sync
        def _(sp):
            def load_context(l, b):
                a = ATT[l]
                sp.wait_ge(sem("ctx_lo"), b * 4 + (32 * a + 4))
                sp.sem_inc(sem("waits_met"), 1)
                if l == 0:
                    sp.wait_ge(sem("mean_done"), b * 2 + 2)
                    sp.sem_inc(sem("waits_met"), 1)
                sp.dma_start(ctxT, A["ctxT"][b]).then_inc(sem("ctx_in"), 16)

            sp.dma_start(w0[:, 1:3, :, :], A["w0"][:, 1:3]).then_inc(sem("wkv_in"), 16)
            sp.dma_start(ctxT, A["ctxT"][0]).then_inc(sem("ctx_in"), 16)
            sp.wait_ge(sem("x_cleared"), 1)
            for b in range(NB):
                sp.dma_start(x[QP * (b % 2):QP * (b % 2) + NQ, b // 2, :], A["x"][b]).then_inc(sem("x_in"), 16)
            for dst, name in ((ident[:, :], "ident"), (turned_ident[:, :], "turned_ident"), (spread[:, :], "spread"), (headmask[:, :, :], "headmask"), (cols[:, :], "cols"),
                              (w2n[:, :, :], "w2n"), (gw[:, :, :, :], "gw")):
                sp.dma_start(dst, A[name]).then_inc(sem("const_in"), 16)
            for m in (0, 3, 4):
                sp.dma_start(w0[:, m, :, :], A["w0"][:, m]).then_inc(sem("const_in"), 16)
            sp.dma_start(tg[:, :], A["gates"].partition_broadcast(128)).then_inc(sem("const_in"), 16)
            sp.dma_start(seg, A["seg"].partition_broadcast(128)).then_inc(sem("const_in"), 16)
            sp.dma_start(gseg[0:GR, :], A["gseg"]).then_inc(sem("const_in"), 16)
            sp.dma_start(gidx[0:GR, 1:3, :], A["gconst"]).then_inc(sem("const_in"), 16)
            for r in range(3):
                sp.dma_start(rows[:, r, :], A["rows"][r].partition_broadcast(128)).then_inc(sem("const_in"), 16)

            def attention_loads(l):
                def load_mask(i, bi):
                    b = i * 2 + bi
                    if l == 0:
                        sp.wait_ge(sem("mask_used"), b + 1)
                        sp.sem_inc(sem("waits_met"), 1)
                        sp.dma_start(maskraw[:, bi, :], A["mask0"][b].partition_broadcast(128)).then_inc(sem(f"mask_in{bi}"), 16)
                    if l == 2:
                        sp.wait_ge(sem("mask_used"), b + (8 + 1))
                        sp.sem_inc(sem("waits_met"), 1)
                        for half in range(2):
                            sp.dma_start(maskf[NQ * half:NQ * half + NQ, bi, :], A["mask2"][b]).then_inc(sem(f"mask_in{bi}"), 16)

                load_mask(0, 0)
                load_context(l, 1)
                load_mask(0, 1)
                with sp.Fori(1, NB // 2) as i:
                    for bi in range(2):
                        load_context(l, i * 2 + bi)
                        load_mask(i, bi)

            def mixture_loads(l):
                s = 2 * l + 1
                I, U, base = MOE[l]["I"], MOE[l]["U"], MOE_BASE[l]

                def unit(q, u):
                    sp.wait_ge(sem("down_split"), u + (base + 1))
                    sp.sem_inc(sem("waits_met"), 1)
                    sp.dma_start(wu[:, q, :, 0:2 * I], A[f"up{l}"][u]).then_inc(sem(f"w_in{q}"), 16)
                    sp.dma_start(wd[0:I, q, :], A[f"down{l}"][u]).then_inc(sem(f"w_in{q}"), 16)

                def probabilities(u):
                    sp.wait_ge(sem("pb_used"), u)
                    sp.dma_start(pb[:, u % 2, :].rearrange("p (b q) -> p b q", q=NQ),
                                 A["prT"][u - 1].rearrange("(b q) -> b q", q=QP)[:, 0:NQ].partition_broadcast(128)
                                 ).then_inc(sem(f"pb_in{u % 2}"), 16)

                sp.wait_ge(sem("sub_done"), 2 * l + 1)
                for q in range(4):
                    unit(q, q)
                if s + 1 < NSUB and l + 1 in ATT:
                    load_context(l + 1, 0)
                if l == 0:
                    for dst, name in ((wuqT, "wuqT"), (wukT, "wukT"), (wuvT, "wuvT"), (wqr2, "wqr2"), (wdq, "wdq"),
                                      (wkvc, "wkvc"), (wkr, "wkr"), (wstk, "wstk"), (blk, "blk"), (wo1, "wo1"),
                                      (wcomb[:, :, 64:128], "wqr"), (cosq[64:128, :], "cosq"), (sinq[64:128, :], "sinq")):
                        sp.dma_start(dst, A[name]).then_inc(sem("w1_in"), 16)
                    sp.dma_start(w3, A["w3"]).then_inc(sem("w1_in"), 16)
                    sp.dma_start(jrow, A["jrow"].partition_broadcast(128)).then_inc(sem("w1_in"), 16)
                if l == 3:
                    sp.wait_ge(sem("prT_sb"), 1)
                    sp.dma_start(A["prT"], qT[0:8, 0, :]).then_inc(sem("prT_out"), 16)
                    sp.wait_ge(sem("prT_out"), 16)
                    for u in range(1, U):
                        probabilities(u)
                        if 2 <= u < U - 2:
                            unit((u + 2) % 4, u + 2)
                    return
                with sp.Fori(1, U // 4) as i:
                    for q in range(4):
                        unit(q, i * 4 + q)

            for s in range(NSUB):
                l = s // 2
                if s % 2 == 0 and l in ATT:
                    attention_loads(l)
                elif s % 2:
                    mixture_loads(l)
            sp.wait_ge(sem("sub_done"), NSUB)
            for b in range(NB):
                sp.dma_start(out[b], x[QP * (b % 2):QP * (b % 2) + NQ, b // 2, :]).then_inc(sem("stored"), 16)
            sp.wait_ge(sem("stored"), 16 * NB)

        @block.tensor
        def _(pe):
            n_tr = [0]

            def tokens_to_T(src, s=None):
                for t in range(TT):
                    if s is not None:
                        pe.wait_ge(sem("h_ready"), TT * s + t + 1)
                    for k in range(KT):
                        last = nc.tensor.transpose(P[6 + k][:, 128 * t:128 * t + 128],
                                                   src[:, t, 128 * k:128 * k + 128], ident[:, :])
                last.then_inc(sem("tr_psum"), 1)
                n_tr[0] += 1

            def wait_T(n=None):
                n = n or n_tr[0]
                pe.wait_ge(sem("tr_act"), n)
                pe.wait_ge(sem("tr_dve"), n)

            def three_passes(out, w, x, k, first, last):
                for j, (wi, xi) in enumerate(((0, 0), (0, 1), (1, 0))):
                    ins = nc.tensor.matmul(out, w(wi, k), x(xi, k), start=first and j == 0, stop=last and j == 2)
                return ins

            def attention(l, part):
                a = ATT[l]
                na, nv, pd = (0, 48, 96)[a], 48 * a, (0, 96, 192)[a]
                pa = NPROJ[l] - 6

                def bank_free(B, g, before):
                    if g < 4:
                        if before is not None and PB[g] < 3:
                            pe.wait_ge(sem("s_taken"), before * 3 + (3 - 2 + PB[g]))
                    elif before is None and g < FIRST + 4:
                        pass
                    elif g - 4 < pa:
                        pe.wait_ge(sem("k_hi"), B * pa + (na + g - 3))
                        pe.wait_ge(sem("k_lo"), B * pa + (na + g - 3))
                    else:
                        pe.wait_ge(sem("v_ready"), B * 6 + (nv + g - 3 - pa))

                def features(B, g, m, src, before, banks):
                    for o in range(KT):
                        for c in range(NCH):
                            if banks is PB:
                                bank_free(B, g, before)
                            for k in range(KT):
                                last = three_passes(P[banks[g % len(banks)]][:, 0:CH],
                                                    lambda wi, k: ws[:, m, wi, k, 128 * o:128 * o + 128],
                                                    lambda xi, k: src[:, xi, k, CH * c:CH * c + CH], k, k == 0, k == 1)
                            last.then_inc(sem("proj_done"), 1)
                            g += 1

                def project_first(B, before, banks=PB):
                    pe.wait_ge(sem("ctx_lo"), B * 4 + (32 * a + 8))
                    features(B, 0, 2 if l == 3 else 0, C, before, banks)

                def support_keys(B, before):
                    pe.wait_ge(sem("sup_lo"), B * 6 + 8)
                    features(B, FIRST, 0, SUP, before, PB)

                def project_rest(B, before):
                    src = SUP if l == 3 else C
                    for j in range(6):
                        g = pa + j
                        bank_free(B, g, before)
                        for jj in range(2):
                            c0 = CT * (2 * j + jj)
                            for k in range(KT):
                                last = three_passes(P[PB[g % 4]][0:CT, D * jj:D * jj + D],
                                                    lambda xi, k: src[:, xi, k, c0:c0 + CT],
                                                    lambda wi, k: ws[:, 1, wi, k, :], k, k == 0, k == 1)
                        last.then_inc(sem("proj_done"), 1)

                def scores(n, B, p):
                    if p == 0:
                        pe.wait_ge(sem("k_hi"), B * pa + (na + pa))
                        pe.wait_ge(sem("k_lo"), B * pa + (na + pa))
                        pe.wait_ge(sem("k_turned"), B * 4 + (32 * a + 4))
                        pe.wait_ge(sem("qb_ready"), B * 6 + (48 * a + 6))
                    for c in range(NCH):
                        pe.wait_ge(sem("s_taken"), n * 3 + (c + 1))
                        if p == 0:
                            g = max(g for g in range(pa + 6) if PB[g % 4] == c)
                            pe.wait_ge(sem("v_ready"), B * 6 + (nv + g - pa + 1))
                        o, e, cs = p // 4, PR * (p % 4), slice(CH * c, CH * c + CH)
                        nc.tensor.matmul(P[c][0:PR, 0:CH], Qb[:, 0, o, e:e + PR], K[:, 0, o, cs], start=True, stop=False)
                        nc.tensor.matmul(P[c][0:PR, 0:CH], Qb[:, 1, o, e:e + PR], K[:, 1, o, cs] if p % 4 < 2 else K2[:, o, cs],
                                         start=False, stop=True).then_inc(sem("s_done"), 1)

                def turn(n, p):
                    pe.wait_ge(sem("exp_done"), n + 1)
                    for g in range(NCH):
                        if g == 0:
                            pe.wait_ge(sem("pt_act"), n * 2 + 1)
                        elif g == 1:
                            pe.wait_ge(sem("pt_dve"), n + 1)
                        else:
                            pe.wait_ge(sem("pt_act"), n * 2 + 2)
                        for j in range(4):
                            c0 = CT * (4 * g + j)
                            last = nc.tensor.transpose(P[TURN[g]][0:CT, PR * j:PR * j + PR],
                                                       Sb[0:PR, p % 2, c0:c0 + CT], ident[0:PR, 0:PR])
                        last.then_inc(sem("t_done"), 1)

                def values(n, B, p, groups):
                    if p == 0 and 0 in groups:
                        pe.wait_ge(sem("v_ready"), B * 6 + (nv + 6))
                        pe.wait_ge(sem("o_taken"), B + (8 * a + 1))
                    if 0 in groups:
                        pe.wait_ge(sem("pt_act"), n * 2 + 3)
                    if 1 in groups:
                        pe.wait_ge(sem("pt_dve"), n + 2)
                    if 2 in groups:
                        pe.wait_ge(sem("pt_act"), n * 2 + 4)
                    for j in range(4 * groups[0], min(NCT, 4 * groups[-1] + 4)):
                        r, c0 = 32 * ((p + 2 * (j % 2)) % 4), D * (j % 2) + 128 * (p // 4)
                        last = nc.tensor.matmul(P[5][r:r + 32, c0:c0 + PR], v[0:CT, j, 32 * p:32 * p + 32],
                                                PT[0:CT, p % 2, j // 4, PR * (j % 4):PR * (j % 4) + PR],
                                                start=j < 2, stop=j >= NCT - 2)
                    if 2 in groups:
                        last.then_inc(sem("pv_done"), 1)

                def heads_to_rows(B, bi):
                    pe.wait_ge(sem("oT_sb"), B + (8 * a + 1))
                    for k in range(KT):
                        for e, turn_to in enumerate((ident, turned_ident)):
                            last = nc.tensor.matmul(P[5][:, 128 * k:128 * k + 128], oTs[:, e, 128 * k:128 * k + 128],
                                                    turn_to[:, :], start=e == 0, stop=e == 1)
                    pe.wait_ge(sem("rinv_ok"), B + (8 * a + 1))
                    last = nc.tensor.matmul(P[5][:, D:D + NP], spread[:, :], rinv[0:PR, bi, :], start=True, stop=True)
                    last.then_inc(sem("on_psum"), 1)

                def batch(B, bi, more):
                    n0 = B * 8 + 64 * a
                    for p in range(NP - 1):
                        scores(n0 + (p + 1), B, p + 1)
                        if p >= 1:
                            values(n0 + (p - 1), B, p - 1, (0,))
                        turn(n0 + p, p)
                        if p >= 1:
                            values(n0 + (p - 1), B, p - 1, (1, 2))
                    if more:
                        project_first(B + 1, n0 + 8)
                    values(n0 + 6, B, 6, (0,))
                    turn(n0 + 7, 7)
                    values(n0 + 6, B, 6, (1, 2))
                    values(n0 + 7, B, 7, (0, 1, 2))
                    if more:
                        if l == 3:
                            support_keys(B + 1, n0 + 8)
                        project_rest(B + 1, n0 + 8)
                        scores(n0 + 8, B + 1, 0)
                    heads_to_rows(B, bi)

                if part == "first":
                    pe.wait_ge(sem("ws_split"), (2, 4, 7)[a])
                    project_first(0, None, (0, 1, 2, 3, 4, 5))
                    return
                if part == "support keys":
                    support_keys(0, None)
                    return
                pe.wait_ge(sem("k_hi"), na + FIRST)
                pe.wait_ge(sem("k_lo"), na + FIRST)
                project_rest(0, None)
                scores(64 * a, 0, 0)
                with pe.Fori(0, NB // 2 - 1) as i:
                    batch(i * 2, 0, True)
                    batch(i * 2 + 1, 1, True)
                batch(NB - 2, 0, True)
                batch(NB - 1, 1, False)

            def mixture(l):
                I, U, base, E = MOE[l]["I"], MOE[l]["U"], MOE_BASE[l], MOE[l]["E"]
                wait_T()
                for t in range(TT):
                    for k in range(KT):
                        last = nc.tensor.matmul(P[5][:, 16 * t:16 * t + E], hT[:, k, 128 * t:128 * t + 128],
                                                gw[:, l, k, 0:E], start=k == 0, stop=k == 1)
                last.then_inc(sem("logits"), 1)
                if l == 3:
                    pe.wait_ge(sem("cw_ready"), 4)
                    for t in range(TT):
                        last = nc.tensor.transpose(P[4][0:8, 128 * t:128 * t + 128], lg[:, 9, t, 0:8], ident[:, :])
                    last.then_inc(sem("prT_psum"), 1)

                pe.wait_ge(sem("hs_ready"), 2 * l + 2)

                def up(q, u):
                    k = q % 2
                    pe.wait_ge(sem("up_split"), u + (base + 1))
                    pe.wait_ge(sem("gu_taken"), u + (base + 1))
                    for half in range(2):
                        for kk in range(KT):
                            last = three_passes(P[k + 2 * half][0:I, 0:NB * NQ],
                                                lambda wi, kk: wus[q][:, wi, kk, I * half:I * half + I],
                                                lambda xi, kk: hs[:, xi, kk, :], kk, kk == 0, kk == 1)
                        last.then_inc(sem("gu_done"), 1)

                def down(q, u):
                    k = q % 2
                    pe.wait_ge(sem("act_ready"), u + (base + 3))
                    pe.wait_ge(sem("down_split"), u + (base + 5))
                    pe.wait_ge(sem("acc_done"), u + (base + 1))
                    for t in range(TT):
                        last = three_passes(P[4 + 2 * k + t // 2][:, D * (t % 2):D * (t % 2) + D],
                                            lambda ai, t: act_b[0:I, k, ai, 128 * t:128 * t + 128],
                                            lambda wi, t: wds[0:I, k, wi, :], t, True, True)
                    last.then_inc(sem("down_done"), 1)

                up(0, 0)
                if U > 12:
                    with pe.Fori(0, U // 4 - 1) as i:
                        for q in range(4):
                            up((q + 1) % 4, i * 4 + (q + 1))
                            down(q, i * 4 + q)
                for u in range(U - 4 if U > 12 else 0, U):
                    if u + 1 < U:
                        up((u + 1) % 4, u + 1)
                    down(u % 4, u)

            def absorbed_weights():
                pe.wait_ge(sem("act_ready"), MOE_BASE[1] + 2)
                pe.wait_ge(sem("w1_in"), 16 * 15)
                pe.wait_ge(sem("acc_done"), MOE_BASE[1] + 1)
                pe.wait_ge(sem("w1_in"), 16 * 15)
                for hh in range(NH):
                    last = nc.tensor.matmul(P[hh // 8][0:QC, 64 * (hh % 8):64 * (hh % 8) + 64], wuqT[:, hh, :],
                                            wukT[:, hh, :], start=True, stop=True)
                for hh in range(NH):
                    r, hp = 64 * (hh % 2), hh // 2
                    last = nc.tensor.matmul(P[2 + hp // 2][r:r + 64, D * (hp % 2):D * (hp % 2) + D], wuvT[:, hh, :],
                                            wo1[:, hh, :], start=True, stop=True)

            def window():
                wait_T()
                for k in range(KT):
                    last = nc.tensor.matmul(P[6][0:QC, :], wdq[:, k, :], hT[:, k, :], start=k == 0, stop=k == 1)
                for k in range(KT):
                    last = nc.tensor.matmul(P[7][0:R, 0:NB], wkvc[:, k, :], meanT[:, k, :], start=k == 0, stop=k == 1)
                last.then_inc(sem("pre1_psum"), 1)
                pe.wait_ge(sem("pre1_act"), 1)
                pe.wait_ge(sem("pre1_dve"), 1)
                for hh in range(NH):
                    r = hh % 4
                    if hh >= 4:
                        pe.wait_ge(sem("qn_taken"), hh - 3)
                        pe.wait_ge(sem("qr_taken"), hh - 3)
                    nc.tensor.matmul(P[r][:, :], wcomb[:, hh, :], qcT, start=True, stop=True)
                    nc.tensor.matmul(P[4 + r][64:128, :], wqr2[:, hh, :], qcT, start=True, stop=True
                                     ).then_inc(sem("qh_psum"), 1)
                pe.wait_ge(sem("qn_taken"), NH)
                pe.wait_ge(sem("qr_taken"), NH)

                def turn_rows(b, i, bi):
                    pe.wait_ge(sem(f"g_in{bi}"), i * 64 + 64)
                    pe.wait_ge(sem("keff_sb"), b + 1)
                    for f in range(3):
                        for t in range(NGT):
                            last = nc.tensor.transpose(P[f][:, GR * t:GR * t + GR],
                                                       G[:, bi, t, 128 * f:128 * f + 128], ident[0:GR, 0:GR])
                    last.then_inc(sem("g_turned"), 1)

                def compress(b):
                    pe.wait_ge(sem("g_sb"), b + 1)
                    for k in range(KT):
                        last = nc.tensor.matmul(P[0][0:R, 0:WB], wkvc[:, k, :], gT[:, k, :], start=k == 0, stop=k == 1)
                    last.then_inc(sem("kv_psum"), 1)

                def key_terms(b, bi):
                    pe.wait_ge(sem("cs_sb"), b + 1)
                    pe.wait_ge(sem("kv_sb"), b + 1)
                    nc.tensor.matmul(P[1][:, 0:WB], wkr, keff[bi][0:R, :], start=True, stop=True).then_inc(sem("kr_psum"), 1)
                    for g in range(NG):
                        last = nc.tensor.transpose(P[2][0:GW, R * g:R * g + R], keff[bi][0:R, GW * g:GW * g + GW],
                                                   ident[0:R, 0:R])
                    last.then_inc(sem("kvn_psum"), 1)

                def rotate(b):
                    pe.wait_ge(sem("prod_sb"), b + 1)
                    nc.tensor.matmul(P[0][64:128, 0:WB], wstk, prod, start=True, stop=True).then_inc(sem("krs_psum"), 1)

                def scores1(b, bi):
                    pe.wait_ge(sem("keff_sb"), b + 2)
                    pe.wait_ge(sem("qb1_sb"), b + 1)
                    for g in range(NG):
                        last = nc.tensor.matmul(P[3][:, GW * g:GW * g + GW], qb1[bi][:, GT * g:GT * g + GT, :].rearrange("p q h -> p (q h)"),
                                                keff[bi][:, GW * g:GW * g + GW], start=True, stop=True)
                    last.then_inc(sem("s1_psum"), 1)

                def turn_weights(b):
                    pe.wait_ge(sem("p1_sb"), b + 1)
                    for g in range(NG):
                        last = nc.tensor.transpose(P[4 + g // 4][0:GW, 128 * (g % 4):128 * (g % 4) + 128],
                                                   P1[:, GW * g:GW * g + GW], ident[:, :])
                    last.then_inc(sem("pt1_psum"), 1)

                def sums(b, bi):
                    pe.wait_ge(sem("pt1_sb"), b + 1)
                    pe.wait_ge(sem("p1_taken"), b + 2)
                    for g in range(NG):
                        last = nc.tensor.matmul(P[6 + g // 4][:, 128 * (g % 4):128 * (g % 4) + 128], kvn[bi][:, g, :],
                                                PT1[:, g, :], start=True, stop=True)
                    last.then_inc(sem("oc_psum"), 1)

                def batch(i, bi, more):
                    b = i * 2 + bi
                    scores1(b, bi)
                    if more:
                        turn_rows(b + 1, i + bi, 1 - bi)
                        compress(b + 1)
                    turn_weights(b)
                    if more:
                        key_terms(b + 1, 1 - bi)
                    sums(b, bi)
                    if more:
                        rotate(b + 1)

                turn_rows(0, 0, 0)
                compress(0)
                key_terms(0, 0)
                rotate(0)
                with pe.Fori(0, NB // 2 - 1) as i:
                    batch(i, 0, True)
                    batch(i, 1, True)
                batch(NB // 2 - 1, 0, True)
                batch(NB // 2 - 1, 1, False)
                pe.wait_ge(sem("p1_taken"), NB + 2)
                for t in range(TT):
                    for hp in range(NP):
                        last = nc.tensor.matmul(P[t // 2][:, D * (t % 2):D * (t % 2) + D], ocT[:, hp, 128 * t:128 * t + 128],
                                                wuvo[:, hp, :], start=hp == 0, stop=hp == NP - 1)
                last.then_inc(sem("out1_psum"), 1)

            def turn_weights2():
                pe.wait_ge(sem("w2n_ready"), 1)
                pe.wait_ge(sem("k_hi"), FIRST)
                pe.wait_ge(sem("k_lo"), FIRST)
                for m in range(2):
                    for k in range(KT):
                        for o in range(KT):
                            last = nc.tensor.transpose(P[3 + m][:, D * k + 128 * o:D * k + 128 * o + 128],
                                                       w2n[:, 2 * m + o, 128 * k:128 * k + 128], ident[:, :])
                last.then_inc(sem("w2T_psum"), 1)

            for s in range(NSUB):
                l = s // 2
                if s % 2 == 0 and l in ATT:
                    if l:
                        pe.wait_ge(sem("acc_done"), MOE_BASE[l] + 2)
                    attention(l, "first")
                if s == 2:
                    absorbed_weights()
                if s == 0:
                    pe.wait_ge(sem("const_in"), 16 * 17)
                tokens_to_T(h, s)
                if s % 2:
                    mixture(l)
                    continue
                if l == 1:
                    window()
                    continue
                a = ATT[l]
                wait_T()
                src = hT
                if l == 3:
                    for o in range(KT):
                        for k in range(KT):
                            last = nc.tensor.matmul(P[6 + o][:, :], w3[:, 0, k, 128 * o:128 * o + 128], hT[:, k, :],
                                                    start=k == 0, stop=k == 1)
                    last.then_inc(sem("refT_psum"), 1)
                    pe.wait_ge(sem("refT_sb"), 2)
                    attention(l, "support keys")
                    src = oT
                    for t in range(TT):
                        for k in range(KT):
                            last = nc.tensor.transpose(P[4 + t // 2][:, D * (t % 2) + 128 * k:D * (t % 2) + 128 * k + 128],
                                                       oT[:, k, 128 * t:128 * t + 128], ident[:, :])
                    last.then_inc(sem("ref_psum"), 1)
                    pe.wait_ge(sem("ref_sb"), 1)
                wq = w0[:, 0] if l == 0 else w3[:, 1] if l == 3 else w2T[:, 0:2]
                for o in range(KT):
                    for k in range(KT):
                        last = nc.tensor.matmul(P[QBANK[l][o]][:, :], wq[:, k, 128 * o:128 * o + 128], src[:, k, :],
                                                start=k == 0, stop=k == 1)
                last.then_inc(sem("q_psum"), 1)
                if l == 0:
                    turn_weights2()
                pe.wait_ge(sem("q_sb"), a + 1)
                if l == 0:
                    for t in range(TT):
                        for k in range(KT):
                            last = nc.tensor.matmul(P[5 + t // 2][:, D * (t % 2):D * (t % 2) + D],
                                                    hT[:, k, 128 * t:128 * t + 128], w0[:, 4, k, :],
                                                    start=k == 0, stop=k == 1)
                    last.then_inc(sem("gate_psum"), 1)
                attention(l, "pairs")
                if l == 3:
                    continue
                pe.wait_ge(sem("o_ready"), a + 1)
                tokens_to_T(onat)
                wait_T()
                wo = w0[:, 3] if l == 0 else w2T[:, 2:4]
                for t in range(TT):
                    for k in range(KT):
                        last = nc.tensor.matmul(P[t // 2][:, D * (t % 2):D * (t % 2) + D],
                                                oT[:, k, 128 * t:128 * t + 128], wo[:, k, :],
                                                start=k == 0, stop=k == 1)
                last.then_inc(sem("out_psum"), 1)

        @block.scalar
        def _(act):
            n_tr = [0]

            def transposed(dst, scale=1.0):
                n_tr[0] += 1
                act.wait_ge(sem("tr_psum"), n_tr[0])
                nc.scalar.activation(dst[:, 0, :], P[6][:, :], ACT.Copy, scale=scale).then_inc(sem("tr_act"), 1)

            def root(dst, src, n):
                act.wait_ge(sem("var_ready"), n)
                nc.scalar.activation(dst, src, ACT.Sqrt).then_inc(sem("std_ready"), 1)

            def context_lead(l, b, j):
                o, c0 = j // 2, NCTX // 2 * (j % 2)
                nc.scalar.activation(C[:, 0, o, c0:c0 + NCTX // 2], ctxT[:, o, c0:c0 + NCTX // 2], ACT.Copy
                                     ).then_inc(sem("ctx_hi"), 1)

            def weights_lead(l):
                if l == 0:
                    act.wait_ge(sem("wkv_in"), 16)
                if l == 2:
                    act.wait_ge(sem("w2_in"), 16)
                for m, src in {0: ((0, w0[:, 1]), (1, w0[:, 2])), 2: ((0, w2[:, 0]), (1, w2[:, 1])),
                               3: ((2, w3[:, 0]), (0, w3[:, 2]), (1, w3[:, 3]))}[l]:
                    nc.scalar.activation(ws[:, m, 0, :, :], src, ACT.Copy).then_inc(sem("ws_lead"), 1)

            def first_context(l):
                act.wait_ge(sem("ctx_in"), 16 * (8 * ATT[l] + 1))
                for j in range(4):
                    context_lead(l, 0, j)

            def attention(l, part):
                a = ATT[l]
                na = (0, 48, 96)[a]
                pa = NPROJ[l] - 6
                pd = (0, 96, 192)[a]

                def leads(B, g, banks=PB):
                    for o in range(KT):
                        for c in range(NCH):
                            act.wait_ge(sem("proj_done"), B * NPROJ[l] + (pd + g + 1))
                            src = P[banks[g % len(banks)]][:, 0:CH]
                            if l == 3 and g < FIRST:
                                nc.scalar.activation(SUP[:, 0, o, CH * c:CH * c + CH], src, ACT.Relu,
                                                     bias=cols[:, 6 + o:7 + o]).then_inc(sem("k_hi"), 1)
                            elif l == 0:
                                nc.scalar.activation(K[:, 0, o, CH * c:CH * c + CH], src, ACT.Copy).then_inc(sem("k_hi"), 1)
                            else:
                                col = 4 + o if l == 2 else 10 + o
                                nc.scalar.activation(K[:, 0, o, CH * c:CH * c + CH], src, ACT.Identity, bias=cols[:, col:col + 1]
                                                     ).then_inc(sem("k_hi"), 1)
                            g += 1

                def keys_turned(B):
                    act.wait_ge(sem("k_hi"), B * pa + (na + pa))
                    for o in range(KT):
                        nc.scalar.activation(K[64:128, 1, o, :], K[0:64, 0, o, :].bitcast(F32), ACT.Copy).then_inc(sem("k_turned"), 1)
                        nc.scalar.activation(K2[0:64, o, :], K[64:128, 0, o, :].bitcast(F32), ACT.Copy).then_inc(sem("k_turned"), 1)

                def exps(n, bi, p):
                    act.wait_ge(sem("nm_ready"), n + 1)
                    nc.scalar.activation(Sb[0:PR, p % 2, :], Sb[0:PR, p % 2, :], ACT.Exp, bias=nm[0:PR, p % 4:p % 4 + 1],
                                         accum_out=rsum[0:PR, bi, p:p + 1]).then_inc(sem("exp_done"), 1)

                def turned(n, p, groups=(0, 2)):
                    act.wait_ge(sem("pv_done"), n + 1)
                    for g in groups:
                        act.wait_ge(sem("t_done"), n * 3 + (12 + g + 1))
                        nc.scalar.activation(PT[0:CT, p % 2, g, 0:4 * PR], P[TURN[g]][0:CT, 0:4 * PR], ACT.Copy
                                             ).then_inc(sem("pt_act"), 1)

                def batch(i, bi, more):
                    B = i * 2 + bi
                    n0 = i * 16 + (64 * a + 8 * bi)
                    for p in range(NP - 1):
                        turned(n0 + p, p, (0,))
                        exps(n0 + (p + 1), bi, p + 1)
                        turned(n0 + p, p, (2,))
                        if more and p < 4:
                            if p == 0:
                                act.wait_ge(sem("ctx_in"), B * 16 + 16 * (8 * a + 2))
                                act.wait_ge(sem("proj_done"), B * NPROJ[l] + (pd + NPROJ[l]))
                            context_lead(l, B + 1, p)
                    if more:
                        leads(B + 1, 0)
                    turned(n0 + 7, 7)
                    if more and l < 3:
                        keys_turned(B + 1)
                    act.wait_ge(sem("pv_done"), n0 + (8 + 2))
                    act.wait_ge(sem("o_taken"), B + (8 * a + 1))
                    src = P[5][:, :].rearrange("p (s n) -> p s n", s=4)[:, :, 0:PR].rearrange("p s (e q) -> p s e q", q=NQ)
                    dst = oTs[:, :, :].rearrange("p j (s n) -> p (j s) n", n=2 * QP).rearrange("p s (e q) -> p s e q", q=QP)[:, :, :, 0:NQ]
                    nc.scalar.activation(dst, src, ACT.Copy
                                         ).then_inc(sem("oT_sb"), 1)
                    if more:
                        if l == 3:
                            leads(B + 1, FIRST)
                            keys_turned(B + 1)
                        exps(n0 + 8, 1 - bi, 0)

                if part == "first":
                    leads(0, 0, (0, 1, 2, 3, 4, 5))
                    return
                if part == "support keys":
                    leads(0, FIRST)
                    return
                keys_turned(0)
                exps(64 * a, 0, 0)
                with act.Fori(0, NB // 2 - 1) as i:
                    batch(i, 0, True)
                    batch(i, 1, True)
                batch(NB // 2 - 1, 0, True)
                batch(NB // 2 - 1, 1, False)

            def up_lead(l, q, u):
                I, base = MOE[l]["I"], MOE_BASE[l]
                act.wait_ge(sem(f"w_in{q}"), (u - q) * 8 + 32 * (base // 4 + 1))
                nc.scalar.activation(wus[q][:, 0, :, 0:2 * I], wu[:, q, :, 0:2 * I], ACT.Copy).then_inc(sem("up_lead"), 1)

            def down_lead(l, q, u):
                I, base = MOE[l]["I"], MOE_BASE[l]
                act.wait_ge(sem("down_done"), u + (base + 3))
                nc.scalar.activation(wds[0:I, q % 2, 0, :], wd[0:I, q, :], ACT.Copy).then_inc(sem("down_lead"), 1)

            def mixture(l):
                I, U, base = MOE[l]["I"], MOE[l]["U"], MOE_BASE[l]
                act.wait_ge(sem("lg_ready"), l + 1)
                if l < 3:
                    nc.scalar.activation(lg[:, 2, :, :], lg[:, 1, :, :], ACT.Exp).then_inc(sem("lg_exp"), 1)
                else:
                    nc.scalar.activation(lg[:, 2, :, 0:8], lg[:, 0, :, 0:8], ACT.Sigmoid).then_inc(sem("lg_exp"), 1)

                def silu(k, u):
                    act.wait_ge(sem("act_ready"), u + (base + 1))
                    if l == 3 and u > 0:
                        act.wait_ge(sem("pb_used"), u + 2)
                        src = sg[0:I, k, :]
                    else:
                        act.wait_ge(sem("gu_done"), u * 2 + (2 * base + 5))
                        src = P[k][0:I, 0:NB * NQ]
                    nc.scalar.activation(sg[0:I, k, :], src, ACT.Silu).then_inc(sem("silu_done"), 1)

                def lead(k, u):
                    act.wait_ge(sem("down_done"), u + (base + 3))
                    act.wait_ge(sem("gu_taken"), u + (base + 3))
                    nc.scalar.activation(real(act_b[0:I, k, 0, :]), sg[0:I, k, :].rearrange("p (b q) -> p b q", q=NQ), ACT.Copy
                                         ).then_inc(sem("act_hi"), 1)

                def step(q, u, more):
                    silu(q % 2, u)
                    if more:
                        up_lead(l, (q + 2) % 4, u + 2)
                    down_lead(l, q, u)
                    lead(q % 2, u)

                if U > 12:
                    with act.Fori(0, U // 4 - 1) as i:
                        for q in range(4):
                            step(q, i * 4 + q, True)
                for u in range(U - 4 if U > 12 else 0, U):
                    step(u % 4, u, u + 2 < U)

            def window():
                act.wait_ge(sem("pre1_psum"), 1)
                nc.scalar.activation(qcT, P[6][0:QC, :], ACT.Copy)
                nc.scalar.activation(mkv[0:R, :], P[7][0:R, 0:NB], ACT.Copy, scale=1.0 / NCTX)
                for j in range(2):
                    last = nc.scalar.activation(wcomb[:, 8 * j:8 * j + 8, 0:R],
                                                P[j][0:QC, :].rearrange("p (h n) -> p h n", h=8), ACT.Copy)
                last.then_inc(sem("pre1_act"), 1)
                for hh in range(NH):
                    act.wait_ge(sem("qh_psum"), hh + 1)
                    nc.scalar.activation(qeff[0:64, :, hh, :], P[hh % 4][0:64, :].rearrange("p (b q) -> p b q", b=NB),
                                         ACT.Copy).then_inc(sem("qn_taken"), 1)
                act.wait_ge(sem("qr_taken"), NH)

                def take_rows(b, bi):
                    act.wait_ge(sem("g_turned"), b + (2 + 1))
                    nc.scalar.activation(gT[:, 0, :], P[0][:, 0:WB], ACT.Copy)
                    nc.scalar.activation(gT[:, 1, :], P[1][:, 0:WB], ACT.Copy).then_inc(sem("g_sb"), 1)

                def take_rotations():
                    nc.scalar.activation(csT, P[2][:, 0:WB], ACT.Copy).then_inc(sem("cs_sb"), 1)

                def take_queries(b, bi):
                    nc.scalar.activation(qb1[bi], qeff[:, bass.ds(b, 1), :, :].rearrange("p b h q -> p q (b h)"),
                                         ACT.Copy).then_inc(sem("qb1_sb"), 1)

                def take_keys(b, bi):
                    act.wait_ge(sem("kvn_psum"), b + 1)
                    src = P[2][0:GW, 0:NG * R].rearrange("p (g n) -> p g n", g=NG)
                    for j in range(2):
                        nc.scalar.activation(kvn[bi][:, :, R * j:R * j + R], src, ACT.Copy)
                    act.wait_ge(sem("krs_psum"), b + 1)
                    nc.scalar.activation(keff[bi][64:128, :], P[0][64:128, 0:WB], ACT.Copy).then_inc(sem("keff_sb"), 1)

                def batch(i, bi, more):
                    b = i * 2 + bi
                    if more:
                        take_rows(b + 1, 1 - bi)
                    act.wait_ge(sem("s1_sb"), b + 3)
                    nc.scalar.activation(P1, P1, ACT.Exp, scale=SCALE1).then_inc(sem("e1_sb"), 1)
                    if more:
                        take_rotations()
                        take_queries(b + 1, 1 - bi)
                    act.wait_ge(sem("pt1_psum"), b + 1)
                    for j, m in ((0, 4), (1, 3)):
                        last = nc.scalar.activation(PT1[:, 4 * j:4 * j + m, :].rearrange("p g n -> p (g n)"),
                                                    P[4 + j][0:GW, 0:128 * m], ACT.Copy)
                    last.then_inc(sem("pt1_sb"), 1)
                    if more:
                        take_keys(b + 1, 1 - bi)

                take_rows(0, 0)
                take_rotations()
                take_queries(0, 0)
                take_keys(0, 0)
                with act.Fori(0, NB // 2 - 1) as i:
                    batch(i, 0, True)
                    batch(i, 1, True)
                batch(NB // 2 - 1, 0, True)
                batch(NB // 2 - 1, 1, False)

            nr = 0
            for s in range(NSUB):
                l = s // 2
                nr += 1
                if s == 0:
                    weights_lead(0)
                    first_context(0)
                root(sm[:, 1, :], sm[:, 0, :], nr)
                if s % 2:
                    act.wait_ge(sem("sub_done"), s)
                    for u in range(2):
                        up_lead(l, u, u)
                if s == 0:
                    nr += 1
                    root(sm[:, 1, :], sm[:, 0, :], nr)
                    act.wait_ge(sem("const_in"), 16 * 17)
                    nc.scalar.activation(tg[:, :], tg[:, :], ACT.Tanh).then_inc(sem("tg_ready"), 1)
                if s % 2 == 0 and l in ATT:
                    attention(l, "first")
                transposed(hT, cols[:, 0:1] if s == 0 else 1.0)
                if s % 2:
                    nc.scalar.activation(hs[:, 0, 0, :].rearrange("p (b q) -> p b q", q=NQ), real(P[6][:, :]), ACT.Copy
                                         ).then_inc(sem("hs_lead"), 1)
                    if s + 1 < NSUB and l + 1 in ATT:
                        first_context(l + 1)
                        weights_lead(l + 1)
                    mixture(l)
                    continue
                if l == 1:
                    window()
                    continue
                if l == 3:
                    act.wait_ge(sem("refT_psum"), 1)
                    for o in range(KT):
                        nc.scalar.activation(oT[:, o, :], P[6 + o][:, :], ACT.Relu, bias=cols[:, 6 + o:7 + o]
                                             ).then_inc(sem("refT_sb"), 1)
                    attention(l, "support keys")
                if l == 0:
                    act.wait_ge(sem("gate_psum"), 1)
                    for j in range(2):
                        nc.scalar.activation(tmp[:, 2 * j:2 * j + 2, :], P[5 + j][:, :], ACT.Sigmoid
                                             ).then_inc(sem("gate_ready"), 1)
                attention(l, "pairs")
                if l < 3:
                    transposed(oT)

        @block.vector
        def _(dve):
            steps, n_tr, n_root, signals = [0], [0], [0], [0]
            V = nc.vector

            def step(ins):
                steps[0] += 1
                ins.then_inc(sem("dve_step"), 1)
                dve.wait_ge(sem("dve_step"), steps[0])

            def signal(name, n=1):
                signals[0] += 1
                V.memset(flags[:, signals[0]:signals[0] + 1], 0.0).then_inc(sem(name), n)

            def wide(col, n):
                return col.rearrange("p (t o) -> p t o", o=1).broadcast_to([128, TT, n])

            def transposed(dst, scale=None):
                n_tr[0] += 1
                dve.wait_ge(sem("tr_psum"), n_tr[0])
                if scale is None:
                    V.tensor_copy(dst[:, 1, :], P[7][:, :]).then_inc(sem("tr_dve"), 1)
                else:
                    V.tensor_scalar(dst[:, 1, :], P[7][:, :], scale, None, ALU.mult).then_inc(sem("tr_dve"), 1)

            def inverse_root(ins):
                n_root[0] += 1
                ins.then_inc(sem("var_ready"), 1)
                dve.wait_ge(sem("std_ready"), n_root[0])
                step(V.reciprocal(sm[:, 2, :], sm[:, 1, :]))

            def layer_norm(announce):
                for t in range(TT):
                    last = V.bn_stats(stats[:, t, :], x[:, t, :])
                step(last)
                for t in range(TT):
                    last = V.bn_aggr(mv[:, t, :], stats[:, t, :])
                step(last)
                inverse_root(V.tensor_scalar(sm[:, 0, :], mv[:, :, 1], 1e-5, None, ALU.add))
                for t in range(TT):
                    last = V.tensor_scalar(h[:, t, :], x[:, t, :], mv[:, t, 0:1], sm[:, 2, t:t + 1],
                                           ALU.subtract, ALU.mult)
                    if announce:
                        last.then_inc(sem("h_ready"), 1)
                if not announce:
                    step(last)

            def fake_quantise(w):
                magic = 12582912.0
                step(V.tensor_reduce(sm[:, 4, :], w[:, :, :], AX.X, ALU.max, apply_absolute_value=True))
                step(V.tensor_scalar(sm[:, 5, :], sm[:, 4, :], 1.0 / 127.0, 1e-8, ALU.mult, ALU.max))
                step(V.reciprocal(sm[:, 6, :], sm[:, 5, :]))
                step(V.tensor_tensor(w[:, :, :], w[:, :, :], wide(sm[:, 6, :], D), ALU.mult))
                step(V.tensor_scalar(w[:, :, :], w[:, :, :], magic, magic, ALU.add, ALU.subtract))
                step(V.tensor_scalar(w[:, :, :], w[:, :, :], 127.0, -127.0, ALU.min, ALU.max))
                return V.tensor_tensor(w[:, :, :], w[:, :, :], wide(sm[:, 5, :], D), ALU.mult)

            def add_gated(g, tiles, y):
                return V.scalar_tensor_tensor(x[:, tiles, :], y, tg[:, g:g + 1], x[:, tiles, :], ALU.mult, ALU.add)

            def add_banks(g):
                for j in range(2):
                    last = add_gated(g, slice(2 * j, 2 * j + 2), P[j][:, :].rearrange("p (t d) -> p t d", t=2))
                last.then_inc(sem("sub_done"), 1)
                dve.wait_ge(sem("sub_done"), 2 * g + 1)

            def residual(g, y):
                V.scalar_tensor_tensor(x[:, :, :].rearrange("p t d -> p (t d)"), y, tg[:, g:g + 1],
                                       x[:, :, :].rearrange("p t d -> p (t d)"), ALU.mult, ALU.add
                                       ).then_inc(sem("sub_done"), 1)
                dve.wait_ge(sem("sub_done"), (2 * g + 1) if g < 4 else 2 * (g - 4) + 2)

            def attention(l, part):
                a = ATT[l]
                pd = (0, 96, 192)[a]

                na = (0, 48, 96)[a]
                pa = NPROJ[l] - 6

                def rests(B, g, banks=PB):
                    for o in range(KT):
                        for c in range(NCH):
                            dve.wait_ge(sem("k_hi"), B * pa + (na + g + 1))
                            src = P[banks[g % len(banks)]][:, 0:CH]
                            cs = slice(CH * c, CH * c + CH)
                            if l == 3 and g < FIRST:
                                dve.wait_ge(sem("sup_lo"), B * 6 + (g + 1))
                                ins = V.tensor_scalar(sup_f[:, g % 2, :], src, cols[:, 6 + o:7 + o], 0.0, ALU.add, ALU.max)
                            else:
                                for rest, r in ((K[0:64, 1, o, cs], slice(0, 64)), (K2[64:128, o, cs], slice(64, 128))):
                                    lead = K[r, 0, o, cs].bitcast(F32)
                                    if l == 0:
                                        ins = V.tensor_tensor(rest, src[r], lead, ALU.subtract)
                                    else:
                                        col = 4 + o if l == 2 else 10 + o
                                        ins = V.scalar_tensor_tensor(rest, src[r], cols[r, col:col + 1], lead, ALU.add, ALU.subtract)
                            ins.then_inc(sem("k_lo"), 1)
                            g += 1

                def take_values(B):
                    for j in range(6):
                        g = pa + j
                        dve.wait_ge(sem("proj_done"), B * NPROJ[l] + (pd + g + 1))
                        V.tensor_copy(v[0:CT, 2 * j:2 * j + 2, :].rearrange("p j d -> p (j d)"),
                                      P[PB[g % 4]][0:CT, :]).then_inc(sem("v_ready"), 1)

                def mean(B, k):
                    V.tensor_reduce(meanT[:, k, bass.ds(B, 1)], ctxT[:, k, :], AX.X, ALU.add).then_inc(sem("mean_done"), 1)

                def mask(B, i, bi):
                    if l == 0:
                        dve.wait_ge(sem(f"mask_in{bi}"), i * 16 + 16)
                        V.tensor_scalar(maskf[:, bi, :], maskraw[:, bi, :].bitcast(U8), -NEG, NEG, ALU.mult, ALU.add
                                        ).then_inc(sem("mask_made"), 1)
                        dve.wait_ge(sem("mask_made"), B + 1)
                    if l == 2:
                        dve.wait_ge(sem(f"mask_in{bi}"), i * 32 + 16 * 4 + 32)

                def maxima(n, B, bi, p):
                    r = p % 4
                    dve.wait_ge(sem("t_done"), n * 3 + 9)
                    for c in range(NCH):
                        dve.wait_ge(sem("s_done"), n * 3 + (c + 1))
                        dve.sem_inc(sem("waits_met"), 1)
                        o = Sb[0:PR, p % 2, CH * c:CH * c + CH]
                        if l == 3:
                            V.tensor_scalar(o, P[c][0:PR, 0:CH], 1.0, None, ALU.mult, ALU.max,
                                            accum_out=mx[0:PR, r, c:c + 1]).then_inc(sem("s_taken"), 1)
                        else:
                            V.tensor_tensor_reduce(o, P[c][0:PR, 0:CH], maskf[0:PR, bi, CH * c:CH * c + CH], 1.0, -3.0e38,
                                                   ALU.add, ALU.max, mx[0:PR, r, c:c + 1]).then_inc(sem("s_taken"), 1)
                    dve.wait_ge(sem("s_taken"), n * 3 + (3 + 3))
                    V.tensor_reduce(nm[0:PR, r:r + 1], mx[0:PR, r, 0:4 if l == 0 else 3], AX.X, ALU.max, negate=True
                                    ).then_inc(sem("nm_ready"), 1)

                def turned(n, p):
                    dve.wait_ge(sem("pv_done"), n + 1)
                    dve.wait_ge(sem("t_done"), n * 3 + (12 + 2))
                    V.tensor_copy(PT[0:CT, p % 2, 1, 0:4 * PR], P[TURN[1]][0:CT, 0:4 * PR]).then_inc(sem("pt_dve"), 1)

                def inverse_sums(B, bi):
                    dve.wait_ge(sem("exp_done"), B * 8 + (64 * a + 8))
                    V.tensor_scalar(rinv[0:PR, bi, :], rsum[0:PR, bi, :], 1e-30, None, ALU.max).then_inc(sem("rsum_ok"), 1)
                    dve.wait_ge(sem("rsum_ok"), B + (8 * a + 1))
                    V.reciprocal(rinv[0:PR, bi, :], rinv[0:PR, bi, :]).then_inc(sem("rinv_ok"), 1)

                def normalise(B, i, bi):
                    dve.wait_ge(sem("on_psum"), B + (8 * a + 1))
                    V.tensor_copy(factors[:, :], P[5][:, D:D + NP]).then_inc(sem("factors"), 1)
                    dve.wait_ge(sem("factors"), B + (8 * a + 1))
                    for e in range(2):
                        src = P[5][QP * e:QP * e + QP, 0:D].rearrange("q (p c) -> q p c", c=32)[:, :, HD * e:HD * e + HD]
                        dst = onat[QP * bi:QP * bi + QP, bass.ds(i, 1), :].rearrange("q o (p c) -> q (o p) c", c=32)[:, :, HD * e:HD * e + HD]
                        last = V.tensor_tensor(dst, src, factors[QP * e:QP * e + QP, :].rearrange("q (p o) -> q p o", o=1).broadcast_to([QP, NP, HD]),
                                               ALU.mult)
                    last.then_inc(sem("o_taken"), 1)

                def batch(i, bi, more):
                    B = i * 2 + bi
                    n0 = i * 16 + (64 * a + 8 * bi)
                    for p in range(NP - 1):
                        maxima(n0 + (p + 1), B, bi, p + 1)
                        if p == NP - 2 and l < 3:
                            V.memset(flags[:, 100:101], 0.0).then_inc(sem("mask_used"), 1)
                        turned(n0 + p, p)
                        if more and l == 0 and p in (3, 5):
                            if p == 3:
                                dve.wait_ge(sem("ctx_in"), B * 16 + 32)
                            mean(B + 1, p // 4)
                    if more:
                        rests(B + 1, 0)
                    turned(n0 + 7, 7)
                    inverse_sums(B, bi)
                    if more:
                        if l == 3:
                            rests(B + 1, FIRST)
                        take_values(B + 1)
                        mask(B + 1, i + bi, 1 - bi)
                        maxima(n0 + 8, B + 1, 1 - bi, 0)
                    normalise(B, i, bi)

                if part == "first":
                    rests(0, 0, (0, 1, 2, 3, 4, 5))
                    if l == 3:
                        rests(0, FIRST)
                    return
                take_values(0)
                mask(0, 0, 0)
                maxima(64 * a, 0, 0, 0)
                if l == 0:
                    dve.wait_ge(sem("ctx_in"), 16)
                    mean(0, 0)
                    mean(0, 1)
                with dve.Fori(0, NB // 2 - 1) as i:
                    batch(i, 0, True)
                    batch(i, 1, True)
                batch(NB // 2 - 1, 0, True)
                batch(NB // 2 - 1, 1, False)
                dve.wait_ge(sem("o_taken"), 8 * (a + 1) + 1)

            def routing_scores(l):
                E, K, U, per = (MOE[l][k] for k in ("E", "K", "U", "per"))

                def L(j):
                    return lg[:, j, :, 0:E]

                def s4(j):
                    return sm[:, j, :]

                dve.wait_ge(sem("logits"), l + 1)
                src = P[5][:, 0:64].rearrange("p (t e) -> p t e", t=TT)[:, :, 0:E]
                if l < 3:
                    step(V.tensor_reduce(s4(8), src, AX.X, ALU.max))
                    V.tensor_tensor(L(1), src, wide(s4(8), E), ALU.subtract).then_inc(sem("lg_ready"), 1)
                    dve.wait_ge(sem("lg_exp"), l + 1)
                    step(V.tensor_reduce(s4(9), L(2), AX.X, ALU.add))
                    step(V.reciprocal(s4(10), s4(9)))
                    step(V.tensor_tensor(L(0), L(2), wide(s4(10), E), ALU.mult))
                else:
                    step(V.tensor_copy(L(0), src))
                    signal("lg_ready")

            def routing_weights(l):
                E, K, U, per = (MOE[l][k] for k in ("E", "K", "U", "per"))

                def L(j):
                    return lg[:, j, :, 0:E]

                def s4(j):
                    return sm[:, j, :]

                for t in range(TT):
                    last = V.max(top8[:, t, :], lg[:, 0, t, 0:E])
                step(last)
                step(V.tensor_tensor(L(3), L(0), top8[:, :, K - 1:K].broadcast_to([128, TT, E]), ALU.is_gt))
                step(V.tensor_tensor(L(4), L(0), top8[:, :, K - 1:K].broadcast_to([128, TT, E]), ALU.is_equal))
                step(V.tensor_reduce(s4(11), L(3), AX.X, ALU.add))
                step(V.tensor_scalar(s4(12), s4(11), -1.0, float(K), ALU.mult, ALU.add))
                step(V.memset(lg[:, 8, :, :], 1.0))
                for t in range(TT):
                    last = V.tensor_tensor_scan(lg[:, 5, t, 0:E], lg[:, 8, t, 0:E], lg[:, 4, t, 0:E], 0.0, ALU.mult, ALU.add)
                step(last)
                step(V.tensor_tensor(L(6), L(5), wide(s4(12), E), ALU.is_le))
                step(V.tensor_tensor(L(6), L(6), L(4), ALU.mult))
                step(V.tensor_tensor(L(6), L(6), L(3), ALU.add))
                if l == 3:
                    dve.wait_ge(sem("lg_exp"), 4)
                    V.tensor_tensor(L(9), L(6), L(2), ALU.mult).then_inc(sem("cw_ready"), 1)
                    dve.wait_ge(sem("cw_ready"), 4)
                    step(V.memset(cw[:, :, 0:1], 1.0))
                    step(V.tensor_copy(cw[:, :, 1:9], L(9)))
                    dve.wait_ge(sem("prT_psum"), 1)
                    V.tensor_copy(qT[0:8, 0, :], P[4][0:8, :]).then_inc(sem("prT_sb"), 1)
                    return
                step(V.tensor_tensor(L(9), L(6), L(0), ALU.mult))
                if l in (1, 2):
                    step(V.tensor_reduce(s4(13), L(9), AX.X, ALU.add))
                    step(V.reciprocal(s4(14), s4(13)))
                    step(V.tensor_tensor(L(9), L(9), wide(s4(14), E), ALU.mult))
                    if l == 1:
                        step(V.tensor_scalar(L(9), L(9), K / (K + 1.0), None, ALU.mult))
                step(V.memset(cw[:, :, :], 1.0 / (K + 1.0) if l == 1 else 1.0))
                for r in range(per):
                    dst = cw[:, :, 0:per * E].rearrange("p t (e r) -> p t e r", r=per)[:, :, :, r]
                    last = V.tensor_copy(dst, L(9))
                last.then_inc(sem("cw_ready"), 1)
                dve.wait_ge(sem("cw_ready"), l + 1)

            def mixture(l):
                I, U, base = MOE[l]["I"], MOE[l]["U"], MOE_BASE[l]
                by_batch = lambda y: y.rearrange("p (b q) -> p b q", q=NQ)
                step(V.tensor_copy(by_batch(hs[:, 0, 1, :]), real(P[7][:, :])))
                V.tensor_tensor(by_batch(hs[:, 1, 1, :]), real(P[7][:, :]), by_batch(hs[:, 0, 1, :].bitcast(F32)), ALU.subtract
                                ).then_inc(sem("hs_ready"), 1)
                dve.wait_ge(sem("hs_lead"), l + 1)
                V.tensor_tensor(by_batch(hs[:, 1, 0, :]), real(P[6][:, :]), by_batch(hs[:, 0, 0, :].bitcast(F32)), ALU.subtract
                                ).then_inc(sem("hs_ready"), 1)
                V.memset(acc[:, :, :], 0.0)
                for k in range(2):
                    for e in range(2):
                        last = V.memset(act_b[:, k, e, :].rearrange("p (b q) -> p b q", q=QP)[:, :, NQ:QP].bitcast(F32), 0.0)
                step(last)
                routing_scores(l)
                if l == 3:
                    routing_weights(l)

                def scale(k, u):
                    dve.wait_ge(sem(f"pb_in{k}"), 16 * ((u + 1) // 2))
                    dve.wait_ge(sem("gu_done"), u * 2 + (2 * base + 6))
                    dve.wait_ge(sem("act_ready"), u + (base + 1))
                    V.tensor_tensor(sg[0:I, k, :], P[k][0:I, 0:NB * NQ], pb[:, k, :], ALU.mult).then_inc(sem("pb_used"), 1)

                def activate(k, u):
                    if l == 3 and u > 0:
                        scale(k, u)
                    else:
                        dve.wait_ge(sem("gu_done"), u * 2 + (2 * base + 6))
                    ups = P[2 + k][0:I, 0:NB * NQ]
                    dve.wait_ge(sem("silu_done"), u + (base + 1))
                    V.tensor_tensor(sg[0:I, k, :], sg[0:I, k, :], ups, ALU.mult).then_inc(sem("gu_taken"), 1)
                    dve.wait_ge(sem("act_hi"), u + (base + 1))
                    V.tensor_tensor(real(act_b[0:I, k, 1, :]), by_batch(sg[0:I, k, :]), real(act_b[0:I, k, 0, :].bitcast(F32)), ALU.subtract
                                    ).then_inc(sem("act_ready"), 1)

                def accumulate(k, u):
                    dve.wait_ge(sem("down_done"), u + (base + 5))
                    dve.wait_ge(sem("acc_done"), u + (base + 2))
                    for t in range(TT):
                        last = V.scalar_tensor_tensor(acc[:, t, :], P[4 + 2 * k + t // 2][:, D * (t % 2):D * (t % 2) + D],
                                                      cw[:, t, bass.ds(u, 1)], acc[:, t, :], ALU.mult, ALU.add)
                    last.then_inc(sem("acc_done"), 1)

                activate(0, 0)
                if l < 3:
                    routing_weights(l)
                if U > 12:
                    with dve.Fori(0, U // 2 - 1) as i:
                        activate(1, i * 2 + 1)
                        accumulate(0, i * 2)
                        activate(0, i * 2 + 2)
                        accumulate(1, i * 2 + 1)
                for u in range(U - 2 if U > 12 else 0, U):
                    if u + 1 < U:
                        activate((u + 1) % 2, u + 1)
                    accumulate(u % 2, u)
                dve.wait_ge(sem("acc_done"), base + U + 2)
                residual(4 + l, acc[:, :, :].rearrange("p t d -> p (t d)"))

            def gather_rows():
                step(V.tensor_copy(segf[:, :], seg))
                step(V.tensor_copy(gidx[0:GR, 0, :], gseg[0:GR, :]))
                step(V.tensor_tensor(gidx[0:GR, 0, :], gidx[0:GR, 0, :], gidx[0:GR, 1, :], ALU.subtract))
                step(V.tensor_scalar(gidx[0:GR, 0, :], gidx[0:GR, 0, :], 0.0, NCTX - 1.0, ALU.max, ALU.min))
                step(V.tensor_tensor(gidx[0:GR, 0, :], gidx[0:GR, 0, :], gidx[0:GR, 2, :], ALU.add))
                step(V.memset(grow[:, :], 0))
                V.tensor_copy(grow[0:GR, :], gidx[0:GR, 0, :]).then_inc(sem("rows_ready"), 1)

            def window():
                dve.wait_ge(sem("pre1_psum"), 1)
                for j in range(4):
                    last = V.tensor_copy(wuvo[:, 2 * j:2 * j + 2, :].rearrange("p h n -> p (h n)"), P[2 + j][:, :])
                V.memset(ocT[:, :, :].rearrange("p h (b q) -> p h b q", q=QP)[:, :, :, NQ:QP], 0.0).then_inc(sem("pre1_dve"), 1)
                for hh in range(NH):
                    dve.wait_ge(sem("qh_psum"), hh + 1)
                    dst = qeff[64:128, :, hh, :]
                    b8 = lambda y: y.rearrange("p (b q) -> p b q", b=NB)
                    step(V.tensor_tensor(dst, b8(P[hh % 4][64:128, :]), b8(cosq[64:128, :]), ALU.mult))
                    step(V.tensor_tensor(rope2[64:128, :], P[4 + hh % 4][64:128, :], sinq[64:128, :], ALU.mult))
                    V.tensor_tensor(dst, dst, b8(rope2[64:128, :]), ALU.add).then_inc(sem("qr_taken"), 1)
                by9 = lambda y: y.rearrange("p (t j) -> p t j", j=NW)
                by72 = lambda y: y.rearrange("p (g n) -> p g n", g=NG)

                def compressed_keys(b, bi):
                    dve.wait_ge(sem("kv_psum"), b + 1)
                    dve.wait_ge(sem("mask1_made"), b + 1)
                    V.tensor_tensor(by9(kvm)[0:R], by9(P[0][0:R, 0:WB]), anyv[0:R, bi, 0, :].rearrange("p (t o) -> p t o", o=1).broadcast_to([R, NQ, NW]),
                                    ALU.mult).then_inc(sem("kvm_made"), 1)
                    dve.wait_ge(sem("kvm_made"), b + 1)
                    V.scalar_tensor_tensor(by9(keff[bi])[0:R], anyv[0:R, bi, 1, :].rearrange("p (t o) -> p t o", o=1).broadcast_to([R, NQ, NW]),
                                           mkv[0:R, bass.ds(b, 1)], by9(kvm)[0:R], ALU.mult, ALU.add).then_inc(sem("kv_sb"), 1)

                def rotations(b):
                    dve.wait_ge(sem("kr_psum"), b + 1)
                    dve.wait_ge(sem("cs_sb"), b + 1)
                    V.tensor_tensor(prod, P[1][:, 0:WB], csT, ALU.mult).then_inc(sem("prod_sb"), 1)

                def batch(i, bi, more):
                    b = i * 2 + bi
                    bc = lambda y: y.rearrange("p (g o) -> p g o", o=1).broadcast_to([128, NG, GW])

                    def own(k, ins):
                        ins.then_inc(sem("w1_step"), 1)
                        dve.wait_ge(sem("w1_step"), b * 4 + k)

                    dve.wait_ge(sem("s1_psum"), b + 1)
                    own(1, V.tensor_tensor(P1, P[3][:, 0:WB], madd[bi], ALU.add))
                    own(2, V.tensor_reduce(sm1[:, 0, :], by72(P1), AX.X, ALU.max))
                    V.tensor_tensor(by72(P1), by72(P1), bc(sm1[:, 0, :]), ALU.subtract).then_inc(sem("s1_sb"), 1)
                    dve.wait_ge(sem("e1_sb"), b + 1)
                    own(3, V.tensor_reduce(sm1[:, 1, :], by72(P1), AX.X, ALU.add))
                    own(4, V.reciprocal(sm1[:, 2, :], sm1[:, 1, :]))
                    V.tensor_tensor(by72(P1), by72(P1), bc(sm1[:, 2, :]), ALU.mult).then_inc(sem("p1_sb"), 1)
                    if more:
                        compressed_keys(b + 1, 1 - bi)
                        rotations(b + 1)
                    dve.wait_ge(sem("oc_psum"), b + 1)
                    for e in range(2):
                        for j, m in ((0, 4), (1, 3)):
                            src = P[6 + j][64 * e:64 * e + 64, 0:128 * m].rearrange("p (t h x) -> p h t x", h=8, x=2)[:, :, :, e]
                            last = V.tensor_copy(ocT[64 * e:64 * e + 64, :, bass.ds(b * QP + GT * 4 * j, GT * m)], src)
                    last.then_inc(sem("p1_taken"), 1)

                compressed_keys(0, 0)
                rotations(0)
                with dve.Fori(0, NB // 2 - 1) as i:
                    batch(i, 0, True)
                    batch(i, 1, True)
                batch(NB // 2 - 1, 0, True)
                batch(NB // 2 - 1, 1, False)
                dve.wait_ge(sem("out1_psum"), 1)
                add_banks(1)

            V.memset(x[:, :, :], 0.0).then_inc(sem("x_cleared"), 1)
            V.memset(oTs[:, :, :], 0.0)
            V.memset(mx[:, :, :], -1.0e29).then_inc(sem("s_taken"), 3)
            signal("t_done", 12)
            signal("pv_done", 2)
            signal("ctx_lo", 4)
            signal("mean_done", 2)
            signal("sup_lo", 2)
            signal("g_turned", 2)
            signal("mask_used", 2)
            signal("down_done", 4)
            signal("act_ready", 2)
            signal("acc_done", 2)
            signal("pt_act", 2)
            for name in ("pt_dve", "o_taken", "keff_sb"):
                signal(name)
            signal("p1_taken", 2)
            signal("s1_sb", 2)
            signal("pb_used", 2)
            signal("gu_done", 4)
            signal("gu_taken", 2)
            signal("down_split", 4)
            dve.wait_ge(sem("x_in"), 16 * NB)

            for s in range(NSUB):
                l = s // 2
                layer_norm(s not in (0, 4))
                if s == 0:
                    for t in range(TT):
                        step(V.tensor_tensor_reduce(tmp[:, t, :], h[:, t, :], h[:, t, :], 1.0, 0.0, ALU.mult, ALU.add,
                                                    sm[:, 3, t:t + 1]))
                    inverse_root(V.tensor_scalar(sm[:, 0, :], sm[:, 3, :], 1.0 / D, 1e-6, ALU.mult, ALU.add))
                    step(V.tensor_tensor(h[:, :, :], h[:, :, :], wide(sm[:, 2, :], D), ALU.mult))
                if s == 4:
                    step(fake_quantise(h))
                if s in (0, 4):
                    signal("h_ready", TT)
                if s == 0:
                    dve.wait_ge(sem("const_in"), 16 * 17)
                    gather_rows()
                    fake_quantise(w2n).then_inc(sem("w2n_ready"), 1)
                transposed(hT, cols[:, 1:2] if s == 0 else None)
                if s % 2:
                    mixture(l)
                    continue
                if l == 1:
                    window()
                    continue
                a = ATT[l]
                attention(l, "first")
                if l == 3:
                    dve.wait_ge(sem("tg_ready"), 1)
                    dve.wait_ge(sem("ref_psum"), 1)
                    for j in range(2):
                        last = add_gated(3, slice(2 * j, 2 * j + 2), P[4 + j][:, :].rearrange("p (t d) -> p t d", t=2))
                    step(last)
                    signal("ref_sb")
                dve.wait_ge(sem("q_psum"), a + 1)
                for o in range(KT):
                    if l == 0:
                        step(V.tensor_scalar(qT[:, o, :], P[QBANK[l][o]][:, :], 0.25, None, ALU.mult))
                    else:
                        col = (2 if l == 2 else 8) + o
                        step(V.tensor_scalar(qT[:, o, :], P[QBANK[l][o]][:, :], cols[:, col:col + 1], 0.25, ALU.add, ALU.mult))
                if l == 0:
                    dve.wait_ge(sem("w2T_psum"), 1)
                    for m in range(2):
                        step(V.tensor_copy(w2T[:, 2 * m:2 * m + 2, :].rearrange("p k d -> p (k d)"), P[3 + m][:, :]))
                signal("q_sb")
                for k in range(KT):
                    step(V.tensor_copy(Qb[:, 0, k, :], qT[:, k, :]))
                step(V.tensor_tensor(qT2[:, :, :], qT[:, :, :], Qb[:, 0, :, :].bitcast(F32), ALU.subtract))
                for r in (0, 64):
                    step(V.tensor_copy(qlo[64 - r:128 - r, :, :], qT2[r:r + 64, :, :]))
                signal("qlo_sb")
                if l == 3:
                    step(add_gated(3, slice(0, TT), rows[:, 2, :].rearrange("p (o d) -> p o d", o=1).broadcast_to([128, TT, D])))
                attention(l, "pairs")
                flat = tmp[:, :, :].rearrange("p t d -> p (t d)")
                row = lambda r: rows[:, r, :].rearrange("p (o d) -> p o d", o=1).broadcast_to([128, TT, D])
                if l == 0:
                    signal("o_ready")
                    transposed(oT)
                    dve.wait_ge(sem("gate_ready"), 2)
                    dve.wait_ge(sem("out_psum"), 1)
                    for j in range(2):
                        step(V.tensor_tensor(tmp[:, 2 * j:2 * j + 2, :].rearrange("p t d -> p (t d)"),
                                             tmp[:, 2 * j:2 * j + 2, :].rearrange("p t d -> p (t d)"), P[j][:, :], ALU.mult))
                    dve.wait_ge(sem("tg_ready"), 1)
                    residual(0, flat)
                if l == 2:
                    step(V.tensor_tensor(onat[:, :, :], onat[:, :, :], row(0), ALU.add))
                    fake_quantise(onat).then_inc(sem("o_ready"), 1)
                    transposed(oT)
                    step(add_gated(2, slice(0, TT), row(1)))
                    dve.wait_ge(sem("out_psum"), 2)
                    add_banks(2)
                if l == 3:
                    residual(3, onat[:, :, :].rearrange("p t d -> p (t d)"))


def _consts():
    c = {}
    c["ident"] = np.eye(128, dtype=np.float32)
    c["turned_ident"] = np.roll(c["ident"], 64, axis=1)
    c["spread"] = np.concatenate([c["ident"][0:NQ], c["ident"][QP:QP + NQ]])
    mask = (np.arange(128)[:, None] // HD == np.arange(NP)[None, :]).astype(np.float32)
    c["headmask"] = np.stack([mask, np.roll(mask, 64, axis=0)], axis=1)
    half = R // 2
    inv_freq = (1.0 / 10000.0 ** (np.arange(half, dtype=np.float32) / np.float32(half))).astype(np.float32)
    ang = np.arange(NCTX, dtype=np.float32)[:, None] * inv_freq
    cos, sin = np.cos(ang).astype(np.float32), np.sin(ang).astype(np.float32)
    c["rope"] = np.concatenate([cos, cos, -sin, sin], axis=1)
    q = np.zeros((NTOK, 128), np.float32)
    for b in range(NB):
        q[QP * b:QP * b + NQ] = c["rope"][0:NQ]
    c["cosq"], c["sinq"] = np.ascontiguousarray(q[:, 0:R].T), np.ascontiguousarray(q[:, R:2 * R].T)
    p = np.arange(128)[:, None] // NH
    c["blk"] = np.where(np.arange(GW)[None, :] // NW == p, 0.0, 3 * NEG).astype(np.float32)
    c["jrow"] = np.arange(NW, dtype=np.float32)
    c["wstk"] = np.concatenate([np.eye(R), np.eye(R)]).astype(np.float32)
    j = np.tile((np.arange(GR) % NW).astype(np.float32)[:, None], (1, NB * NGT))
    first = np.tile((np.arange(NB * NGT) // NGT * NCTX).astype(np.float32)[None, :], (GR, 1))
    c["gconst"] = np.stack([j, first], axis=1)
    return c


def _io(w):
    return w.reshape(-1, 128, w.shape[1]).transpose(1, 0, 2)


def kernel(**inputs):
    import concourse.bacc as bacc
    from concourse.bass_utils import run_bass_kernel_spmd as run
    a = {k: np.asarray(v) for k, v in inputs.items()}
    c = _consts()
    m = {k: c[k] for k in ("ident", "turned_ident", "spread", "headmask", "cosq", "sinq", "blk", "jrow", "wstk", "gconst")}
    m["x"] = a["x"]
    ctx = a["ctx_2048"]
    m["ctxT"] = ctx.transpose(0, 2, 1).reshape(NB, KT, 128, NCTX).transpose(0, 2, 1, 3)
    m["ctxrows"] = np.concatenate([ctx.reshape(NB * NCTX, D), np.tile(c["rope"], (NB, 1))], axis=1)
    m["mask0"] = a["mask_BxS2_bk0"].view(np.int32)
    m["mask2"] = a["mask_BxSxS2_ff0"]
    seg = a["itok_BxS_0_1023"]
    m["seg"] = seg.reshape(-1)
    m["gseg"] = np.repeat(seg.reshape(NB, NGT, GR // NW), NW, axis=2).reshape(NB * NGT, GR).T
    m["gates"] = np.concatenate([a["g_xattn"], a["g_ffn"]])
    zero = np.zeros(D, np.float32)
    m["rows"] = np.stack([a["L2_xattn_bv"], a["L2_xattn_bo"], a["L3_xattn_b_v"]])
    m["cols"] = np.concatenate([v.reshape(KT, 128).T for v in (
        a["L0_xattn_norm_w"], a["L2_xattn_bq"], a["L2_xattn_bk"], a["L3_xattn_b_fc"], a["L3_xattn_b_q"],
        a["L3_xattn_b_k"], zero, zero)], axis=1)
    m["w0"] = np.stack([_io(a["L0_xattn_" + n].T) for n in ("wq", "wk", "wv", "wo", "wg")], axis=1)
    m["w2"] = np.stack([_io(a["L2_xattn_" + n].T) for n in ("wk", "wv")], axis=1)
    m["w2n"] = np.concatenate([_io(a["L2_xattn_" + n]) for n in ("wq", "wo")], axis=1)
    m["w3"] = np.stack([_io(a["L3_xattn_W_fc"].T), _io(a["L3_xattn_W_q"].T), _io(a["L3_xattn_W_k"].T),
                        _io(a["L3_xattn_W_v"].reshape(D, D).T)], axis=1)
    gate = [a["L0_ffn_gate_w"].T, a["L1_ffn_w_router"], a["L2_ffn_router_gate"].T, a["L3_ffn_router_w"]]
    m["gw"] = np.stack([np.pad(_io(g), ((0, 0), (0, 0), (0, 16 - g.shape[1]))) for g in gate], axis=1)

    def heads(w, n):
        return w.reshape(w.shape[0], NH, n)

    m["wuqT"] = heads(a["L1_xattn_W_uq"], HDL).transpose(2, 1, 0)
    m["wukT"] = heads(a["L1_xattn_W_uk"], HDL).transpose(2, 1, 0)
    m["wuvT"] = heads(a["L1_xattn_W_uv"], HDL).transpose(2, 1, 0)
    qr = heads(a["L1_xattn_W_qr"], R)
    m["wqr"] = qr
    m["wqr2"] = np.concatenate([qr[:, :, R // 2:], qr[:, :, :R // 2]], axis=2)
    m["wdq"] = _io(a["L1_xattn_W_dq"])
    m["wkvc"] = _io(a["L1_xattn_W_kvc"])
    kr = a["L1_xattn_W_kr"]
    m["wkr"] = np.concatenate([kr, kr[:, R // 2:], kr[:, :R // 2]], axis=1)
    m["wo1"] = a["L1_xattn_W_o"].reshape(NH, HDL, D).transpose(1, 0, 2)

    def ups(gate_w, up_w):
        w = np.concatenate([gate_w, up_w], axis=2)
        return w.reshape(len(w), KT, 128, -1).transpose(0, 2, 1, 3)

    def cut(w, n):
        return w.reshape(w.shape[0], D, n, -1).transpose(0, 2, 1, 3).reshape(w.shape[0] * n, D, -1)

    w1, s1 = a["L0_ffn_w1"].transpose(0, 2, 1), a["L0_ffn_shared_w1"].T[None]
    m["up0"] = np.concatenate([ups(cut(w1[:, :, :176], 2), cut(w1[:, :, 176:], 2)),
                               ups(cut(s1[:, :, :352], 4), cut(s1[:, :, 352:], 4))])
    m["down0"] = np.concatenate([a["L0_ffn_w2"].transpose(0, 2, 1).reshape(32, 88, D),
                                 a["L0_ffn_shared_w2"].T.reshape(4, 88, D)])
    m["up0"] = np.pad(m["up0"].reshape(36, 128, KT, 2, 88), ((0, 0),) * 4 + ((0, 8),)).reshape(36, 128, KT, 192)
    m["down0"] = np.pad(m["down0"], ((0, 0), (0, 8), (0, 0)))
    m["up1"] = np.concatenate([ups(a["L1_ffn_we1"], a["L1_ffn_we3"]),
                               ups(cut(a["L1_ffn_ws1"][None], 4), cut(a["L1_ffn_ws3"][None], 4))])
    m["down1"] = np.concatenate([a["L1_ffn_we2"], a["L1_ffn_ws2"].reshape(4, 128, D)])
    gu = a["L2_ffn_expert_gate_up"]
    m["up2"], m["down2"] = ups(gu[:, :, 0::2], gu[:, :, 1::2]), a["L2_ffn_expert_down"]
    gu = a["L3_ffn_gate_up_w"]
    m["up3"] = np.concatenate([ups(a["L3_ffn_shared_gate_w"][None], a["L3_ffn_shared_up_w"][None]),
                               ups(gu[:, :, :128], gu[:, :, 128:])])
    m["down3"] = np.concatenate([a["L3_ffn_shared_down_w"][None], a["L3_ffn_down_w"]])

    nc = bacc.Bacc("TRN2", target_bir_lowering=False, num_devices=1)
    arrays = {f"in_{k}": np.ascontiguousarray(w) for k, w in m.items()}
    A = {k[3:]: nc.dram_tensor(k, w.shape, mybir.dt.from_np(w.dtype), kind="ExternalInput").ap()
         for k, w in arrays.items()}
    A["prT"] = nc.dram_tensor("prT", (8, NTOK), mybir.dt.float32, kind="Internal").ap()
    out = nc.dram_tensor("out_x", (NB, NQ, D), mybir.dt.float32, kind="ExternalOutput").ap()
    flamingo_kernel(nc, A, out)
    r = run(nc, [arrays], core_ids=[0])
    return r.results[0]["out_x"]
```
